# Optimizing a Trainium2 kernel written in Bass

```python
import numpy as np
import jax
import jax.numpy as jnp

def _softmax(x, axis=-1):
    return jax.nn.softmax(x, axis=axis)

def _gelu(x):
    return jax.nn.gelu(x, approximate=True)

def _silu(x):
    return jax.nn.silu(x)

def _sigmoid(x):
    return jax.nn.sigmoid(x)

def _layernorm(x, axis=-1, eps=1e-05):
    m = jnp.mean(x, axis=axis, keepdims=True)
    v = jnp.var(x, axis=axis, keepdims=True)
    return (x - m) / jnp.sqrt(v + eps)

def _scatter_add(tgt, idx, src, axis=0):
    return tgt.at[idx].add(src)

def _segment_sum(src, seg, n):
    return jax.ops.segment_sum(src, seg, n)
kernel_name = 'mk_conv_preact_d4_conv_nhwc256_r4_08f536'

def setup_inputs(seed: int=0):
    np.random.seed(seed)
    _w = jnp.asarray

    def _rec_inputs():
        import jax
        import jax.numpy as jnp
        _gk = jax.random.key(seed)
        x = 7.22e-05 + 1 * jax.random.normal(jax.random.fold_in(_gk, 1), (8, 16, 16, 64), jnp.float32)
        return x
    x = _rec_inputs()

    def _L0_conv_setup():
        import jax, jax.numpy as jnp
        import numpy as np
        B, IN_C, IN_L, T = (8, 16, 16, 64)
        OUT_C, OUT_L = (16, 16)
        KH, KW = (3, 3)
        K = IN_C * KH * KW
        EPS = 1e-05

        def _unfold3x3(x):
            xp = jnp.pad(x, ((0, 0), (0, 0), (1, 1), (1, 1)))
            pats = jnp.stack([xp[:, :, i:i + IN_L, j:j + T] for i in range(KH) for j in range(KW)], axis=2)
            return pats.reshape(x.shape[0], K, IN_L, T)
        key = jax.random.key(seed)
        k1, k2 = jax.random.split(key, 2)
        x = jax.random.normal(k1, (B, IN_C, IN_L, T), dtype=jnp.float32)
        weight = jax.random.normal(k2, (K, OUT_C, OUT_L), dtype=jnp.float32) * (1.0 / np.sqrt(K))
        bias = jnp.zeros((OUT_C, OUT_L), dtype=jnp.float32)
        gamma = jnp.ones((OUT_C,), dtype=jnp.float32)
        beta = jnp.zeros((OUT_C,), dtype=jnp.float32)
        alpha = jnp.full((1,), 0.25, dtype=jnp.float32)
        return {'x': x, 'weight': weight, 'bias': bias, 'gamma': gamma, 'beta': beta, 'alpha': alpha}
    _L0_conv_all = _L0_conv_setup()
    _L0_conv_in = {k: v for k, v in _L0_conv_all.items() if k in ('weight', 'bias', 'gamma', 'beta', 'alpha')}
    del _L0_conv_all

    def _L1_conv_setup():
        import jax, jax.numpy as jnp
        import numpy as np
        MAX_LR = 0.1

        def _l2norm(x):
            n = jnp.linalg.norm(x, axis=-1, keepdims=True)
            return x / jnp.maximum(n, 1e-12)

        def _mlp(params, h):
            for w1, w2 in params:
                h = h + jax.nn.gelu(h @ w1) @ w2
            return h
        key = jax.random.key(seed)
        ks = jax.random.split(key, 11)
        B, T, C, D, DE = (4, 16, 16, 64, 128)
        s = 0.02
        return {'x': jax.random.normal(ks[0], (B, T, C, D), jnp.float32), 'Wq': jax.random.normal(ks[1], (D, D), jnp.float32) * s, 'Wk': jax.random.normal(ks[2], (D, D), jnp.float32) * s, 'Wv': jax.random.normal(ks[3], (D, D), jnp.float32) * s, 'w_lr': jax.random.normal(ks[4], (D,), jnp.float32) * s, 'w_forget': jax.random.normal(ks[5], (D,), jnp.float32) * s, 'w_eta': jax.random.normal(ks[6], (D,), jnp.float32) * s, 'w1_0': jax.random.normal(ks[7], (D, DE), jnp.float32) * s, 'w2_0': jax.random.normal(ks[8], (DE, D), jnp.float32) * s, 'w1_1': jax.random.normal(ks[9], (D, DE), jnp.float32) * s, 'w2_1': jax.random.normal(ks[10], (DE, D), jnp.float32) * s}
    _L1_conv_all = _L1_conv_setup()
    _L1_conv_in = {k: v for k, v in _L1_conv_all.items() if k in ('Wq', 'Wk', 'Wv', 'w_lr', 'w_forget', 'w_eta', 'w1_0', 'w2_0', 'w1_1', 'w2_1')}
    del _L1_conv_all

    def _L2_conv_setup():
        import jax, jax.numpy as jnp
        import numpy as np
        B, H, W, C = (8, 16, 16, 64)
        NUM_HEADS = 8
        DILATION = 3
        KERNEL = 3

        def _unfold(t, kernel, dilation):
            b, c, h, w = t.shape
            p = dilation * (3 - 1) // 2
            tp = jnp.pad(t, ((0, 0), (0, 0), (p, p), (p, p)))
            pats = [tp[:, :, i * dilation:i * dilation + h, j * dilation:j * dilation + w] for i in range(kernel) for j in range(kernel)]
            return jnp.stack(pats, axis=2)
        key = jax.random.key(seed)
        k1, k2 = jax.random.split(key)
        x = jax.random.normal(k1, (B, H, W, C), dtype=jnp.float32)
        W_qkv = jax.random.normal(k2, (3 * C, C), dtype=jnp.float32) * 0.02
        return {'x': x, 'W_qkv': W_qkv}
    _L2_conv_all = _L2_conv_setup()
    _L2_conv_in = {k: v for k, v in _L2_conv_all.items() if k in ('W_qkv',)}
    del _L2_conv_all

    def _L3_conv_setup():
        import jax, jax.numpy as jnp
        import numpy as np
        E = 2
        EPS = 1e-05

        def _linear_scan(inp, lam):

            def comb(l, r):
                al, bl = l
                ar, br = r
                return (ar * al, ar * bl + br)
            _, h = jax.lax.associative_scan(comb, (lam, inp), axis=0)
            return h

        def _bidir_scan(inp, lam):
            fwd = _linear_scan(inp, lam)
            rev = jnp.flip(_linear_scan(jnp.flip(inp, 0), jnp.flip(lam, 0)), 0)
            return fwd + rev
        key = jax.random.key(seed)
        ks = jax.random.split(key, 7)
        H, W, B, D = (16, 16, 8, 64)
        s = 0.02
        return {'x': jax.random.normal(ks[0], (H, W, B, D), dtype=jnp.float32), 'in_w': jax.random.normal(ks[1], (D, 3 * D), dtype=jnp.float32) * s, 'in_b': jnp.zeros((3 * D,), dtype=jnp.float32), 'out_w': jax.random.normal(ks[2], (D, D), dtype=jnp.float32) * s, 'out_b': jnp.zeros((D,), dtype=jnp.float32), 'gamma': jnp.ones((D,), dtype=jnp.float32), 'beta': jnp.zeros((D,), dtype=jnp.float32)}
    _L3_conv_all = _L3_conv_setup()
    _L3_conv_in = {k: v for k, v in _L3_conv_all.items() if k in ('in_w', 'in_b', 'out_w', 'out_b', 'gamma', 'beta')}
    del _L3_conv_all
    return {'x': x, 'L0_conv_weight': _L0_conv_in['weight'], 'L0_conv_bias': _L0_conv_in['bias'], 'L0_conv_gamma': _L0_conv_in['gamma'], 'L0_conv_beta': _L0_conv_in['beta'], 'L0_conv_alpha': _L0_conv_in['alpha'], 'L1_conv_Wq': _L1_conv_in['Wq'], 'L1_conv_Wk': _L1_conv_in['Wk'], 'L1_conv_Wv': _L1_conv_in['Wv'], 'L1_conv_w_lr': _L1_conv_in['w_lr'], 'L1_conv_w_forget': _L1_conv_in['w_forget'], 'L1_conv_w_eta': _L1_conv_in['w_eta'], 'L1_conv_w1_0': _L1_conv_in['w1_0'], 'L1_conv_w2_0': _L1_conv_in['w2_0'], 'L1_conv_w1_1': _L1_conv_in['w1_1'], 'L1_conv_w2_1': _L1_conv_in['w2_1'], 'L2_conv_W_qkv': _L2_conv_in['W_qkv'], 'L3_conv_in_w': _L3_conv_in['in_w'], 'L3_conv_in_b': _L3_conv_in['in_b'], 'L3_conv_out_w': _L3_conv_in['out_w'], 'L3_conv_out_b': _L3_conv_in['out_b'], 'L3_conv_gamma': _L3_conv_in['gamma'], 'L3_conv_beta': _L3_conv_in['beta']}

def reference(x, L0_conv_weight, L0_conv_bias, L0_conv_gamma, L0_conv_beta, L0_conv_alpha, L1_conv_Wq, L1_conv_Wk, L1_conv_Wv, L1_conv_w_lr, L1_conv_w_forget, L1_conv_w_eta, L1_conv_w1_0, L1_conv_w2_0, L1_conv_w1_1, L1_conv_w2_1, L2_conv_W_qkv, L3_conv_in_w, L3_conv_in_b, L3_conv_out_w, L3_conv_out_b, L3_conv_gamma, L3_conv_beta):
    import jax
    import jax.numpy as jnp

    def _L0_conv_ref(x, weight, bias, gamma, beta, alpha):
        import jax, jax.numpy as jnp
        import numpy as np
        B, IN_C, IN_L, T = (8, 16, 16, 64)
        OUT_C, OUT_L = (16, 16)
        KH, KW = (3, 3)
        K = IN_C * KH * KW
        EPS = 1e-05

        def _unfold3x3(x):
            xp = jnp.pad(x, ((0, 0), (0, 0), (1, 1), (1, 1)))
            pats = jnp.stack([xp[:, :, i:i + IN_L, j:j + T] for i in range(KH) for j in range(KW)], axis=2)
            return pats.reshape(x.shape[0], K, IN_L, T)
        patches = _unfold3x3(x)
        out = jnp.einsum('bklt,kcl->bclt', patches, weight)
        out = out + bias[None, :, :, None]
        mean = out.mean(axis=(0, 2, 3), keepdims=True)
        var = out.var(axis=(0, 2, 3), keepdims=True)
        out = (out - mean) * jax.lax.rsqrt(var + EPS) * gamma[None, :, None, None] + beta[None, :, None, None]
        return jnp.where(out >= 0, out, alpha[0] * out)

    def _L1_conv_ref(x, Wq, Wk, Wv, w_lr, w_forget, w_eta, w1_0, w2_0, w1_1, w2_1):
        import jax, jax.numpy as jnp
        import numpy as np
        MAX_LR = 0.1

        def _l2norm(x):
            n = jnp.linalg.norm(x, axis=-1, keepdims=True)
            return x / jnp.maximum(n, 1e-12)

        def _mlp(params, h):
            for w1, w2 in params:
                h = h + jax.nn.gelu(h @ w1) @ w2
            return h
        B = x.shape[0]
        mem0 = ((w1_0, w2_0), (w1_1, w2_1))
        params0 = jax.tree.map(lambda p: jnp.broadcast_to(p, (B,) + p.shape), mem0)
        mom0 = jax.tree.map(jnp.zeros_like, params0)
        q = _l2norm(jnp.einsum('btcd,de->btce', x, Wq))

        def assoc_loss(p, k, v):
            pred = _mlp(p, k)
            return jnp.mean((pred - v) ** 2)
        grad_fn = jax.vmap(jax.grad(assoc_loss))

        def step(carry, x_t):
            params, mom = carry
            k = _l2norm(x_t @ Wk)
            v = x_t @ Wv
            lr = MAX_LR * jnp.mean(jax.nn.sigmoid(x_t @ w_lr), axis=1)
            forget = jnp.mean(jax.nn.sigmoid(x_t @ w_forget), axis=1)
            eta = jnp.mean(jax.nn.sigmoid(x_t @ w_eta), axis=1)
            g = grad_fn(params, k, v)

            def upd_m(m, gg):
                sh = (B,) + (1,) * (m.ndim - 1)
                return eta.reshape(sh) * m - lr.reshape(sh) * gg
            new_mom = jax.tree.map(upd_m, mom, g)

            def upd_p(p, nm):
                sh = (B,) + (1,) * (p.ndim - 1)
                return p * (1.0 - forget.reshape(sh)) + nm
            new_params = jax.tree.map(upd_p, params, new_mom)
            return ((new_params, new_mom), None)
        (paramsT, momT), _ = jax.lax.scan(step, (params0, mom0), jnp.swapaxes(x, 0, 1))
        final = jax.tree.map(lambda p: jnp.mean(p, axis=0), paramsT)
        return _mlp(final, q)

    def _L2_conv_ref(x, W_qkv):
        import jax, jax.numpy as jnp
        import numpy as np
        B, H, W, C = (8, 16, 16, 64)
        NUM_HEADS = 8
        DILATION = 3
        KERNEL = 3

        def _unfold(t, kernel, dilation):
            b, c, h, w = t.shape
            p = dilation * (3 - 1) // 2
            tp = jnp.pad(t, ((0, 0), (0, 0), (p, p), (p, p)))
            pats = [tp[:, :, i * dilation:i * dilation + h, j * dilation:j * dilation + w] for i in range(kernel) for j in range(kernel)]
            return jnp.stack(pats, axis=2)
        b, h, w, c = x.shape
        dph = c // NUM_HEADS
        scale = dph ** (-0.5)
        k2 = KERNEL * KERNEL
        qkv = jnp.einsum('bhwc,oc->bhwo', x, W_qkv).reshape(b, h, w, 3, c)
        qkv = jnp.transpose(qkv, (3, 0, 4, 1, 2))
        q, k, v = (qkv[0], qkv[1], qkv[2])
        k = _unfold(k, KERNEL, DILATION).reshape(b, NUM_HEADS, dph, k2, h * w)
        v = _unfold(v, KERNEL, DILATION).reshape(b, NUM_HEADS, dph, k2, h * w)
        q = q.reshape(b, NUM_HEADS, dph, h * w)
        attn = jnp.einsum('bndm,bndkm->bnmk', q, k) * scale
        attn = jax.nn.softmax(attn, axis=-1)
        out = jnp.einsum('bnmk,bndkm->bnmd', attn, v)
        out = jnp.transpose(out, (0, 2, 1, 3)).reshape(b, h, w, c)
        return out

    def _L3_conv_ref(x, in_w, in_b, out_w, out_b, gamma, beta):
        import jax, jax.numpy as jnp
        import numpy as np
        E = 2
        EPS = 1e-05

        def _linear_scan(inp, lam):

            def comb(l, r):
                al, bl = l
                ar, br = r
                return (ar * al, ar * bl + br)
            _, h = jax.lax.associative_scan(comb, (lam, inp), axis=0)
            return h

        def _bidir_scan(inp, lam):
            fwd = _linear_scan(inp, lam)
            rev = jnp.flip(_linear_scan(jnp.flip(inp, 0), jnp.flip(lam, 0)), 0)
            return fwd + rev
        H, W, B, D = x.shape
        nh = D // E
        feat = x @ in_w + in_b
        inp, og, fg = jnp.split(feat, 3, axis=-1)
        inp = jax.nn.silu(inp)
        og = jax.nn.sigmoid(og)
        lam = jax.nn.sigmoid(fg)
        lam = lam.reshape(H, W, B, nh, E)
        inp = inp.reshape(H, W, B, nh, E)
        og = og.reshape(H, W, B, nh, E)
        inp_o = jnp.einsum('...hd,...he->...hde', 1.0 - lam, inp)
        lam_o = jnp.broadcast_to(lam[..., None], inp_o.shape)
        C = nh * E * E
        inp_f = inp_o.reshape(H, W, B, C)
        lam_f = lam_o.reshape(H, W, B, C)
        s_h = _bidir_scan(inp_f, lam_f)
        inp_w = jnp.swapaxes(inp_f, 0, 1)
        lam_w = jnp.swapaxes(lam_f, 0, 1)
        s_w = jnp.swapaxes(_bidir_scan(inp_w, lam_w), 0, 1)
        state = (s_h + s_w).reshape(H, W, B, nh, E, E)
        out = jnp.einsum('...hde,...hd->...he', state, og)
        out = out.reshape(H, W, B, D)
        mu = out.mean(-1, keepdims=True)
        var = out.var(-1, keepdims=True)
        out = (out - mu) * jax.lax.rsqrt(var + EPS) * gamma + beta
        return out @ out_w + out_b

    def _gn(v, G=32, eps=1e-05):
        B_, H_, W_, C_ = v.shape
        g = v.reshape(B_, H_, W_, G, C_ // G)
        m = jnp.mean(g, axis=(1, 2, 4), keepdims=True)
        s = jnp.var(g, axis=(1, 2, 4), keepdims=True)
        return ((g - m) / jnp.sqrt(s + eps)).reshape(v.shape)

    def _ln_c(v, eps=1e-06):
        m = jnp.mean(v, axis=-1, keepdims=True)
        s = jnp.var(v, axis=-1, keepdims=True)
        return (v - m) / jnp.sqrt(s + eps)

    def _ln_t(v, eps=1e-05):
        m = jnp.mean(v, axis=-1, keepdims=True)
        s = jnp.var(v, axis=-1, keepdims=True)
        return (v - m) / jnp.sqrt(s + eps)

    def _to_tokens(v):
        B_, H_, W_, C_ = v.shape
        return v.reshape(B_, H_ * W_, C_)

    def _from_tokens(t, like):
        return t.reshape(like.shape)
    x = x + _L0_conv_ref(_gn(x), L0_conv_weight, L0_conv_bias, L0_conv_gamma, L0_conv_beta, L0_conv_alpha)
    x = x + _L1_conv_ref(_gn(x), L1_conv_Wq, L1_conv_Wk, L1_conv_Wv, L1_conv_w_lr, L1_conv_w_forget, L1_conv_w_eta, L1_conv_w1_0, L1_conv_w2_0, L1_conv_w1_1, L1_conv_w2_1)
    x = x + _L2_conv_ref(_gn(x), L2_conv_W_qkv)
    x = x + _L3_conv_ref(_gn(x), L3_conv_in_w, L3_conv_in_b, L3_conv_out_w, L3_conv_out_b, L3_conv_gamma, L3_conv_beta)
    return x

_drawn_inputs = setup_inputs


def setup_inputs(seed=0):
    import zlib

    import numpy as np

    out = dict(_drawn_inputs(seed))
    spreads = {'L0_conv_bias': (0.0, 0.1),
     'L0_conv_gamma': (1.0, 0.2),
     'L0_conv_beta': (0.0, 0.1),
     'L3_conv_in_b': (0.0, 0.1),
     'L3_conv_out_b': (0.0, 0.1),
     'L3_conv_gamma': (1.0, 0.6),
     'L3_conv_beta': (0.0, 0.587)}
    factors = {}
    for name, (base, spread) in spreads.items():
        noise = np.random.default_rng([zlib.crc32(name.encode()), seed]).standard_normal(out[name].shape)
        drawn = base * np.exp(spread * noise) if base else spread * noise
        out[name] = jnp.asarray(drawn.astype(out[name].dtype))
    for name, factor in factors.items():
        out[name] = (out[name] * factor).astype(out[name].dtype)
    return out
```

```python
from contextlib import ExitStack

import numpy as np

import concourse.bass as bass
from concourse import mybir

F32 = mybir.dt.float32
BF16 = mybir.dt.bfloat16
ALU = mybir.AluOpType
ACT = mybir.ActivationFunctionType
AX_X = mybir.AxisListType.X

B, H, W, C = 8, 16, 16, 64
BH, J = 2, 4
HW = H * W
POS = J * HW
NT = 2 * POS
P = 128
E1 = 128
NS = H
TOK = B * W
NK = 9
PADW = H + 6
NHD = 8
BANK = 512
GEPS = 1e-5
GC = 0.044715
GS = float(np.sqrt(2.0 / np.pi))
FILL = (1, 1, 1, 2)
GRAD_SCALE = 2.0 / (W * C)
MAX_LR = 0.1

CONST_COLS = {}


def _const_layout():
    at = 0
    for name, width in (("ident", P), ("pair_half", P), ("sum16", P), ("ones64", P), ("dup64", P), ("head_sel", BH * NHD),
                        ("center_d", C), ("block_j", J), ("half_sel", 2 * P), ("tok_sel", J * P), ("gate_scale", 2),
                        ("eps", 1)):
        CONST_COLS[name] = (at, at + width)
        at += width
    return at


NCONST = _const_layout()

PARAM_COLS = {}


def _param_layout():
    at = 0
    for name, width in (("conv_bias", 2), ("conv_gamma", 2), ("conv_beta", 2), ("conv_alpha", 1), ("wk", P), ("wv", P),
                        ("wq", P), ("gates", 6), ("mats_e", 3 * C), ("w1_0", E1), ("attn_q", P),
                        ("attn_k", P), ("attn_v", P), ("scan_w", 3 * P), ("scan_b", 3), ("out_w", P), ("out_b", 1),
                        ("ln_gamma", 1), ("ln_beta", 1)):
        PARAM_COLS[name] = (at, at + width)
        at += width
    return at


NPARAM = _param_layout()


def conv_attn_scan_kernel(nc, xs_d, band_d, const_d, param_d, out_d):
    ctx = ExitStack()
    with ctx:
        def sb(name, shape):
            return ctx.enter_context(nc.sbuf_tensor(name, shape, F32))

        sems = {}

        def sem(name):
            if name not in sems:
                sems[name] = ctx.enter_context(nc.semaphore(name))
            return sems[name]

        ps = ctx.enter_context(nc.psum_tensor("ps", [P, 8, BANK], F32))
        psf = ps[:, :, :].rearrange("p b n -> p (b n)")

        const = sb("const_sb", [P, NCONST])
        param = sb("param_sb", [P, NPARAM])

        def cst(name, rows=P):
            a, b = CONST_COLS[name]
            return const[0:rows, a:b]

        def par(name):
            a, b = PARAM_COLS[name]
            return param[:, a:b]

        ident = cst("ident")

        def carve(arena):
            at = [0]

            def take(*dims):
                n = int(np.prod(dims))
                flat = arena[:, at[0]:at[0] + n]
                at[0] += n
                if len(dims) == 1:
                    return flat
                names = "abc"[:len(dims)]
                return flat.rearrange(f"p ({' '.join(names)}) -> p {' '.join(names)}", **dict(zip(names, dims)))
            return take

        arena_conv = sb("arena_conv", [P, 1536 + 1056 + 2048])
        arena_mem = sb("arena_mem", [P, 3 * 512 * 3 + 512 * 6])
        arena_att = sb("arena_att", [P, 2 * J * PADW * PADW + 2 * POS + NK * P + 2 * P])
        conv_cols, mem_cols, att_cols = carve(arena_conv), carve(arena_mem), carve(arena_att)

        xs = sb("xs_sb", [P, 2, BANK])
        sq = sb("sq", [P, 2, BANK])
        band = conv_cols(2 * 3 * 2 * P)
        bandv = band[:, :].rearrange("p (q d m n) -> p q d m n", q=2, d=3, m=2)
        inv512 = sb("inv512", [P, P])
        gst = sb("gst", [P, 4, 256])
        xpad = conv_cols(2, B, C + 2)
        cstat = sb("cstat", [P, 2, 6])
        cmv = sb("cmv", [P, 2, 2])
        csum = sb("csum", [P, 2, 2])
        csm = sb("csm", [P, 8, 2])
        relu_p = conv_cols(2, BANK)
        relu_n = conv_cols(2, BANK)
        alpha_n = sb("alpha_n", [P, 1])

        xc = sb("xc", [P, POS])
        xn = sb("xn", [P, POS])
        nst = sb("nst", [P, J, 6])
        nmv = sb("nmv", [P, J, 2])
        nsm = sb("nsm", [P, 8, J])

        kraw = sb("kraw", [P, POS])
        qraw = sb("qraw", [P, POS])
        nrm = sb("nrm", [P, POS])
        qt = sb("qt", [P, POS])
        kbd = sb("kbd", [P, NS * TOK])
        vbd = sb("vbd", [P, NS * TOK])
        ktok = sb("ktok", [P, NS * P])
        gates = sb("gates", [6, POS])
        gsum = sb("gsum", [6, J * NS])
        vals = sb("vals", [6, J * NS])
        eta_e = sb("eta_e", [P, NS * 8])
        keep_e = sb("keep_e", [P, NS * 8])
        eta_d = sb("eta_d", [P, NS * J])
        keep_d = sb("keep_d", [P, NS * J])
        keep_now = sb("keep_now", [P, 12])
        lrn = sb("lrn", [P, NS])
        lrh = sb("lrh", [P, NS])
        we = mem_cols(3, 8 * C)
        w10 = mem_cols(J * E1)
        wd = mem_cols(3, J * E1)
        qe = mem_cols(3, 8 * C)
        q10 = mem_cols(J * E1)
        zero = sb("zero", [P, BANK])
        zero_bf = zero[:, 0:BANK // 2].bitcast(BF16)
        act_u = sb("act_u", [P, 2, P])
        z_sq = sb("z_sq", [P, 2, P])
        z_cp = sb("z_cp", [P, 2, P])
        z_y = sb("z_y", [P, 2, P])
        z_t = sb("z_t", [P, 2, P])
        z_t2 = sb("z_t2", [P, 2, P])
        z_s1 = sb("z_s1", [P, 2, P])
        z_s2 = sb("z_s2", [P, 2, P])
        z_g = sb("z_g", [P, 2, P])
        h1bd = sb("h1bd", [P, P])
        h1mv = sb("h1mv", [P, P])
        h1_tok = sb("h1_tok", [P, P])
        spread_h1 = sb("spread_h1", [P, J])
        rbd = sb("rbd", [P, P])
        dhbd = sb("dhbd", [P, P])
        dz = sb("dz", [P, 2, P])
        u_tok = sb("u_tok", [P, 2, P])
        dz_tok = sb("dz_tok", [P, 2, P])
        k_fbd = mem_cols(BANK)
        h1_fbd = mem_cols(BANK)
        r_fbd = mem_cols(BANK)
        dh_fbd = mem_cols(BANK)
        wme = sb("wme", [P, 3, C])
        wms = sb("wms", [P, 3, C])
        w11s = sb("w11s", [P, 2, C])
        w10s = sb("w10s", [P, E1])
        w10m = sb("w10m", [P, E1])
        w11m = sb("w11m", [P, E1])
        uf = sb("uf", [P, NT])
        hf = sb("hf", [P, POS])
        xh = sb("xh", [P, POS])

        aq = kraw
        kpad = att_cols(J, PADW, PADW)
        vpad = att_cols(J, PADW, PADW)
        prod = att_cols(2, POS)
        mx = att_cols(P)
        att = att_cols(NK, P)
        rs = att_cols(P)
        attx = (qraw, qt)

        SW, SH = B * W, H * W
        mem_again, att_again, conv_again = carve(arena_mem), carve(arena_att), carve(arena_conv)
        in_w = sb("in_w", [P, SW * (H + 1)])
        lam_w = mem_again(SW * (H + 1))
        lam_h = mem_again(SH * (B + 1))
        in_h = mem_again(SH * (B + 1))
        fw = att_again(SW * (H + 1))
        rw = att_again(SW * (H + 1))
        fh = att_again(SH * (B + 1))
        rh = conv_again(SH * (B + 1))
        oml = kbd
        sig_i = vbd
        silu = ktok
        og = uf
        nbias = sb("nbias", [P, 1])
        tot = conv_again(NT)
        yc = qraw
        ysq = qt
        xo = xh[:, :].rearrange("p (q j n) -> p q j n", q=2, j=J)

        def seq_w(buf, lo, hi):
            return buf[:, :].rearrange("p (b w s) -> p b s w", b=B, w=W)[:, lo:hi, 1:H + 1, :]

        def seq_h(buf, lo, hi):
            return buf[:, :].rearrange("p (h w s) -> p s h w", h=H, w=W)[:, 1 + lo:1 + hi, :, :]

        def bhw(ap, n=B):
            return ap.rearrange("p (b h w) -> p b h w", b=n, h=H)

        def halves(buf_cols, b2):
            return buf_cols.rearrange("p (j g w) -> p j g w", j=J, g=BH)[64 * b2:64 * b2 + 64, :, b2, :]

        block = ctx.enter_context(nc.Block())

        @block.sync
        def _(sp):
            sp.dma_start(xs[:, :, :], xs_d).then_inc(sem("x_in"), 16)
            sp.dma_start(const[:, :], const_d).then_inc(sem("const_in"), 16)
            sp.dma_start(band[:, :], band_d).then_inc(sem("band_in"), 16)
            sp.dma_start(param[:, :], param_d).then_inc(sem("param_in"), 16)
            for q in range(2):
                sp.wait_ge(sem("xo_ready"), q + 1)
                sp.dma_start(out_d[:, q, :, :], xo[:, q, :, :]).then_inc(sem("out_done"), 16)
            sp.wait_ge(sem("out_done"), 32)

        @block.gpsimd
        def _(pool):
            pool.memset(inv512[:, :], 1.0 / 512.0).then_inc(sem("inv512_set"), 1)
            pool.memset(xpad[:, :, :, :], 0.0).then_inc(sem("xpad_zero"), 1)
            pool.memset(zero[:, :], 0.0).then_inc(sem("zero_set"), 1)
            pool.memset(kbd[:, :], 0.0).then_inc(sem("bd_zero"), 1)
            pool.memset(vbd[:, :], 0.0).then_inc(sem("bd_zero"), 1)
            pool.memset(h1bd[:, :], 0.0).then_inc(sem("bd_zero"), 1)
            pool.memset(rbd[:, :], 0.0).then_inc(sem("bd_zero"), 1)
            pool.memset(dhbd[:, :], 0.0).then_inc(sem("bd_zero"), 1)
            pool.memset(r_fbd[:, :], 0.0).then_inc(sem("bd_zero"), 1)
            pool.memset(u_tok[:, 1, :], 0.0).then_inc(sem("bd_zero"), 1)
            pool.memset(kpad[:, :, :, :], 0.0).then_inc(sem("kv_zero"), 1)
            pool.memset(vpad[:, :, :, :], 0.0).then_inc(sem("kv_zero"), 1)
            pool.wait_ge(sem("const_in"), 16)
            pool.wait_ge(sem("coef_ready"), 1)
            pool.wait_ge(sem("ktok_ready"), 1)
            with pool.Fori(0, NS) as t:
                pool.wait_ge(sem("g10"), t + 1)
                pool.wait_ge(sem("ktok_ready"), 1)
                pool.tensor_tensor(k_fbd[:, :].rearrange("p (j n) -> p j n", j=J),
                                   ktok[:, bass.ts(t, P)].unsqueeze(1).broadcast_to([P, J, P]),
                                   cst("block_j").unsqueeze(2).broadcast_to([P, J, P]), ALU.mult).then_inc(sem("k_fbd"), 1)
                pool.tensor_copy(keep_now[:, 0:8], keep_e[:, bass.ts(t, 8)]).then_inc(sem("keep_now"), 1)
                pool.tensor_copy(keep_now[:, 8:12], keep_d[:, bass.ts(t, J)]).then_inc(sem("keep_now"), 1)
                pool.tensor_tensor(spread_h1[:, :], cst("block_j"), lrh[:, bass.ds(t, 1)].broadcast_to([P, J]),
                                   ALU.mult).then_inc(sem("keep_now"), 1)
                pool.wait_ge(sem("keep_now"), 3 * t + 3)

                def kept_part(m, new, done):
                    pool.wait_ge(sem(new), t + 1)
                    pool.tensor_tensor(qe[:, m, :].rearrange("p (b d) -> p b d", b=8),
                                       we[:, m, :].rearrange("p (b d) -> p b d", b=8),
                                       keep_now[:, 0:8].unsqueeze(2).broadcast_to([P, 8, C]),
                                       ALU.mult).then_inc(sem(done), 1)

                kept_part(1, "w11_new", "q_11")
                kept_part(2, "w21_new", "q_21")
                pool.wait_ge(sem("h1_ready"), t + 1)
                pool.wait_ge(sem("v_ready"), 2)
                pool.tensor_tensor(h1mv[:, :], h1bd[:, :], vbd[:, bass.ts(t, P)], ALU.subtract).then_inc(sem("h1mv"), 1)
                kept_part(0, "w20_new", "q_20")
                pool.wait_ge(sem("w10_new"), t + 1)
                pool.tensor_tensor(q10[:, :].rearrange("p (j e) -> p j e", j=J), w10[:, :].rearrange("p (j e) -> p j e", j=J),
                                   keep_now[:, 8:12].unsqueeze(2).broadcast_to([P, J, E1]),
                                   ALU.mult).then_inc(sem("q_10"), 1)
                pool.wait_ge(sem("h1_tok"), t + 1)
                pool.tensor_tensor(h1_fbd[:, :].rearrange("p (j n) -> p j n", j=J),
                                   h1_tok[:, :].unsqueeze(1).broadcast_to([P, J, P]),
                                   spread_h1[:, :].unsqueeze(2).broadcast_to([P, J, P]), ALU.mult).then_inc(sem("h1_fbd"), 1)
            pool.wait_ge(sem("hf_done"), 2)
            for buf, n in ((lam_w, H), (in_w, H), (lam_h, B), (in_h, B)):
                pool.memset(buf[:, :].rearrange("p (n s) -> p n s", s=n + 1)[:, :, 0], 0.0).then_inc(sem("scan_zero"), 1)

        @block.scalar
        def _(act):
            act.wait_ge(sem("x_in"), 16)
            act.activation(sq[:, :, :], xs[:, :, :], ACT.Square).then_inc(sem("sq0"), 1)
            act.wait_ge(sem("const_in"), 16)
            act.wait_ge(sem("gvar0"), 1)
            act.activation(gst[:, 3, :], gst[:, 2, :], ACT.Sqrt, bias=cst("eps")).then_inc(sem("gstd0"), 1)
            act.wait_ge(sem("cvar"), 1)
            act.activation(csm[:, 2, :], csm[:, 1, :], ACT.Sqrt, bias=cst("eps")).then_inc(sem("cstd"), 1)
            act.wait_ge(sem("caff"), 1)
            for m in range(2):
                act.activation(relu_p[:, m, :], ps[:, m, :], ACT.Relu, bias=csm[:, 5, m:m + 1], scale=csm[:, 4, m:m + 1])
                act.activation(relu_n[:, m, :], ps[:, m, :], ACT.Relu, bias=csm[:, 7, m:m + 1],
                               scale=csm[:, 6, m:m + 1]).then_inc(sem("relu"), 1)
            act.wait_ge(sem("x1_tp"), 1)
            act.activation(xc[:, :], psf[:, 2 * BANK:4 * BANK], ACT.Copy).then_inc(sem("x1_ready"), 1)
            act.wait_ge(sem("nvar"), 1)
            act.activation(nsm[:, 2, :], nsm[:, 1, :], ACT.Sqrt, bias=cst("eps")).then_inc(sem("nstd"), 1)
            for n, raw in ((0, kraw), (1, qraw)):
                act.wait_ge(sem("kq_done"), n + 1)
                act.activation(raw[:, :], psf[:, 2 * n * BANK:(2 * n + 2) * BANK], ACT.Copy)
                act.activation(sq[:, :, :], ps[:, 2 * n:2 * n + 2, :], ACT.Square).then_inc(sem("kq_sq"), 1)
                act.wait_ge(sem("kq_sum"), n + 1)
                act.activation(nrm[:, :], psf[:, 4 * BANK:6 * BANK], ACT.Sqrt).then_inc(sem("kq_norm"), 1)
                act.wait_ge(sem("kq_unit"), n + 1)
            act.wait_ge(sem("bd_zero"), 5)
            act.wait_ge(sem("v_done"), 1)
            for b2 in range(BH):
                act.activation(vbd[:, :].rearrange("p (t j g w) -> p g t j w", t=NS, j=J, g=BH)[64 * b2:64 * b2 + 64, b2],
                               psf[64 * b2:64 * b2 + 64, 6 * BANK:8 * BANK].rearrange("p (j t w) -> p t j w", j=J, t=NS),
                               ACT.Copy).then_inc(sem("v_ready"), 1)
            act.wait_ge(sem("gate_done"), 1)
            act.activation(gates[:, :], psf[0:6, 0:POS], ACT.Sigmoid).then_inc(sem("gate_sig"), 1)
            act.preload_act_table_set("gelu_apprx_tanh_and_others")
            with act.Fori(0, NS) as t:
                def hidden(i, done, ready, kept):
                    act.wait_ge(sem(done), t + 1)
                    act.activation(act_u[:, i, :], ps[:, 4, P * i:P * i + P], ACT.Gelu_apprx_tanh).then_inc(sem(ready), 1)
                    act.activation(z_sq[:, i, :], ps[:, 4, P * i:P * i + P], ACT.Square)
                    act.activation(z_cp[:, i, :], ps[:, 4, P * i:P * i + P], ACT.Copy).then_inc(sem(kept), 1)

                def tanh(i, y, th):
                    act.wait_ge(sem(y), t + 1)
                    act.activation(z_t[:, i, :], z_y[:, i, :], ACT.Tanh, scale=GS * GC).then_inc(sem(th), 1)

                def tanh_sq(i, th, t2):
                    act.wait_ge(sem(th), t + 1)
                    act.activation(z_t2[:, i, :], z_t[:, i, :], ACT.Square).then_inc(sem(t2), 1)

                def turned(m, bank, tp, cp):
                    act.wait_ge(sem(tp), t + 1)
                    act.activation(wd[:, m, :], ps[:, bank, :], ACT.Copy).then_inc(sem(cp), 1)

                def token_rows(out, bank, col, tp, done):
                    act.wait_ge(sem(tp), t + 1)
                    act.activation(out, ps[:, bank, col:col + P], ACT.Copy).then_inc(sem(done), 1)

                hidden(0, "z0_done", "u0_ready", "z0_kept")
                turned(1, 7, "w11_tp", "w11_d")
                token_rows(u_tok[:, 0, :], 7, P, "u0_tp", "u0_tok")
                tanh(0, "y0", "tanh0")
                turned(2, 6, "w21_tp", "w21_d")
                tanh_sq(0, "tanh0", "t2_0")
                hidden(1, "z1_done", "u1_ready", "z1_kept")
                turned(0, 6, "w20_tp", "w20_d")
                token_rows(h1_tok[:, :], 7, 0, "h1_tp", "h1_tok")
                tanh(1, "y1", "tanh1")
                tanh_sq(1, "tanh1", "t2_1")
                token_rows(u_tok[:, 1, :], 7, P, "u1_tp", "u1_tok")
                token_rows(dz_tok[:, 1, :], 6, 2 * P, "dz1_tp", "dz1_tok")
                token_rows(dz_tok[:, 0, :], 6, 3 * P, "dz0_tp", "dz0_tok")

            act.wait_ge(sem("wm_tp"), 1)
            act.activation(w10m[:, :], ps[:, 4, 0:E1], ACT.Copy, scale=1.0 / B)
            act.activation(w11m[:, :], ps[:, 4, E1:2 * E1], ACT.Copy).then_inc(sem("wm_ready"), 1)
            for i in range(2):
                for n in range(4):
                    act.wait_ge(sem("zf_done"), 4 * i + n + 1)
                    act.activation(uf[:, n * BANK:(n + 1) * BANK], ps[:, n, :], ACT.Gelu_apprx_tanh).then_inc(sem("uf_ready"), 1)

            act.wait_ge(sem("nvar"), 2)
            act.activation(nsm[:, 2, :], nsm[:, 1, :], ACT.Sqrt, bias=cst("eps")).then_inc(sem("nstd"), 1)
            act.wait_ge(sem("aqkv_done"), 1)
            act.activation(aq[:, :], psf[:, 0:2 * BANK], ACT.Copy).then_inc(sem("aq_ready"), 1)
            act.wait_ge(sem("kv_zero"), 2)
            act.wait_ge(sem("aqkv_done"), 3)
            act.activation(vpad[:, :, 3:3 + H, 3:3 + W], bhw(psf[:, 4 * BANK:6 * BANK], J), ACT.Copy).then_inc(sem("av_ready"), 1)
            act.wait_ge(sem("sub_ready"), 1)
            act.activation(att[:, :, :], att[:, :, :], ACT.Exp, scale=float((C // NHD) ** -0.5)).then_inc(sem("exp_done"), 1)

            act.wait_ge(sem("att_ready"), 1)
            for n in range(NK):
                if n >= 2:
                    act.wait_ge(sem("att_tp"), n - 1)
                act.activation(attx[n % 2][:, :].rearrange("p (h d) -> p h d", d=C // NHD),
                               att[:, n, :].unsqueeze(2).broadcast_to([P, P, C // NHD]), ACT.Copy).then_inc(sem("attx_ready"), 1)

            act.wait_ge(sem("nvar"), 3)
            act.activation(nsm[:, 2, :], nsm[:, 1, :], ACT.Sqrt, bias=cst("eps")).then_inc(sem("nstd"), 1)
            act.wait_ge(sem("scan_zero"), 4)
            act.wait_ge(sem("nbias_set"), 1)
            for n in range(4):
                act.wait_ge(sem("feat_done"), n + 1)
                act.activation(seq_w(lam_w, 2 * n, 2 * n + 2), bhw(ps[:, n, :], 2), ACT.Sigmoid, bias=par("scan_b")[:, 0:1])
                act.activation(oml[:, n * BANK:(n + 1) * BANK], ps[:, n, :], ACT.Sigmoid, bias=nbias[:, :], scale=-1.0)\
                   .then_inc(sem("lam_ready"), 1)
            for n in range(4):
                act.wait_ge(sem("feat_done"), 4 + n + 1)
                act.activation(sig_i[:, n * BANK:(n + 1) * BANK], ps[:, 4 + n, :], ACT.Sigmoid, bias=par("scan_b")[:, 1:2])\
                   .then_inc(sem("sig_ready"), 1)
            for n in range(4):
                act.wait_ge(sem("feat_done"), 8 + n + 1)
                act.activation(og[:, n * BANK:(n + 1) * BANK], ps[:, n, :], ACT.Sigmoid, bias=par("scan_b")[:, 2:3])\
                   .then_inc(sem("og_ready"), 1)
            act.activation(seq_h(lam_h, 0, B), seq_w(lam_w, 0, B), ACT.Copy).then_inc(sem("lam_h"), 1)
            act.wait_ge(sem("in_w"), 4)
            act.activation(seq_h(in_h, 0, B), seq_w(in_w, 0, B), ACT.Copy).then_inc(sem("in_h"), 1)
            act.wait_ge(sem("yc_done"), 1)
            act.activation(yc[:, :], psf[:, 0:2 * BANK], ACT.Copy)
            act.activation(ysq[:, :], psf[:, 0:2 * BANK], ACT.Square).then_inc(sem("ysq"), 1)
            act.wait_ge(sem("yvar_done"), 1)
            act.activation(nrm[:, :], psf[:, 2 * BANK:4 * BANK], ACT.Sqrt, scale=1.0 / C, bias=cst("eps")).then_inc(sem("ystd"), 1)
            for q in range(2):
                act.wait_ge(sem("xo_tp"), q + 1)
                act.activation(xo[:, q, :, :], ps[:, 6 + q, :].rearrange("p (j n) -> p j n", j=J), ACT.Copy)\
                   .then_inc(sem("xo_ready"), 1)

        @block.vector
        def _(dve):
            linked = [0]

            def link(ins):
                linked[0] += 1
                ins.then_inc(sem("dve_link"), 1)
                dve.wait_ge(sem("dve_link"), linked[0])

            dve.wait_ge(sem("gsum0"), 1)
            dve.tensor_reduce(gst[:, 0, :], ps[:, 0, :].rearrange("p (g k) -> p g k", k=2), AX_X, ALU.add)
            link(dve.tensor_reduce(gst[:, 1, :], ps[:, 1, :].rearrange("p (g k) -> p g k", k=2), AX_X, ALU.add))
            link(dve.tensor_tensor(gst[:, 2, :], gst[:, 0, :], gst[:, 0, :], ALU.mult))
            dve.tensor_tensor(gst[:, 2, :], gst[:, 1, :], gst[:, 2, :], ALU.subtract).then_inc(sem("gvar0"), 1)
            dve.wait_ge(sem("gstd0"), 1)
            link(dve.reciprocal(gst[:, 3, :], gst[:, 3, :]))

            def group_cols(row):
                return gst[:, row, :].rearrange("p (b g) -> p b g", b=B).unsqueeze(3).broadcast_to([P, B, C // 2, 2])

            dve.wait_ge(sem("xpad_zero"), 1)
            for q in range(2):
                inner = xpad[:, q, :, 1:C + 1].rearrange("p b (g k) -> p b g k", k=2)
                link(dve.tensor_tensor(inner, xs[:, q, :].rearrange("p (b g k) -> p b g k", b=B, k=2), group_cols(0), ALU.subtract))
                dve.tensor_tensor(inner, inner, group_cols(3), ALU.mult).then_inc(sem("xpad_ready"), 1)

            dve.wait_ge(sem("param_in"), 16)
            for m in range(2):
                dve.wait_ge(sem("conv_done"), m + 1)
                link(dve.bn_stats(cstat[:, m, :], ps[:, m, :]))
                link(dve.bn_aggr(cmv[:, m, :], cstat[:, m, :]))
            mean, var = cmv[:, :, 0], cmv[:, :, 1]
            link(dve.tensor_tensor(csum[:, 0, :], mean, par("conv_bias"), ALU.add))
            link(dve.tensor_tensor(csum[:, 1, :], csum[:, 0, :], csum[:, 0, :], ALU.mult))
            dve.tensor_tensor(csum[:, 1, :], csum[:, 1, :], var, ALU.add).then_inc(sem("csum"), 1)
            dve.wait_ge(sem("cgroup"), 1)
            link(dve.tensor_copy(csm[:, 0:2, :], ps[:, 2, 0:4].rearrange("p (s m) -> p s m", s=2)))
            link(dve.tensor_tensor(csm[:, 3, :], csm[:, 0, :], csm[:, 0, :], ALU.mult))
            dve.tensor_tensor(csm[:, 1, :], csm[:, 1, :], csm[:, 3, :], ALU.subtract).then_inc(sem("cvar"), 1)
            dve.wait_ge(sem("cstd"), 1)
            link(dve.reciprocal(csm[:, 2, :], csm[:, 2, :]))
            link(dve.tensor_tensor(csm[:, 4, :], csm[:, 2, :], par("conv_gamma"), ALU.mult))
            link(dve.tensor_tensor(csm[:, 3, :], par("conv_bias"), csm[:, 0, :], ALU.subtract))
            link(dve.tensor_tensor(csm[:, 3, :], csm[:, 3, :], csm[:, 4, :], ALU.mult))
            link(dve.tensor_tensor(csm[:, 5, :], csm[:, 3, :], par("conv_beta"), ALU.add))
            dve.tensor_scalar(alpha_n[:, :], par("conv_alpha"), -1.0, None, ALU.mult)
            dve.tensor_scalar(csm[:, 6:8, :], csm[:, 4:6, :], -1.0, None, ALU.mult).then_inc(sem("caff"), 1)
            for m in range(2):
                dve.wait_ge(sem("relu"), m + 1)
                link(dve.tensor_tensor(xs[:, m, :], xs[:, m, :], relu_p[:, m, :], ALU.add))
                dve.scalar_tensor_tensor(xs[:, m, :], relu_n[:, m, :], alpha_n[:, 0:1], xs[:, m, :], ALU.mult, ALU.add)\
                   .then_inc(sem("x1_rows"), 1)

            def group_norm(n):
                for j in range(J):
                    dve.bn_stats(nst[:, j, :], xc[:, j * HW:(j + 1) * HW]).then_inc(sem("bn_part"), 1)
                dve.wait_ge(sem("bn_part"), J * (n + 1))
                for j in range(J):
                    last = dve.bn_aggr(nmv[:, j, :], nst[:, j, :])
                link(last)
                link(dve.tensor_tensor(nsm[:, 4, :], nmv[:, :, 0], nmv[:, :, 0], ALU.mult))
                dve.tensor_copy(nsm[:, 6, :], nmv[:, :, 0])
                dve.tensor_tensor(nsm[:, 7, :], nsm[:, 4, :], nmv[:, :, 1], ALU.add).then_inc(sem("npart"), 1)
                dve.wait_ge(sem("ngroup"), n + 1)
                link(dve.tensor_copy(nsm[:, 0:2, :], ps[:, 7, 0:2 * J].rearrange("p (s j) -> p s j", s=2)))
                link(dve.tensor_tensor(nsm[:, 3, :], nsm[:, 0, :], nsm[:, 0, :], ALU.mult))
                dve.tensor_tensor(nsm[:, 1, :], nsm[:, 1, :], nsm[:, 3, :], ALU.subtract).then_inc(sem("nvar"), 1)
                dve.wait_ge(sem("nstd"), n + 1)
                link(dve.reciprocal(nsm[:, 5, :], nsm[:, 2, :]))
                for j in range(J):
                    dve.tensor_scalar(xn[:, j * HW:(j + 1) * HW], xc[:, j * HW:(j + 1) * HW], nsm[:, 0, j:j + 1],
                                      nsm[:, 5, j:j + 1], ALU.subtract, ALU.mult).then_inc(sem("xn_ready"), 1)

            dve.wait_ge(sem("x1_ready"), 1)
            group_norm(0)
            for m, new, buf in ((0, "w20_new", we), (1, "w11_new", we), (2, "q_21", qe)):
                dve.tensor_copy(buf[:, m, :].rearrange("p (b d) -> p b d", b=8),
                                par("mats_e")[:, m * C:(m + 1) * C].unsqueeze(1).broadcast_to([P, 8, C])).then_inc(sem(new), 1)
            dve.tensor_copy(w10[:, :].rearrange("p (j e) -> p j e", j=J), par("w1_0").unsqueeze(1).broadcast_to([P, J, E1]))\
               .then_inc(sem("w10_new"), 1)
            for n in range(2):
                dve.wait_ge(sem("kq_norm"), n + 1)
                link(dve.tensor_scalar(nrm[:, :], nrm[:, :], 1e-12, None, ALU.max))
                link(dve.reciprocal(nrm[:, :], nrm[:, :]))
                if n == 0:
                    dve.wait_ge(sem("bd_zero"), 5)
                    for b2 in range(BH):
                        s = slice(64 * b2, 64 * b2 + 64)
                        last = dve.tensor_tensor(kbd[:, :].rearrange("p (t j g w) -> p g t j w", t=NS, j=J, g=BH)[s, b2],
                                                 kraw[s, :].rearrange("p (j t w) -> p t j w", j=J, t=NS),
                                                 nrm[s, :].rearrange("p (j t w) -> p t j w", j=J, t=NS), ALU.mult)
                    last.then_inc(sem("kq_unit"), 1)
                else:
                    dve.tensor_tensor(qt[:, :], qraw[:, :], nrm[:, :], ALU.mult).then_inc(sem("kq_unit"), 1)
            dve.wait_ge(sem("gate_sig"), 1)
            link(dve.tensor_reduce(gsum[:, :], gates[:, :].rearrange("p (n w) -> p n w", w=W), AX_X, ALU.add))
            dve.tensor_scalar(vals[:, :], gsum[:, :], cst("gate_scale", 6)[:, 0:1], cst("gate_scale", 6)[:, 1:2], ALU.mult, ALU.add)\
               .then_inc(sem("vals"), 1)
            dve.wait_ge(sem("coef_ps"), 1)
            for i, buf in ((0, eta_e), (1, keep_e)):
                dve.tensor_copy(buf[:, :].rearrange("p (t j g) -> p g j t", t=NS, j=J),
                                ps[:, 7, 128 * i:128 * i + 128].rearrange("p (g j t) -> p g j t", g=BH, j=J))
            for i, buf in ((0, eta_d), (1, keep_d)):
                dve.tensor_copy(buf[:, :].rearrange("p (t j) -> p j t", t=NS),
                                ps[:, 7, 256 + 64 * i:320 + 64 * i].rearrange("p (j t) -> p j t", j=J))
            dve.tensor_copy(lrn[:, :], ps[:, 7, 384:384 + NS])
            dve.tensor_scalar(lrh[:, :], ps[:, 7, 384:384 + NS], 0.5, None, ALU.mult).then_inc(sem("coef_ready"), 1)
            dve.wait_ge(sem("coef_ready"), 1)
            dve.wait_ge(sem("ktok_tp"), 1)
            dve.tensor_tensor(ktok[:, :].rearrange("p (t n) -> p t n", t=NS),
                              psf[:, 2 * BANK:6 * BANK].rearrange("p (t n) -> p t n", t=NS),
                              lrh[:, :].unsqueeze(2).broadcast_to([P, NS, P]), ALU.mult).then_inc(sem("ktok_ready"), 1)
            dve.wait_ge(sem("m_zero"), 3)
            dve.wait_ge(sem("g10"), 1)
            dve.wait_ge(sem("v_ready"), 2)

            with dve.Fori(0, NS) as t:
                def mom_scale(m, done):
                    if m < 3:
                        v = ps[:, m, :].rearrange("p (b d) -> p b d", b=8)
                        dve.tensor_tensor(v, v, eta_e[:, bass.ts(t, 8)].unsqueeze(2).broadcast_to([P, 8, C]), ALU.mult)\
                           .then_inc(sem(done), 1)
                    else:
                        v = ps[:, 3, :].rearrange("p (j e) -> p j e", j=J)
                        dve.tensor_tensor(v, v, eta_d[:, bass.ts(t, J)].unsqueeze(2).broadcast_to([P, J, E1]), ALU.mult)\
                           .then_inc(sem(done), 1)

                def arg(i, kept, y):
                    dve.wait_ge(sem(kept), t + 1)
                    dve.scalar_tensor_tensor(z_y[:, i, :], z_sq[:, i, :], 1.0 / GC, z_cp[:, i, :], ALU.add, ALU.mult)\
                       .then_inc(sem(y), 1)

                def slope_1(i, t2, s1):
                    dve.wait_ge(sem(t2), t + 1)
                    dve.scalar_tensor_tensor(z_s1[:, i, :], z_t2[:, i, :], -1.0, z_cp[:, i, :], ALU.add, ALU.mult).then_inc(sem(s1), 1)

                def slope_2(i, s1, s2):
                    dve.wait_ge(sem(s1), t + 1)
                    dve.scalar_tensor_tensor(z_s2[:, i, :], z_sq[:, i, :], 1.0 / (3.0 * GC), z_s1[:, i, :], ALU.add, ALU.mult)\
                       .then_inc(sem(s2), 1)

                def slope_3(i, s2, g):
                    dve.wait_ge(sem(s2), t + 1)
                    dve.scalar_tensor_tensor(z_g[:, i, :], z_s2[:, i, :], -3.0 * GC * GS, z_t[:, i, :], ALU.mult, ALU.add)\
                       .then_inc(sem(g), 1)

                def by_pair(out, col, tp, done, scale):
                    dve.wait_ge(sem(tp), t + 1)
                    dve.scalar_tensor_tensor(out[:, :].rearrange("p (j n) -> p j n", j=J),
                                             ps[:, 7, col:col + P].unsqueeze(1).broadcast_to([P, J, P]), scale,
                                             cst("block_j").unsqueeze(2).broadcast_to([P, J, P]), ALU.mult, ALU.mult)\
                       .then_inc(sem(done), 1)

                def updated(m, grad, q, done):
                    dve.wait_ge(sem(grad), t + (1 if m < 3 else 2))
                    dve.wait_ge(sem(q), t + 1)
                    if m < 3:
                        dve.tensor_tensor(we[:, m, :], ps[:, m, :], qe[:, m, :], ALU.add).then_inc(sem(done), 1)
                    else:
                        dve.tensor_tensor(w10[:, :], ps[:, 3, :], q10[:, :], ALU.add).then_inc(sem(done), 1)

                mom_scale(1, "m11_scaled")
                updated(2, "g21", "q_21", "w21_new")
                dve.wait_ge(sem("h1_ps"), t + 1)
                for b2 in range(BH):
                    last = dve.tensor_tensor(halves(h1bd[:, :], b2), halves(ps[:, 5, 0:P], b2),
                                             halves(kbd[:, bass.ts(t, P)], b2), ALU.add)
                last.then_inc(sem("h1_ready"), 1)
                arg(0, "z0_kept", "y0")
                mom_scale(0, "m20_scaled")
                mom_scale(2, "m21_scaled")
                slope_1(0, "t2_0", "s1_0")
                arg(1, "z1_kept", "y1")
                slope_2(0, "s1_0", "s2_0")
                slope_3(0, "s2_0", "g_0")
                dve.wait_ge(sem("h1mv"), t + 1)
                dve.wait_ge(sem("h2_ps"), t + 1)
                for b2 in range(BH):
                    last = dve.tensor_tensor(halves(rbd[:, :], b2), halves(ps[:, 5, P:2 * P], b2), halves(h1mv[:, :], b2), ALU.add)
                last.then_inc(sem("r_ready"), 1)
                slope_1(1, "t2_1", "s1_1")
                slope_2(1, "s1_1", "s2_1")
                slope_3(1, "s2_1", "g_1")
                dve.wait_ge(sem("g_1"), t + 1)
                dve.wait_ge(sem("du1_done"), t + 1)
                dve.scalar_tensor_tensor(dz[:, 1, :], z_g[:, 1, :], 1.0, ps[:, 4, 2 * P:3 * P], ALU.add, ALU.mult).then_inc(sem("dz1_ready"), 1)
                by_pair(r_fbd, 2 * P, "r_tp", "r_fbd", lrn[:, bass.ds(t, 1)])
                dve.wait_ge(sem("r_ready"), t + 1)
                dve.wait_ge(sem("dh1_ps"), t + 1)
                for b2 in range(BH):
                    last = dve.scalar_tensor_tensor(halves(dhbd[:, :], b2), halves(ps[:, 5, 2 * P:3 * P], b2), 0.5,
                                                    halves(rbd[:, :], b2), ALU.mult, ALU.add)
                last.then_inc(sem("dh1_ready"), 1)
                mom_scale(3, "m10_scaled")
                dve.wait_ge(sem("g_0"), t + 1)
                dve.wait_ge(sem("du0_done"), t + 1)
                dve.scalar_tensor_tensor(dz[:, 0, :], z_g[:, 0, :], 1.0, ps[:, 4, 3 * P:4 * P], ALU.add, ALU.mult).then_inc(sem("dz0_ready"), 1)
                by_pair(dh_fbd, 3 * P, "dh1_tp", "dh_fbd", lrn[:, bass.ds(t, 1)])
                updated(1, "g11", "q_11", "w11_new")
                updated(3, "g10", "q_10", "w10_new")
                updated(0, "g20", "q_20", "w20_new")

            dve.wait_ge(sem("g21"), NS + 1)
            dve.wait_ge(sem("q_21"), NS + 1)
            dve.tensor_tensor(we[:, 2, :], ps[:, 2, :], qe[:, 2, :], ALU.add).then_inc(sem("w21_new"), 1)

            dve.wait_ge(sem("w10_new"), NS + 1)
            dve.wait_ge(sem("w21_new"), NS + 1)
            dve.tensor_reduce(wms[:, :, :], we[:, :, :].rearrange("p m (b d) -> p m d b", b=8), AX_X, ALU.add)
            link(dve.tensor_reduce(w10s[:, :], w10[:, :].rearrange("p (j e) -> p e j", j=J), AX_X, ALU.add))
            dve.tensor_scalar(w11s[:, :, :], wms[:, 1, :].unsqueeze(1).broadcast_to([P, 2, C]), 1.0 / B, None, ALU.mult)
            dve.tensor_scalar(wme[:, :, :], wms[:, :, :], 1.0 / B, None, ALU.mult).then_inc(sem("wm_sum"), 1)
            dve.wait_ge(sem("hf_done"), 1)
            link(dve.tensor_tensor(hf[:, :], psf[:, 4 * BANK:6 * BANK], qt[:, :], ALU.add))
            dve.tensor_tensor(xh[:, :], xc[:, :], hf[:, :], ALU.add).then_inc(sem("hf_ready"), 1)
            dve.wait_ge(sem("hf_ready"), 1)
            dve.wait_ge(sem("hf_done"), 2)
            link(dve.tensor_tensor(xc[:, :], psf[:, 6 * BANK:8 * BANK], xh[:, :], ALU.add))
            group_norm(1)

            dve.wait_ge(sem("kv_zero"), 1)
            dve.wait_ge(sem("aqkv_done"), 2)
            dve.tensor_copy(kpad[:, :, 3:3 + H, 3:3 + W], bhw(psf[:, 2 * BANK:4 * BANK], J)).then_inc(sem("ak_ready"), 1)
            dve.wait_ge(sem("ak_ready"), 1)
            dve.wait_ge(sem("aq_ready"), 1)

            def shifted(buf, n):
                dy, dx = 3 * (n // 3), 3 * (n % 3)
                return buf[:, :, dy:dy + H, dx:dx + W]

            for n in range(NK):
                if n >= 2:
                    dve.wait_ge(sem("score_done"), n - 1)
                dve.tensor_tensor(bhw(prod[:, n % 2, :], J), bhw(aq[:, :], J), shifted(kpad, n), ALU.mult).then_inc(sem("qk_ready"), 1)
            dve.wait_ge(sem("score_done"), NK)
            s_all = psf[:, 0:NK * P]
            link(dve.tensor_reduce(mx[:, :], s_all.rearrange("p (k n) -> p n k", k=NK), AX_X, ALU.max))
            dve.tensor_tensor(att[:, :, :], s_all.rearrange("p (k n) -> p k n", k=NK),
                              mx[:, :].unsqueeze(1).broadcast_to([P, NK, P]), ALU.subtract).then_inc(sem("sub_ready"), 1)
            dve.wait_ge(sem("exp_done"), 1)
            link(dve.tensor_reduce(rs[:, :], att[:, :, :].rearrange("p k n -> p n k"), AX_X, ALU.add))
            link(dve.reciprocal(rs[:, :], rs[:, :]))
            dve.tensor_tensor(att[:, :, :], att[:, :, :], rs[:, :].unsqueeze(1).broadcast_to([P, NK, P]), ALU.mult)\
               .then_inc(sem("att_ready"), 1)
            dve.wait_ge(sem("av_ready"), 1)
            for n in range(NK):
                dve.wait_ge(sem("att_tp"), n + 1)
                if n >= 2:
                    dve.wait_ge(sem("av_done"), n - 1)
                a0 = (2 if n % 2 else 0) * BANK
                dve.tensor_tensor(bhw(prod[:, n % 2, :], J), bhw(psf[:, a0:a0 + 2 * BANK], J), shifted(vpad, n), ALU.mult)\
                   .then_inc(sem("pv_ready"), 1)
            dve.wait_ge(sem("av_done"), NK)
            link(dve.tensor_tensor(xc[:, :], psf[:, 4 * BANK:6 * BANK], xc[:, :], ALU.add))
            group_norm(2)

            dve.tensor_scalar(nbias[:, :], par("scan_b")[:, 0:1], -1.0, None, ALU.mult).then_inc(sem("nbias_set"), 1)
            for n in range(4):
                cols = slice(n * BANK, (n + 1) * BANK)
                dve.wait_ge(sem("lam_ready"), n + 1)
                dve.wait_ge(sem("sig_ready"), n + 1)
                link(dve.scalar_tensor_tensor(silu[:, cols], ps[:, 4 + n, :], par("scan_b")[:, 1:2], sig_i[:, cols], ALU.add, ALU.mult))
                dve.tensor_tensor(seq_w(in_w, 2 * n, 2 * n + 2), bhw(silu[:, cols], 2), bhw(oml[:, cols], 2), ALU.mult)\
                   .then_inc(sem("in_w"), 1)
            dve.wait_ge(sem("in_w"), 4)
            dve.tensor_tensor_scan(fw[:, :], lam_w[:, :], in_w[:, :], 0.0, ALU.mult, ALU.add)
            link(dve.tensor_tensor_scan(rw[:, ::-1], lam_w[:, ::-1], in_w[:, ::-1], 0.0, ALU.mult, ALU.add))
            link(dve.tensor_tensor(fw[:, :], fw[:, :], rw[:, :], ALU.add))
            dve.wait_ge(sem("lam_h"), 1)
            dve.wait_ge(sem("in_h"), 1)
            dve.tensor_tensor_scan(fh[:, :], lam_h[:, :], in_h[:, :], 0.0, ALU.mult, ALU.add)
            link(dve.tensor_tensor_scan(rh[:, ::-1], lam_h[:, ::-1], in_h[:, ::-1], 0.0, ALU.mult, ALU.add))
            link(dve.tensor_tensor(fh[:, :], fh[:, :], rh[:, :], ALU.add))
            link(dve.tensor_tensor(bhw(tot[:, :]), seq_w(fw, 0, B), seq_h(fh, 0, B), ALU.add))
            dve.wait_ge(sem("og_ready"), 4)
            dve.tensor_tensor(tot[:, :], tot[:, :], og[:, :], ALU.mult).then_inc(sem("tot_ready"), 1)
            dve.wait_ge(sem("ystd"), 1)
            link(dve.reciprocal(nrm[:, :], nrm[:, :]))
            link(dve.tensor_tensor(yc[:, :], yc[:, :], nrm[:, :], ALU.mult))
            dve.tensor_scalar(yc[:, :], yc[:, :], par("ln_gamma"), par("ln_beta"), ALU.mult, ALU.add).then_inc(sem("yn_ready"), 1)
            dve.wait_ge(sem("proj_done"), 1)
            dve.scalar_tensor_tensor(xc[:, :], psf[:, 4 * BANK:6 * BANK], par("out_b"), xc[:, :], ALU.add, ALU.add)\
               .then_inc(sem("x4_ready"), 1)

        @block.tensor
        def _(pe):
            pe.wait_ge(sem("inv512_set"), 1)
            pe.wait_ge(sem("x_in"), 16)
            for q in range(2):
                pe.matmul(ps[:, 0, :], inv512[:, :], xs[:, q, :], start=(q == 0), stop=(q == 1))
            pe.wait_ge(sem("sq0"), 1)
            for q in range(2):
                mm = pe.matmul(ps[:, 1, :], inv512[:, :], sq[:, q, :], start=(q == 0), stop=(q == 1))
            mm.then_inc(sem("gsum0"), 1)
            pe.wait_ge(sem("band_in"), 16)
            pe.wait_ge(sem("const_in"), 16)
            for m in range(2):
                for q in range(2):
                    pe.wait_ge(sem("xpad_ready"), q + 1)
                    for d in range(3):
                        mm = pe.matmul(ps[:, m, :], bandv[:, q, d, m, :], xpad[:, q, :, d:d + C],
                                       start=(q == 0 and d == 0), stop=(q == 1 and d == 2))
                mm.then_inc(sem("conv_done"), 1)
            pe.wait_ge(sem("csum"), 1)
            pe.matmul(ps[:, 2, 0:4], cst("sum16"), csum[:, :, :].rearrange("p s m -> p (s m)"), start=True, stop=True)\
              .then_inc(sem("cgroup"), 1)
            pe.wait_ge(sem("caff"), 1)
            pe.wait_ge(sem("x1_rows"), 2)
            for j in range(J):
                for q in range(2):
                    col = 2 * BANK + j * HW + q * P
                    mm = pe.transpose(psf[:, col:col + P], xs[:, q, j * P:(j + 1) * P], ident)
            mm.then_inc(sem("x1_tp"), 1)

            def norm_group(n):
                pe.wait_ge(sem("npart"), n + 1)
                pe.matmul(ps[:, 7, 0:2 * J], cst("pair_half"), nsm[:, 6:8, :].rearrange("p s j -> p (s j)"), start=True, stop=True)\
                  .then_inc(sem("ngroup"), 1)

            norm_group(0)
            pe.wait_ge(sem("param_in"), 16)
            pe.wait_ge(sem("xn_ready"), J)

            def project(bank, w, src):
                for n in range(2):
                    mm = pe.matmul(ps[:, bank + n, :], w, src[:, n * BANK:(n + 1) * BANK], start=True, stop=True)
                return mm

            project(0, par("wk"), xn).then_inc(sem("kq_done"), 1)
            project(2, par("wq"), xn).then_inc(sem("kq_done"), 1)
            project(6, par("wv"), xn).then_inc(sem("v_done"), 1)
            for n in range(2):
                pe.wait_ge(sem("kq_sq"), n + 1)
                if n:
                    pe.wait_ge(sem("kq_norm"), n)
                for i in range(2):
                    mm = pe.matmul(ps[:, 4 + i, :], cst("ones64"), sq[:, i, :], start=True, stop=True)
                mm.then_inc(sem("kq_sum"), 1)
            pe.wait_ge(sem("kq_sq"), 2)
            for n in range(2):
                mm = pe.matmul(ps[0:6, n, :], par("gates"), xn[:, n * BANK:(n + 1) * BANK], start=True, stop=True)
            mm.then_inc(sem("gate_done"), 1)
            pe.wait_ge(sem("kq_unit"), 1)
            pe.wait_ge(sem("kq_norm"), 2)
            for t in range(NS):
                mm = pe.transpose(psf[:, 2 * BANK + t * P:2 * BANK + (t + 1) * P], kbd[:, t * P:(t + 1) * P], ident)
            mm.then_inc(sem("ktok_tp"), 1)
            pe.wait_ge(sem("vals"), 1)
            pe.wait_ge(sem("v_ready"), 2)
            for i, gate in ((0, 2), (1, 1)):
                for b2 in range(BH):
                    r = 3 * b2 + gate
                    pe.matmul(ps[:, 7, 128 * i + 64 * b2:128 * i + 64 * b2 + 64], const[0:6, r:r + 1].broadcast_to([6, P]),
                              vals[:, :], start=True, stop=True)
                pe.matmul(ps[:, 7, 256 + 64 * i:320 + 64 * i], cst("half_sel", 6)[:, i * P:(i + 1) * P], vals[:, :], start=True, stop=True)
            for j in range(J):
                mm = pe.matmul(ps[:, 7, 384:384 + NS], cst("tok_sel", 6)[:, j * P:(j + 1) * P], vals[:, j * NS:(j + 1) * NS],
                               start=(j == 0), stop=(j == J - 1))
            mm.then_inc(sem("coef_ps"), 1)
            pe.wait_ge(sem("zero_set"), 1)
            pe.wait_ge(sem("ktok_ready"), 1)
            for m in range(4):
                pe.matmul(ps[:, m, :], zero[:, 0:P], zero[:, :], start=True, stop=True)\
                  .then_inc(sem("m_zero" if m < 3 else "g10"), 1)
            pe.wait_ge(sem("coef_ready"), 1)
            pe.wait_ge(sem("bd_zero"), 7)

            with pe.Fori(0, NS) as t:
                def per_pair(bank, col, w, x):
                    for j in range(J):
                        mm = pe.matmul(ps[:, bank, col + 32 * j:col + 32 * j + 32], w[:, P * j:P * j + P],
                                       x[:, 32 * j:32 * j + 32], start=True, stop=True)
                    return mm

                def turn(bank, col, x):
                    return pe.transpose(ps[:, bank, col:col + P], x, ident)

                def turn_weights(bank, m):
                    for j in range(J):
                        mm = turn(bank, P * j, we[:, m, P * j:P * j + P])
                    return mm

                def keep_warm(bank, n):
                    for _ in range(n):
                        pe.matmul(ps[:, bank, :], zero_bf[:, 0:P], zero_bf[:, :], start=True, stop=True)

                def gradient(m, left, right, half):
                    cols = slice(half * BANK // 2, (half + 1) * BANK // 2)
                    return pe.matmul(ps[:, m, cols], left, right[:, cols], start=False, stop=False, skip_group_check=True)

                pe.wait_ge(sem("w10_new"), t + 1)
                for j in range(J):
                    mm = pe.matmul(ps[:, 4, 32 * j:32 * j + 32], w10[:, P * j:P * j + P], kbd[:, bass.ds(t * P + 32 * j, 32)],
                                   start=True, stop=True)
                mm.then_inc(sem("z0_done"), 1)
                gradient(2, u_tok[:, 1, :], r_fbd, 1).then_inc(sem("g21"), 1)
                pe.wait_ge(sem("w11_new"), t + 1)
                turn_weights(7, 1).then_inc(sem("w11_tp"), 1)
                pe.wait_ge(sem("w20_new"), t + 1)
                pe.wait_ge(sem("u0_ready"), t + 1)
                per_pair(5, 0, we[:, 0, :], act_u[:, 0, :]).then_inc(sem("h1_ps"), 1)
                pe.wait_ge(sem("w21_new"), t + 1)
                turn_weights(6, 2).then_inc(sem("w21_tp"), 1)
                pe.wait_ge(sem("w11_d"), t + 1)
                turn(7, P, act_u[:, 0, :]).then_inc(sem("u0_tp"), 1)
                pe.wait_ge(sem("z0_kept"), t + 1)
                keep_warm(4, FILL[0])
                pe.wait_ge(sem("h1_ready"), t + 1)
                per_pair(4, P, wd[:, 1, :], h1bd).then_inc(sem("z1_done"), 1)
                pe.wait_ge(sem("u0_tok"), t + 1)
                turn(7, 0, h1bd[:, :]).then_inc(sem("h1_tp"), 1)
                pe.wait_ge(sem("w21_d"), t + 1)
                turn_weights(6, 0).then_inc(sem("w20_tp"), 1)
                keep_warm(5, FILL[1])
                pe.wait_ge(sem("u1_ready"), t + 1)
                per_pair(5, P, we[:, 2, :], act_u[:, 1, :]).then_inc(sem("h2_ps"), 1)
                pe.wait_ge(sem("h1_tok"), t + 1)
                turn(7, P, act_u[:, 1, :]).then_inc(sem("u1_tp"), 1)
                pe.wait_ge(sem("z1_kept"), t + 1)
                keep_warm(4, FILL[2])
                pe.wait_ge(sem("r_ready"), t + 1)
                per_pair(4, 2 * P, wd[:, 2, :], rbd).then_inc(sem("du1_done"), 1)
                pe.wait_ge(sem("u1_tok"), t + 1)
                turn(7, 2 * P, rbd[:, :]).then_inc(sem("r_tp"), 1)
                keep_warm(5, FILL[3])
                pe.wait_ge(sem("dz1_ready"), t + 1)
                per_pair(5, 2 * P, we[:, 1, :], dz[:, 1, :]).then_inc(sem("dh1_ps"), 1)
                pe.wait_ge(sem("w20_d"), t + 1)
                turn(6, 2 * P, dz[:, 1, :]).then_inc(sem("dz1_tp"), 1)
                pe.wait_ge(sem("m21_scaled"), t + 1)
                pe.wait_ge(sem("r_fbd"), t + 1)
                gradient(2, u_tok[:, 1, :], r_fbd, 0)
                pe.wait_ge(sem("dh1_ready"), t + 1)
                per_pair(4, 3 * P, wd[:, 0, :], dhbd).then_inc(sem("du0_done"), 1)
                turn(7, 3 * P, dhbd[:, :]).then_inc(sem("dh1_tp"), 1)
                pe.wait_ge(sem("dz1_tok"), t + 1)
                pe.wait_ge(sem("m11_scaled"), t + 1)
                pe.wait_ge(sem("h1_fbd"), t + 1)
                gradient(1, dz_tok[:, 1, :], h1_fbd, 0)
                pe.wait_ge(sem("dz0_ready"), t + 1)
                turn(6, 3 * P, dz[:, 0, :]).then_inc(sem("dz0_tp"), 1)
                gradient(1, dz_tok[:, 1, :], h1_fbd, 1).then_inc(sem("g11"), 1)
                pe.wait_ge(sem("m10_scaled"), t + 1)
                pe.wait_ge(sem("k_fbd"), t + 1)
                pe.wait_ge(sem("dz0_tok"), t + 1)
                for j in range(J):
                    mm = pe.matmul(ps[:, 3, P * j:P * j + P], k_fbd[:, P * j:P * j + P], dz_tok[:, 0, :], start=False, stop=False,
                                   skip_group_check=True)
                mm.then_inc(sem("g10"), 1)
                pe.wait_ge(sem("m20_scaled"), t + 1)
                pe.wait_ge(sem("dh_fbd"), t + 1)
                gradient(0, u_tok[:, 0, :], dh_fbd, 0)
                gradient(0, u_tok[:, 0, :], dh_fbd, 1).then_inc(sem("g20"), 1)

            pe.matmul(ps[:, 2, BANK // 2:], u_tok[:, 1, :], r_fbd[:, BANK // 2:], start=False, stop=False,
                      skip_group_check=True).then_inc(sem("g21"), 1)

            pe.wait_ge(sem("wm_sum"), 1)
            pe.matmul(ps[:, 4, 0:E1], cst("dup64"), w10s[:, :], start=True, stop=True)
            pe.transpose(ps[:, 4, E1:2 * E1], w11s[:, :, :].rearrange("p g d -> p (g d)"), ident).then_inc(sem("wm_tp"), 1)
            pe.wait_ge(sem("wm_ready"), 1)

            def up(w, src, i):
                for n in range(4):
                    bh, half = n // 2, n % 2
                    if i:
                        pe.wait_ge(sem("uf_ready"), 4 * i)
                    pe.matmul(ps[:, n, :], w[64 * bh:64 * bh + 64, :], src[64 * bh:64 * bh + 64, half * BANK:(half + 1) * BANK],
                              start=True, stop=True).then_inc(sem("zf_done"), 1)

            def down(w, bank, i):
                for n in range(4):
                    bh, half = n // 2, n % 2
                    pe.wait_ge(sem("uf_ready"), 4 * i + n + 1)
                    mm = pe.matmul(ps[64 * bh:64 * bh + 64, bank + half, :], w, uf[:, n * BANK:(n + 1) * BANK], start=True, stop=True)
                mm.then_inc(sem("hf_done"), 1)

            up(w10m, qt, 0)
            down(wme[:, 0, :], 4, 0)
            pe.wait_ge(sem("hf_ready"), 1)
            up(w11m, hf, 1)
            down(wme[:, 2, :], 6, 1)

            norm_group(1)
            pe.wait_ge(sem("xn_ready"), 2 * J)
            project(0, par("attn_q"), xn).then_inc(sem("aqkv_done"), 1)
            project(2, par("attn_k"), xn).then_inc(sem("aqkv_done"), 1)
            project(4, par("attn_v"), xn).then_inc(sem("aqkv_done"), 1)
            pe.wait_ge(sem("aq_ready"), 1)
            pe.wait_ge(sem("ak_ready"), 1)
            for n in range(NK):
                pe.wait_ge(sem("qk_ready"), n + 1)
                for i in range(8):
                    col = P * n + 16 * i
                    mm = pe.matmul(psf[:, col:col + 16], prod[:, n % 2, i * P:(i + 1) * P], cst("head_sel"), start=True, stop=True)
                mm.then_inc(sem("score_done"), 1)

            def turn_att(n):
                if n >= 2:
                    pe.wait_ge(sem("pv_ready"), n - 1)
                a0 = (2 if n % 2 else 0) * BANK
                pe.wait_ge(sem("attx_ready"), n + 1)
                for i in range(8):
                    mm = pe.transpose(psf[:, a0 + i * P:a0 + (i + 1) * P], attx[n % 2][:, i * P:(i + 1) * P], ident)
                mm.then_inc(sem("att_tp"), 1)

            pe.wait_ge(sem("av_ready"), 1)
            pe.wait_ge(sem("att_ready"), 1)
            turn_att(0)
            for n in range(NK):
                if n + 1 < NK:
                    turn_att(n + 1)
                pe.wait_ge(sem("pv_ready"), n + 1)
                for i in range(2):
                    mm = pe.matmul(ps[:, 4 + i, :], ident, prod[:, n % 2, i * BANK:(i + 1) * BANK], start=(n == 0), stop=(n == NK - 1))
                mm.then_inc(sem("av_done"), 1)

            norm_group(2)
            pe.wait_ge(sem("xn_ready"), 3 * J)
            for f in range(3):
                for n in range(4):
                    bh, half = n // 2, n % 2
                    bank = (4 if f == 1 else 0) + n
                    if f == 1 and n == 3:
                        pe.wait_ge(sem("nvar"), 3)
                    if f == 2:
                        pe.wait_ge(sem("lam_ready"), n + 1)
                    pe.matmul(ps[:, bank, :], par("scan_w")[64 * bh:64 * bh + 64, f * P:(f + 1) * P],
                              xn[64 * bh:64 * bh + 64, half * BANK:(half + 1) * BANK], start=True, stop=True).then_inc(sem("feat_done"), 1)
            pe.wait_ge(sem("tot_ready"), 1)
            for n in range(4):
                bh, half = n // 2, n % 2
                mm = pe.matmul(ps[64 * bh:64 * bh + 64, half, :], cst("center_d"), tot[:, n * BANK:(n + 1) * BANK], start=True, stop=True)
            mm.then_inc(sem("yc_done"), 1)
            pe.wait_ge(sem("ysq"), 1)
            for n in range(2):
                mm = pe.matmul(ps[:, 2 + n, :], cst("ones64"), ysq[:, n * BANK:(n + 1) * BANK], start=True, stop=True)
            mm.then_inc(sem("yvar_done"), 1)
            pe.wait_ge(sem("yn_ready"), 1)
            project(4, par("out_w"), yc).then_inc(sem("proj_done"), 1)
            pe.wait_ge(sem("x4_ready"), 1)
            for q in range(2):
                for j in range(J):
                    mm = pe.transpose(ps[:, 6 + q, j * P:(j + 1) * P], xc[:, j * HW + q * P:j * HW + (q + 1) * P], ident)
                mm.then_inc(sem("xo_tp"), 1)


def _constants():
    c = np.zeros((P, NCONST), np.float32)

    def put(name, value):
        a, b = CONST_COLS[name]
        v = np.asarray(value, np.float32).reshape(-1, b - a)
        c[:v.shape[0], a:b] = v

    i = np.arange(P)
    put("ident", np.eye(P))
    put("pair_half", 0.5 * (i[:, None] // 2 == i[None] // 2))
    put("sum16", (i[:, None] // 16 == i[None] // 16) / 16.0)
    put("ones64", i[:, None] // 64 == i[None] // 64)
    put("dup64", i[:, None] % 64 == i[None] % 64)
    put("head_sel", i[:, None] // 8 == np.arange(BH * NHD)[None])
    ch = 2 * (i // 4) + i % 2
    put("center_d", (ch[:, None] == np.arange(C)[None]) - 1.0 / C)
    put("block_j", i[:, None] // 32 == np.arange(J)[None])
    half = np.zeros((6, 2, BH, 64), np.float32)
    tok = np.zeros((6, J, J, BH, W), np.float32)
    for b2 in range(BH):
        half[3 * b2 + 2, 0, b2] = 1
        half[3 * b2 + 1, 1, b2] = 1
        for j in range(J):
            tok[3 * b2, j, j, b2] = 1
    put("half_sel", half.reshape(6, -1))
    put("tok_sel", tok.reshape(6, -1))
    one = [(-MAX_LR / W * GRAD_SCALE, 0.0), (-1.0 / W, 1.0), (1.0 / W, 0.0)]
    put("gate_scale", np.array(one * 2))
    put("eps", np.full((P, 1), GEPS))
    return c


def _block_diag(m):
    out = np.zeros((2 * m.shape[0], 2 * m.shape[1]), np.float32)
    out[:m.shape[0], :m.shape[1]] = m
    out[m.shape[0]:, m.shape[1]:] = m
    return out


def kernel(x, L0_conv_weight, L0_conv_bias, L0_conv_gamma, L0_conv_beta, L0_conv_alpha, L1_conv_Wq, L1_conv_Wk, L1_conv_Wv,
           L1_conv_w_lr, L1_conv_w_forget, L1_conv_w_eta, L1_conv_w1_0, L1_conv_w2_0, L1_conv_w1_1, L1_conv_w2_1,
           L2_conv_W_qkv, L3_conv_in_w, L3_conv_in_b, L3_conv_out_w, L3_conv_out_b, L3_conv_gamma, L3_conv_beta):
    import concourse.bacc as bacc
    from concourse.bass_utils import run_bass_kernel_spmd

    xs = np.asarray(x).reshape(BH, J, 2, P, C).transpose(3, 2, 1, 0, 4)
    w = np.asarray(L0_conv_weight).reshape(2, 8, 3, 3, 2, 8, 16)
    band = np.zeros((8, 16, 2, 3, 2, 8, 16), np.float32)
    for i in range(3):
        for l in range(16):
            if 0 <= l + i - 1 < 16:
                band[:, l + i - 1, :, :, :, :, l] = w[:, :, i, :, :, :, l].transpose(1, 0, 2, 3, 4)
    blk = np.zeros((P, NPARAM), np.float32)

    def put(name, value):
        a, b = PARAM_COLS[name]
        blk[:, a:b] = np.asarray(value).reshape(P, b - a)

    def rows16(v):
        return np.repeat(np.asarray(v).reshape(2, 8), 16, axis=1).T

    def twice(m):
        return np.concatenate([np.asarray(m)] * 2, axis=0)

    put("conv_bias", np.asarray(L0_conv_bias).reshape(2, P).T)
    put("conv_gamma", rows16(L0_conv_gamma))
    put("conv_beta", rows16(L0_conv_beta))
    put("conv_alpha", np.broadcast_to(np.asarray(L0_conv_alpha), (P, 1)))
    put("wk", _block_diag(np.asarray(L1_conv_Wk)))
    put("wv", _block_diag(np.asarray(L1_conv_Wv)))
    put("wq", _block_diag(np.asarray(L1_conv_Wq)))
    put("gates", _block_diag(np.stack([np.asarray(L1_conv_w_lr), np.asarray(L1_conv_w_forget), np.asarray(L1_conv_w_eta)], axis=1)))
    put("mats_e", np.concatenate([np.asarray(L1_conv_w2_0), np.asarray(L1_conv_w1_1).T, np.asarray(L1_conv_w2_1)], axis=1))
    put("w1_0", twice(L1_conv_w1_0))
    wqkv = np.asarray(L2_conv_W_qkv).reshape(3, C, C)
    for n, name in enumerate(("attn_q", "attn_k", "attn_v")):
        put(name, _block_diag(wqkv[n].T))
    hd = np.repeat(np.arange(C), 2)
    he = (np.arange(C).reshape(-1, 1, 2).repeat(2, axis=1)).reshape(-1)
    pick = (2 * C + hd, he, C + hd)
    put("scan_w", twice(np.concatenate([np.asarray(L3_conv_in_w)[:, s] for s in pick], axis=1)))
    put("scan_b", np.stack([np.asarray(L3_conv_in_b)[s] for s in pick], axis=1))
    put("out_w", _block_diag(np.asarray(L3_conv_out_w)))
    put("out_b", twice(L3_conv_out_b))
    put("ln_gamma", twice(L3_conv_gamma))
    put("ln_beta", twice(L3_conv_beta))

    arrays = {"xs": np.ascontiguousarray(xs.reshape(P, 2, BANK)), "band": band.reshape(P, -1), "const": _constants(), "param": blk}
    nc = bacc.Bacc("TRN2", target_bir_lowering=False, num_devices=1)
    args = [nc.dram_tensor(n, a.shape, F32, kind="ExternalInput").ap() for n, a in arrays.items()]
    out = nc.dram_tensor("out", (P, 2, J, P), F32, kind="ExternalOutput").ap()
    conv_attn_scan_kernel(nc, *args, out)
    r = run_bass_kernel_spmd(nc, [arrays], core_ids=[0])
    got = r.results[0]["out"].reshape(P, 2, J, BH, C).transpose(3, 2, 1, 0, 4)
    return np.ascontiguousarray(got.reshape(B, H, W, C))
```

```python
from contextlib import ExitStack

import numpy as np

import concourse.bass as bass
from concourse import mybir

F32 = mybir.dt.float32
BF16 = mybir.dt.bfloat16
ALU = mybir.AluOpType
ACT = mybir.ActivationFunctionType
AX_X = mybir.AxisListType.X

B, H, W, C = 8, 16, 16, 64
BH, J = 2, 4
HW = H * W
POS = J * HW
NT = 2 * POS
P = 128
E1 = 128
NS = H
TOK = B * W
NK = 9
PADW = H + 6
NHD = 8
BANK = 512
GEPS = 1e-5
GC = 0.044715
GS = float(np.sqrt(2.0 / np.pi))
FILL = (0, 1, 1, 1)
UP_BANKS = ((0, 1, 3, 7), (0, 1, 2, 3))
POOL_SET = {"inv512": 1, "xpad": 2, "zero": 3, "bd": 10, "kv": 12, "scan": 16}
GRAD_SCALE = 2.0 / (W * C)
MAX_LR = 0.1

CONST_COLS = {}


def _const_layout():
    at = 0
    for name, width in (("ident", P), ("twice", P), ("own_half", P), ("pair_half", P), ("sum16", P), ("ones64", P), ("dup64", P), ("head_sel", BH * NHD),
                        ("center_neg", C), ("center_neg_t", P), ("block_j", J), ("half_sel", 2 * P), ("tok_sel", J * P), ("gate_scale", 2),
                        ("eps", 1)):
        CONST_COLS[name] = (at, at + width)
        at += width
    return at


NCONST = _const_layout()

PARAM_COLS = {}


def _param_layout():
    at = 0
    for name, width in (("conv_bias", 2), ("conv_gamma", 2), ("conv_beta", 2), ("conv_alpha", 1), ("wk", P), ("wv", P),
                        ("wq", P), ("gates", 6), ("mats_e", 3 * C), ("w1_0", E1), ("attn_q", P),
                        ("attn_k", P), ("attn_v", P), ("scan_w", 3 * P), ("scan_b", 3), ("out_w", P), ("out_b", 1),
                        ("ln_gamma", 1), ("ln_beta", 1)):
        PARAM_COLS[name] = (at, at + width)
        at += width
    return at


NPARAM = _param_layout()


def conv_attn_scan_kernel(nc, xs_d, band_d, const_d, param_d, out_d):
    ctx = ExitStack()
    with ctx:
        def sb(name, shape):
            return ctx.enter_context(nc.sbuf_tensor(name, shape, F32))

        sems = {}

        def sem(name):
            if name not in sems:
                sems[name] = ctx.enter_context(nc.semaphore(name))
            return sems[name]

        ps = ctx.enter_context(nc.psum_tensor("ps", [P, 8, BANK], F32))
        psf = ps[:, :, :].rearrange("p b n -> p (b n)")

        const = sb("const_sb", [P, NCONST])
        param = sb("param_sb", [P, NPARAM])

        def cst(name, rows=P):
            a, b = CONST_COLS[name]
            return const[0:rows, a:b]

        def par(name):
            a, b = PARAM_COLS[name]
            return param[:, a:b]

        ident = cst("ident")

        def carve(arena):
            at = [0]

            def take(*dims):
                n = int(np.prod(dims))
                flat = arena[:, at[0]:at[0] + n]
                at[0] += n
                if len(dims) == 1:
                    return flat
                names = "abc"[:len(dims)]
                return flat.rearrange(f"p ({' '.join(names)}) -> p {' '.join(names)}", **dict(zip(names, dims)))
            return take

        arena_conv = sb("arena_conv", [P, 1536 + 1056 + 2048])
        arena_mem = sb("arena_mem", [P, 3 * 512 * 3 + 512 * 6])
        arena_att = sb("arena_att", [P, 2 * J * PADW * PADW + 2 * POS + NK * P + 2 * P])
        conv_cols, mem_cols, att_cols = carve(arena_conv), carve(arena_mem), carve(arena_att)

        xs = sb("xs_sb", [P, 2, BANK])
        sq = sb("sq", [P, 2, BANK])
        band = conv_cols(2 * 3 * 2 * P)
        bandv = band[:, :].rearrange("p (q d m n) -> p q d m n", q=2, d=3, m=2)
        inv512 = sb("inv512", [P, P])
        gst = sb("gst", [P, 4, 256])
        xpad = conv_cols(2, B, C + 2)
        cstat = sb("cstat", [P, 2, 6])
        cmv = sb("cmv", [P, 2, 2])
        csum = sb("csum", [P, 2, 2])
        csm = sb("csm", [P, 8, 2])
        relu_p = conv_cols(2, BANK)
        relu_n = conv_cols(2, BANK)
        alpha_n = sb("alpha_n", [P, 1])

        xc = sb("xc", [P, POS])
        xn = sb("xn", [P, POS])
        nst = sb("nst", [P, J, 6])
        nmv = sb("nmv", [P, J, 2])
        nsm = sb("nsm", [P, 8, J])

        kraw = sb("kraw", [P, POS])
        qraw = sb("qraw", [P, POS])
        nrm = sb("nrm", [P, POS])
        qt = sb("qt", [P, POS])
        kbd = sb("kbd", [P, NS * TOK])
        vbd = sb("vbd", [P, NS * TOK])
        ktok = sb("ktok", [P, NS * P])
        gates = sb("gates", [6, POS])
        gsum = sb("gsum", [6, J * NS])
        vals = sb("vals", [6, J * NS])
        eta_e = sb("eta_e", [P, NS * 8])
        keep_e = sb("keep_e", [P, NS * 8])
        eta_d = sb("eta_d", [P, NS * J])
        keep_d = sb("keep_d", [P, NS * J])
        keep_now = sb("keep_now", [P, 12])
        lrn = sb("lrn", [P, NS])
        lrh = sb("lrh", [P, NS])
        we = mem_cols(3, 8 * C)
        w10 = mem_cols(J * E1)
        wd = mem_cols(3, J * E1)
        qe = mem_cols(3, 8 * C)
        q10 = mem_cols(J * E1)
        zero = sb("zero", [P, BANK])
        zero_bf = zero[:, 0:BANK // 2].bitcast(BF16)
        act_u = sb("act_u", [P, 2, P])
        z_sq = sb("z_sq", [P, 2, P])
        z_cp = sb("z_cp", [P, 2, P])
        z_y = sb("z_y", [P, 2, P])
        z_t = sb("z_t", [P, 2, P])
        z_t2 = sb("z_t2", [P, 2, P])
        z_s1 = sb("z_s1", [P, 2, P])
        z_s2 = sb("z_s2", [P, 2, P])
        z_g = sb("z_g", [P, 2, P])
        h1bd = sb("h1bd", [P, P])
        h1mv = sb("h1mv", [P, P])
        h1_tok = sb("h1_tok", [P, P])
        spread_now = sb("spread_now", [P, J])
        k_inv = sb("k_inv", [P, 2 * J * BH])
        q_inv = sb("q_inv", [P, 2 * J * BH])
        rbd = sb("rbd", [P, P])
        dhbd = sb("dhbd", [P, P])
        dz1 = sb("dz1", [P, P])
        u_tok = sb("u_tok", [P, 2, P])
        dz_tok = sb("dz_tok", [P, 3, P])
        k_fbd = mem_cols(BANK)
        h1_fbd = mem_cols(BANK)
        r_fbd = mem_cols(BANK)
        dh_fbd = mem_cols(BANK)
        wme = sb("wme", [P, 3, C])
        wms = sb("wms", [P, 3, C])
        w11s = sb("w11s", [P, 2, C])
        w10s = sb("w10s", [P, E1])
        w10m = sb("w10m", [P, E1])
        w11m = sb("w11m", [P, E1])
        uf = sb("uf", [P, NT])
        hf = sb("hf", [P, POS])
        xh = sb("xh", [P, POS])

        aq = kraw
        kpad = att_cols(J, PADW, PADW)
        vpad = att_cols(J, PADW, PADW)
        prod2 = att_cols(2, POS)
        mx = att_cols(P)
        att = att_cols(NK, P)
        rs = att_cols(P)
        attx = (qraw, qt)
        ex = ktok[:, 0:NK * P]
        acc = hf
        prod = (prod2[:, 0], prod2[:, 1], uf[:, 0:POS], uf[:, POS:2 * POS])

        ROW = W * (H + 1)
        mem_again, att_again, conv_again = carve(arena_mem), carve(arena_att), carve(arena_conv)
        lam = mem_again(B * ROW)
        inp = mem_again(B * ROW)
        sw = mem_again(B * ROW)
        rw = att_again(B * ROW)
        lam_b = att_again(HW * (B + 1))
        inp_b = att_again(HW * (B + 1))
        fb = conv_again(HW * (B + 1))
        rb = sb("rb", [P, HW * (B + 1)])
        tot = conv_again(NT)
        xrow = mem_again(2, J, P)
        sig_i = vbd
        silu = ktok
        og = uf
        wout = sb("wout", [P, C])
        cm = sb("cm", [P, 2 * C])
        bout = sb("bout", [P, C])
        ysq = qt
        yv = sb("yv", [P, 2 * B])
        xo = xh[:, :].rearrange("p (q j n) -> p q j n", q=2, j=J)
        NWC = 4

        def seq_w(buf, lo, hi):
            return buf[:, :].rearrange("p (b w s) -> p b s w", w=W, s=H + 1)[:, lo:hi, 1:H + 1, :]

        def seq_b(buf, n):
            return buf[:, :].rearrange("p (w h s) -> p s h w", w=W, h=H)[:, 1 + 2 * n:3 + 2 * n]

        def seqs_b(buf, wc):
            n = W // NWC * H * (B + 1)
            return buf[:, wc * n:(wc + 1) * n]

        def bhw(ap, n=B):
            return ap.rearrange("p (b h w) -> p b h w", b=n, h=H)

        def halves(buf_cols, b2):
            return buf_cols.rearrange("p (j g w) -> p j g w", j=J, g=BH)[64 * b2:64 * b2 + 64, :, b2, :]

        def shifted(buf, n):
            dy, dx = 3 * (n // 3), 3 * (n % 3)
            return buf[:, :, dy:dy + H, dx:dx + W]

        block = ctx.enter_context(nc.Block())

        @block.sync
        def _(sp):
            sp.dma_start(xs[:, :, :], xs_d).then_inc(sem("x_in"), 16)
            sp.dma_start(const[:, :], const_d).then_inc(sem("const_in"), 16)
            sp.dma_start(band[:, :], band_d).then_inc(sem("band_in"), 16)
            sp.dma_start(param[:, :], param_d).then_inc(sem("param_in"), 16)
            for q in range(2):
                sp.wait_ge(sem("xo_ready"), q + 1)
                sp.dma_start(out_d[:, q, :, :], xo[:, q, :, :]).then_inc(sem("out_done"), 16)
            sp.wait_ge(sem("out_done"), 32)

        @block.gpsimd
        def _(pool):
            pool.memset(inv512[:, :], 1.0 / 512.0).then_inc(sem("pool_set"), 1)
            pool.memset(xpad[:, :, :, :], 0.0).then_inc(sem("pool_set"), 1)
            pool.memset(zero[:, :], 0.0).then_inc(sem("pool_set"), 1)
            pool.memset(kbd[:, :], 0.0).then_inc(sem("pool_set"), 1)
            pool.memset(vbd[:, :], 0.0).then_inc(sem("pool_set"), 1)
            pool.memset(h1bd[:, :], 0.0).then_inc(sem("pool_set"), 1)
            pool.memset(rbd[:, :], 0.0).then_inc(sem("pool_set"), 1)
            pool.memset(dhbd[:, :], 0.0).then_inc(sem("pool_set"), 1)
            pool.memset(r_fbd[:, :], 0.0).then_inc(sem("pool_set"), 1)
            pool.memset(u_tok[:, 1, :], 0.0).then_inc(sem("pool_set"), 1)
            pool.memset(kpad[:, :, :, :], 0.0).then_inc(sem("pool_set"), 1)
            pool.memset(vpad[:, :, :, :], 0.0).then_inc(sem("pool_set"), 1)
            pool.wait_ge(sem("q_inv"), 1)
            pool.tensor_copy(hf[:, :].rearrange("p (n c) -> p n c", c=C),
                             q_inv[:, :].unsqueeze(2).broadcast_to([P, 2 * J * BH, C])).then_inc(sem("q_spread"), 1)
            pool.wait_ge(sem("const_in"), 16)
            pool.wait_ge(sem("coef_ready"), 1)
            with pool.Fori(0, NS) as t:
                pool.wait_ge(sem("g10"), t + 1)
                pool.wait_ge(sem("ktok_ready"), 2)
                pool.tensor_copy(keep_now[:, 0:8], keep_e[:, bass.ts(t, 8)]).then_inc(sem("keep_now"), 1)
                pool.tensor_copy(keep_now[:, 8:12], keep_d[:, bass.ts(t, J)]).then_inc(sem("keep_now"), 1)
                pool.tensor_tensor(spread_now[:, :], cst("block_j"), lrh[:, bass.ds(t, 1)].broadcast_to([P, J]),
                                   ALU.mult).then_inc(sem("keep_now"), 1)
                pool.wait_ge(sem("keep_now"), 3 * t + 3)
                pool.wait_ge(sem("ktok_ready"), 2)
                pool.tensor_tensor(k_fbd[:, :].rearrange("p (j n) -> p j n", j=J),
                                   ktok[:, bass.ts(t, P)].unsqueeze(1).broadcast_to([P, J, P]),
                                   spread_now[:, :].unsqueeze(2).broadcast_to([P, J, P]), ALU.mult).then_inc(sem("k_fbd"), 1)

                def kept_part(m, new, done):
                    pool.wait_ge(sem(new), t + 1)
                    pool.tensor_tensor(qe[:, m, :].rearrange("p (b d) -> p b d", b=8),
                                       we[:, m, :].rearrange("p (b d) -> p b d", b=8),
                                       keep_now[:, 0:8].unsqueeze(2).broadcast_to([P, 8, C]),
                                       ALU.mult).then_inc(sem(done), 1)

                kept_part(1, "w11_new", "q_11")
                kept_part(0, "w20_new", "q_20")
                pool.wait_ge(sem("h1_ready"), t + 1)
                pool.wait_ge(sem("v_ready"), 2)
                pool.tensor_tensor(h1mv[:, :], h1bd[:, :], vbd[:, bass.ts(t, P)], ALU.subtract).then_inc(sem("h1mv"), 1)
                kept_part(2, "w21_new", "q_21")
                pool.wait_ge(sem("w10_new"), t + 1)
                pool.tensor_tensor(q10[:, :].rearrange("p (j e) -> p j e", j=J), w10[:, :].rearrange("p (j e) -> p j e", j=J),
                                   keep_now[:, 8:12].unsqueeze(2).broadcast_to([P, J, E1]),
                                   ALU.mult).then_inc(sem("q_10"), 1)
                pool.wait_ge(sem("h1_tok"), t + 1)
                pool.tensor_tensor(h1_fbd[:, :].rearrange("p (j n) -> p j n", j=J),
                                   h1_tok[:, :].unsqueeze(1).broadcast_to([P, J, P]),
                                   spread_now[:, :].unsqueeze(2).broadcast_to([P, J, P]), ALU.mult).then_inc(sem("h1_fbd"), 1)
            pool.wait_ge(sem("aq_ready"), 1)
            pool.wait_ge(sem("ak_ready"), 1)
            for n in range(1, NK, 2):
                if n >= 4:
                    pool.wait_ge(sem("qk_tp"), n - 3)
                pool.tensor_tensor(bhw(prod[n % 4], J), bhw(aq[:, :], J), shifted(kpad, n), ALU.mult).then_inc(sem("qk_pool"), 1)
            def separators(buf, length):
                pool.memset(buf[:, :].rearrange("p (n s) -> p n s", s=length + 1)[:, :, 0], 0.0).then_inc(sem("pool_set"), 1)

            pool.wait_ge(sem("hf_done"), 2)
            separators(lam, H)
            separators(inp, H)
            for n in range(1, NK, 2):
                pool.wait_ge(sem("pv_ready"), n + 1)
                if n > 1:
                    pool.wait_ge(sem("odd_sum"), n // 2)
                pool.tensor_tensor(prod[0], prod[0], prod[1 + n // 2 % 2], ALU.add).then_inc(sem("odd_sum"), 1)
            pool.wait_ge(sem("x3_ready"), 1)
            separators(lam_b, B)
            separators(inp_b, B)
            for n in range(4):
                cols = slice(2 * n * ROW, 2 * (n + 1) * ROW)
                pool.wait_ge(sem("scan_w"), n + 1)
                pool.tensor_tensor(sw[:, cols], sw[:, cols], rw[:, cols], ALU.add).then_inc(sem("sw_ready"), 1)
            for wc in range(NWC):
                pool.wait_ge(sem("scan_b"), wc + 1)
                pool.tensor_tensor(seqs_b(fb, wc), seqs_b(fb, wc), seqs_b(rb, wc), ALU.add).then_inc(sem("sb_ready"), 1)
            pool.wait_ge(sem("scaled_out"), 1)
            pool.tensor_tensor(xo[:, 0], xo[:, 0], xrow[:, 0], ALU.add).then_inc(sem("xo_ready"), 1)

        @block.scalar
        def _(act):
            act.wait_ge(sem("x_in"), 16)
            act.activation(sq[:, :, :], xs[:, :, :], ACT.Square).then_inc(sem("sq0"), 1)
            act.wait_ge(sem("const_in"), 16)
            act.wait_ge(sem("gvar0"), 1)
            act.activation(gst[:, 3, :], gst[:, 2, :], ACT.Sqrt, bias=cst("eps")).then_inc(sem("gstd0"), 1)
            act.wait_ge(sem("cvar"), 1)
            act.activation(csm[:, 2, :], csm[:, 1, :], ACT.Sqrt, bias=cst("eps")).then_inc(sem("cstd"), 1)
            act.wait_ge(sem("caff"), 1)
            for m in range(2):
                act.activation(relu_p[:, m, :], ps[:, m, :], ACT.Relu, bias=csm[:, 5, m:m + 1], scale=csm[:, 4, m:m + 1])
                act.activation(relu_n[:, m, :], ps[:, m, :], ACT.Relu, bias=csm[:, 7, m:m + 1],
                               scale=csm[:, 6, m:m + 1]).then_inc(sem("relu"), 1)
            act.wait_ge(sem("x1_tp"), 1)
            act.activation(xc[:, :], psf[:, 2 * BANK:4 * BANK], ACT.Copy).then_inc(sem("x1_ready"), 1)
            act.wait_ge(sem("nvar"), 1)
            act.activation(nsm[:, 2, :], nsm[:, 1, :], ACT.Sqrt, bias=cst("eps")).then_inc(sem("nstd"), 1)
            act.preload_act_table_set("gelu_apprx_tanh_and_others")
            act.wait_ge(sem("gate_done"), 1)
            act.activation(gates[:, :], psf[0:6, 0:POS], ACT.Tanh, scale=0.5).then_inc(sem("gate_sig"), 1)
            act.wait_ge(sem("kq_done"), 1)
            act.activation(sq[:, :, :], ps[:, 2:4, :], ACT.Square).then_inc(sem("kq_sq"), 1)
            act.preload_act_table_set("sqrt_and_others")
            act.activation(kraw[:, :], psf[:, 2 * BANK:4 * BANK], ACT.Copy).then_inc(sem("kraw"), 1)
            act.wait_ge(sem("kq_sum"), 1)
            act.activation(k_inv[:, :], ps[:, 6, 0:2 * J * BH], ACT.Sqrt).then_inc(sem("kq_norm"), 1)
            act.wait_ge(sem("kq_done"), 2)
            act.activation(sq[:, :, :], ps[:, 4:6, :], ACT.Square).then_inc(sem("kq_sq"), 1)
            act.activation(qraw[:, :], psf[:, 4 * BANK:6 * BANK], ACT.Copy).then_inc(sem("qraw"), 1)
            act.wait_ge(sem("kq_sum"), 2)
            act.activation(q_inv[:, :], ps[:, 6, 2 * J * BH:4 * J * BH], ACT.Sqrt).then_inc(sem("kq_norm"), 1)
            act.preload_act_table_set("gelu_apprx_tanh_and_others")
            act.wait_ge(sem("pool_set"), POOL_SET["bd"] - 2)
            act.wait_ge(sem("v_done"), 1)
            for b2 in range(BH):
                act.activation(vbd[:, :].rearrange("p (t j g w) -> p g t j w", t=NS, j=J, g=BH)[64 * b2:64 * b2 + 64, b2],
                               psf[64 * b2:64 * b2 + 64, 4 * BANK:6 * BANK].rearrange("p (j t w) -> p t j w", j=J, t=NS),
                               ACT.Copy).then_inc(sem("v_ready"), 1)
            for half, bank in ((0, 6), (1, 4)):
                act.wait_ge(sem("ktok_tp"), half + 1)
                act.activation(ktok[:, half * POS:(half + 1) * POS], psf[:, bank * BANK:(bank + 2) * BANK], ACT.Copy)\
                   .then_inc(sem("ktok_ready"), 1)
            with act.Fori(0, NS) as t:
                def hidden(i, done, ready, kept):
                    act.wait_ge(sem(done), t + 1)
                    act.activation(act_u[:, i, :], ps[:, 4, P * i:P * i + P], ACT.Gelu_apprx_tanh).then_inc(sem(ready), 1)
                    act.activation(z_sq[:, i, :], ps[:, 4, P * i:P * i + P], ACT.Square)
                    act.activation(z_cp[:, i, :], ps[:, 4, P * i:P * i + P], ACT.Copy).then_inc(sem(kept), 1)

                def tanh(i, y, th):
                    act.wait_ge(sem(y), t + 1)
                    act.activation(z_t[:, i, :], z_y[:, i, :], ACT.Tanh, scale=GS * GC).then_inc(sem(th), 1)

                def tanh_sq(i, th, t2):
                    act.wait_ge(sem(th), t + 1)
                    act.activation(z_t2[:, i, :], z_t[:, i, :], ACT.Square).then_inc(sem(t2), 1)

                def turned(m, bank, tp, cp):
                    act.wait_ge(sem(tp), t + 1)
                    act.activation(wd[:, m, :], ps[:, bank, :], ACT.Copy).then_inc(sem(cp), 1)

                def token_rows(out, bank, col, tp, done):
                    act.wait_ge(sem(tp), t + 1)
                    act.activation(out, ps[:, bank, col:col + P], ACT.Copy).then_inc(sem(done), 1)

                hidden(0, "z0_done", "u0_ready", "z0_kept")
                turned(1, 7, "w11_tp", "w11_d")
                token_rows(u_tok[:, 0, :], 7, P, "u0_tp", "u0_tok")
                tanh(0, "y0", "tanh0")
                tanh_sq(0, "tanh0", "t2_0")
                hidden(1, "z1_done", "u1_ready", "z1_kept")
                turned(2, 6, "w21_tp", "w21_d")
                token_rows(h1_tok[:, :], 7, 0, "h1_tp", "h1_tok")
                tanh(1, "y1", "tanh1")
                tanh_sq(1, "tanh1", "t2_1")
                token_rows(u_tok[:, 1, :], 7, P, "u1_tp", "u1_tok")
                turned(0, 6, "w20_tp", "w20_d")
                act.wait_ge(sem("dz1_tp"), t + 1)
                act.activation(dz_tok[:, 1:3, :], ps[:, 6, 2 * P:4 * P].rearrange("p (s n) -> p s n", s=2), ACT.Copy)\
                   .then_inc(sem("dz1_tok"), 1)

            act.wait_ge(sem("wm_tp"), 1)
            act.activation(w10m[:, :], ps[:, 4, 0:E1], ACT.Copy, scale=1.0 / B).then_inc(sem("wm_ready"), 1)
            for i in range(2):
                for n in range(4):
                    act.wait_ge(sem("zf_done"), 4 * i + n + 1)
                    act.activation(uf[:, n * BANK:(n + 1) * BANK], ps[:, UP_BANKS[i][n], :], ACT.Gelu_apprx_tanh).then_inc(sem("uf_ready"), 1)
                if i == 0:
                    act.wait_ge(sem("wm_tp"), 2)
                    act.activation(w11m[:, :], ps[:, 6, 0:E1], ACT.Copy).then_inc(sem("wm_ready"), 1)

            act.wait_ge(sem("nvar"), 2)
            act.activation(nsm[:, 2, :], nsm[:, 1, :], ACT.Sqrt, bias=cst("eps")).then_inc(sem("nstd"), 1)
            act.wait_ge(sem("aqkv_done"), 1)
            act.activation(aq[:, :], psf[:, 0:2 * BANK], ACT.Copy).then_inc(sem("aq_ready"), 1)
            act.wait_ge(sem("pool_set"), POOL_SET["kv"])
            act.wait_ge(sem("aqkv_done"), 3)
            act.activation(vpad[:, :, 3:3 + H, 3:3 + W], bhw(psf[:, 4 * BANK:6 * BANK], J), ACT.Copy).then_inc(sem("av_ready"), 1)
            act.wait_ge(sem("sub_ready"), 1)
            def spread_heads(n, src, func, scale):
                if n >= 2:
                    act.wait_ge(sem("att_tp"), n - 1)
                act.activation(attx[n % 2][:, :].rearrange("p (h d) -> p h d", d=C // NHD),
                               src.unsqueeze(2).broadcast_to([P, P, C // NHD]), func, scale=scale).then_inc(sem("attx_ready"), 1)

            dph_scale = float((C // NHD) ** -0.5)
            for n in range(NK):
                spread_heads(n, att[:, n, :], ACT.Exp, dph_scale)
                if n == 1:
                    act.activation(ex, att[:, :, :].rearrange("p k n -> p (k n)"), ACT.Exp, scale=dph_scale).then_inc(sem("exp_done"), 1)
            act.wait_ge(sem("att_ready"), 1)
            spread_heads(NK, rs[:, :], ACT.Copy, 1.0)

            act.wait_ge(sem("nvar"), 3)
            act.activation(nsm[:, 2, :], nsm[:, 1, :], ACT.Sqrt, bias=cst("eps")).then_inc(sem("nstd"), 1)
            act.preload_act_table_set("sigmoid_and_others")
            act.wait_ge(sem("pool_set"), POOL_SET["scan"])
            for n in range(4):
                act.wait_ge(sem("feat_done"), 2 * n + 1)
                act.activation(seq_w(lam, 2 * n, 2 * n + 2), bhw(ps[:, n, :], 2), ACT.Sigmoid, bias=par("scan_b")[:, 0:1])\
                   .then_inc(sem("lam_ready"), 1)
                act.activation(seq_b(lam_b, n), bhw(ps[:, n, :], 2), ACT.Sigmoid, bias=par("scan_b")[:, 0:1])\
                   .then_inc(sem("lam_b"), 1)
                act.wait_ge(sem("feat_done"), 2 * n + 2)
                act.activation(sig_i[:, n * BANK:(n + 1) * BANK], ps[:, 4 + n, :], ACT.Sigmoid, bias=par("scan_b")[:, 1:2])\
                   .then_inc(sem("sig_ready"), 1)
            for n in range(4):
                act.wait_ge(sem("feat_done"), 8 + n + 1)
                act.activation(og[:, n * BANK:(n + 1) * BANK], ps[:, n, :], ACT.Sigmoid, bias=par("scan_b")[:, 2:3])\
                   .then_inc(sem("og_ready"), 1)
                act.wait_ge(sem("inp_ready"), n + 1)
                act.activation(seq_b(inp_b, n), seq_w(inp, 2 * n, 2 * n + 2), ACT.Copy).then_inc(sem("inp_b"), 1)
            act.preload_act_table_set("sqrt_and_others")
            for n in range(4):
                act.wait_ge(sem("out_mm"), n + 1)
                act.activation(ysq[:, n * 4 * C:(n + 1) * 4 * C].rearrange("p (i c) -> p i c", c=C),
                               ps[:, n, :].rearrange("p (i c) -> p i c", c=2 * C)[:, :, 0:C], ACT.Square).then_inc(sem("ysq"), 1)
            act.wait_ge(sem("yvar"), 4)
            act.activation(yv[:, :], yv[:, :], ACT.Sqrt, scale=1.0 / C, bias=cst("eps")).then_inc(sem("ystd"), 1)

        @block.vector
        def _(dve):
            linked = [0]

            def link(ins):
                linked[0] += 1
                ins.then_inc(sem("dve_link"), 1)
                dve.wait_ge(sem("dve_link"), linked[0])

            dve.wait_ge(sem("gsum0"), 1)
            dve.tensor_reduce(gst[:, 0, :], ps[:, 0, :].rearrange("p (g k) -> p g k", k=2), AX_X, ALU.add)
            link(dve.tensor_reduce(gst[:, 1, :], ps[:, 1, :].rearrange("p (g k) -> p g k", k=2), AX_X, ALU.add))
            link(dve.tensor_tensor(gst[:, 2, :], gst[:, 0, :], gst[:, 0, :], ALU.mult))
            dve.tensor_tensor(gst[:, 2, :], gst[:, 1, :], gst[:, 2, :], ALU.subtract).then_inc(sem("gvar0"), 1)
            dve.wait_ge(sem("gstd0"), 1)
            link(dve.reciprocal(gst[:, 3, :], gst[:, 3, :]))

            def group_cols(row):
                return gst[:, row, :].rearrange("p (b g) -> p b g", b=B).unsqueeze(3).broadcast_to([P, B, C // 2, 2])

            dve.wait_ge(sem("pool_set"), POOL_SET["xpad"])
            for q in range(2):
                inner = xpad[:, q, :, 1:C + 1].rearrange("p b (g k) -> p b g k", k=2)
                link(dve.tensor_tensor(inner, xs[:, q, :].rearrange("p (b g k) -> p b g k", b=B, k=2), group_cols(0), ALU.subtract))
                dve.tensor_tensor(inner, inner, group_cols(3), ALU.mult).then_inc(sem("xpad_ready"), 1)

            dve.wait_ge(sem("param_in"), 16)
            for m in range(2):
                dve.wait_ge(sem("conv_done"), m + 1)
                link(dve.bn_stats(cstat[:, m, :], ps[:, m, :]))
                link(dve.bn_aggr(cmv[:, m, :], cstat[:, m, :]))
            mean, var = cmv[:, :, 0], cmv[:, :, 1]
            link(dve.tensor_tensor(csum[:, 0, :], mean, par("conv_bias"), ALU.add))
            link(dve.tensor_tensor(csum[:, 1, :], csum[:, 0, :], csum[:, 0, :], ALU.mult))
            dve.tensor_tensor(csum[:, 1, :], csum[:, 1, :], var, ALU.add).then_inc(sem("csum"), 1)
            dve.wait_ge(sem("cgroup"), 1)
            link(dve.tensor_copy(csm[:, 0:2, :], ps[:, 2, 0:4].rearrange("p (s m) -> p s m", s=2)))
            link(dve.tensor_tensor(csm[:, 3, :], csm[:, 0, :], csm[:, 0, :], ALU.mult))
            dve.tensor_tensor(csm[:, 1, :], csm[:, 1, :], csm[:, 3, :], ALU.subtract).then_inc(sem("cvar"), 1)
            dve.wait_ge(sem("cstd"), 1)
            link(dve.reciprocal(csm[:, 2, :], csm[:, 2, :]))
            link(dve.tensor_tensor(csm[:, 4, :], csm[:, 2, :], par("conv_gamma"), ALU.mult))
            link(dve.tensor_tensor(csm[:, 3, :], par("conv_bias"), csm[:, 0, :], ALU.subtract))
            link(dve.tensor_tensor(csm[:, 3, :], csm[:, 3, :], csm[:, 4, :], ALU.mult))
            link(dve.tensor_tensor(csm[:, 5, :], csm[:, 3, :], par("conv_beta"), ALU.add))
            dve.tensor_scalar(alpha_n[:, :], par("conv_alpha"), -1.0, None, ALU.mult)
            dve.tensor_scalar(csm[:, 6:8, :], csm[:, 4:6, :], -1.0, None, ALU.mult).then_inc(sem("caff"), 1)
            for m in range(2):
                dve.wait_ge(sem("relu"), m + 1)
                link(dve.tensor_tensor(xs[:, m, :], xs[:, m, :], relu_p[:, m, :], ALU.add))
                dve.scalar_tensor_tensor(xs[:, m, :], relu_n[:, m, :], alpha_n[:, 0:1], xs[:, m, :], ALU.mult, ALU.add)\
                   .then_inc(sem("x1_rows"), 1)

            def group_norm(n):
                for j in range(J):
                    dve.bn_stats(nst[:, j, :], xc[:, j * HW:(j + 1) * HW]).then_inc(sem("bn_part"), 1)
                dve.wait_ge(sem("bn_part"), J * (n + 1))
                for j in range(J):
                    last = dve.bn_aggr(nmv[:, j, :], nst[:, j, :])
                link(last)
                link(dve.tensor_tensor(nsm[:, 4, :], nmv[:, :, 0], nmv[:, :, 0], ALU.mult))
                dve.tensor_copy(nsm[:, 6, :], nmv[:, :, 0])
                dve.tensor_tensor(nsm[:, 7, :], nsm[:, 4, :], nmv[:, :, 1], ALU.add).then_inc(sem("npart"), 1)
                dve.wait_ge(sem("ngroup"), n + 1)
                link(dve.tensor_copy(nsm[:, 0:2, :], ps[:, 7, 0:2 * J].rearrange("p (s j) -> p s j", s=2)))
                link(dve.tensor_tensor(nsm[:, 3, :], nsm[:, 0, :], nsm[:, 0, :], ALU.mult))
                dve.tensor_tensor(nsm[:, 1, :], nsm[:, 1, :], nsm[:, 3, :], ALU.subtract).then_inc(sem("nvar"), 1)
                dve.wait_ge(sem("nstd"), n + 1)
                link(dve.reciprocal(nsm[:, 5, :], nsm[:, 2, :]))
                for j in range(J):
                    dve.tensor_scalar(xn[:, j * HW:(j + 1) * HW], xc[:, j * HW:(j + 1) * HW], nsm[:, 0, j:j + 1],
                                      nsm[:, 5, j:j + 1], ALU.subtract, ALU.mult).then_inc(sem("xn_ready"), 1)

            dve.wait_ge(sem("x1_ready"), 1)
            group_norm(0)
            for m, new, buf in ((0, "w20_new", we), (1, "w11_new", we), (2, "q_21", qe)):
                dve.tensor_copy(buf[:, m, :].rearrange("p (b d) -> p b d", b=8),
                                par("mats_e")[:, m * C:(m + 1) * C].unsqueeze(1).broadcast_to([P, 8, C])).then_inc(sem(new), 1)
            dve.tensor_copy(w10[:, :].rearrange("p (j e) -> p j e", j=J), par("w1_0").unsqueeze(1).broadcast_to([P, J, E1]))\
               .then_inc(sem("w10_new"), 1)
            dve.wait_ge(sem("gate_sig"), 1)
            link(dve.tensor_reduce(gsum[:, :], gates[:, :].rearrange("p (n w) -> p n w", w=W), AX_X, ALU.add))
            dve.tensor_scalar(vals[:, :], gsum[:, :], cst("gate_scale", 6)[:, 0:1], cst("gate_scale", 6)[:, 1:2], ALU.mult, ALU.add)\
               .then_inc(sem("vals"), 1)
            dve.wait_ge(sem("kq_norm"), 1)
            link(dve.tensor_scalar(k_inv[:, :], k_inv[:, :], 1e-12, None, ALU.max))
            link(dve.reciprocal(k_inv[:, :], k_inv[:, :]))
            dve.tensor_copy(nrm[:, :].rearrange("p (n c) -> p n c", c=C),
                            k_inv[:, :].unsqueeze(2).broadcast_to([P, 2 * J * BH, C])).then_inc(sem("k_spread"), 1)
            dve.wait_ge(sem("coef_ps"), 1)
            for i, buf in ((0, eta_e), (1, keep_e)):
                dve.tensor_copy(buf[:, :].rearrange("p (t j g) -> p g j t", t=NS, j=J),
                                ps[:, 7, 128 * i:128 * i + 128].rearrange("p (g j t) -> p g j t", g=BH, j=J))
            for i, buf in ((0, eta_d), (1, keep_d)):
                dve.tensor_copy(buf[:, :].rearrange("p (t j) -> p j t", t=NS),
                                ps[:, 7, 256 + 64 * i:320 + 64 * i].rearrange("p (j t) -> p j t", j=J))
            dve.tensor_copy(lrn[:, :], ps[:, 7, 384:384 + NS])
            dve.tensor_scalar(lrh[:, :], ps[:, 7, 384:384 + NS], 0.5, None, ALU.mult).then_inc(sem("coef_ready"), 1)
            dve.wait_ge(sem("pool_set"), POOL_SET["bd"] - 2)
            dve.wait_ge(sem("kraw"), 1)
            dve.wait_ge(sem("inv_tp"), 1)
            for b2 in range(BH):
                s = slice(64 * b2, 64 * b2 + 64)
                last = dve.tensor_tensor(kbd[:, :].rearrange("p (t j g w) -> p g t j w", t=NS, j=J, g=BH)[s, b2],
                                         kraw[s, :].rearrange("p (j t w) -> p t j w", j=J, t=NS),
                                         psf[s, 0:2 * BANK].rearrange("p (j t w) -> p t j w", j=J, t=NS), ALU.mult)
            last.then_inc(sem("kbd_ready"), 1)
            dve.wait_ge(sem("kq_norm"), 2)
            link(dve.tensor_scalar(q_inv[:, :], q_inv[:, :], 1e-12, None, ALU.max))
            dve.reciprocal(q_inv[:, :], q_inv[:, :]).then_inc(sem("q_inv"), 1)
            dve.wait_ge(sem("qraw"), 1)
            dve.wait_ge(sem("inv_tp"), 2)
            dve.tensor_tensor(qt[:, :], qraw[:, :], psf[:, 2 * BANK:4 * BANK], ALU.mult).then_inc(sem("qt_ready"), 1)
            dve.wait_ge(sem("m_zero"), 3)
            dve.wait_ge(sem("g10"), 1)
            dve.wait_ge(sem("coef_ready"), 1)

            with dve.Fori(0, NS) as t:
                def mom_scale(m):
                    if m < 3:
                        v = ps[:, m, :].rearrange("p (b d) -> p b d", b=8)
                        dve.tensor_tensor(v, v, eta_e[:, bass.ts(t, 8)].unsqueeze(2).broadcast_to([P, 8, C]), ALU.mult)\
                           .then_inc(sem("scaled"), 1)
                    else:
                        v = ps[:, 3, :].rearrange("p (j e) -> p j e", j=J)
                        dve.tensor_tensor(v, v, eta_d[:, bass.ts(t, J)].unsqueeze(2).broadcast_to([P, J, E1]), ALU.mult)\
                           .then_inc(sem("scaled"), 1)

                def arg(i, kept, y):
                    dve.wait_ge(sem(kept), t + 1)
                    dve.scalar_tensor_tensor(z_y[:, i, :], z_sq[:, i, :], 1.0 / GC, z_cp[:, i, :], ALU.add, ALU.mult)\
                       .then_inc(sem(y), 1)

                def slope_1(i, t2):
                    dve.wait_ge(sem(t2), t + 1)
                    dve.scalar_tensor_tensor(z_s1[:, i, :], z_t2[:, i, :], -1.0, z_cp[:, i, :], ALU.add, ALU.mult).then_inc(sem("slope"), 1)

                def slope_2(i):
                    dve.wait_ge(sem("slope"), 6 * t + 3 * i + 1)
                    dve.scalar_tensor_tensor(z_s2[:, i, :], z_sq[:, i, :], 1.0 / (3.0 * GC), z_s1[:, i, :], ALU.add, ALU.mult)\
                       .then_inc(sem("slope"), 1)

                def slope_3(i):
                    dve.wait_ge(sem("slope"), 6 * t + 3 * i + 2)
                    dve.scalar_tensor_tensor(z_g[:, i, :], z_s2[:, i, :], -3.0 * GC * GS, z_t[:, i, :], ALU.mult, ALU.add)\
                       .then_inc(sem("slope"), 1)

                def by_pair(out, col, tp, done, scale):
                    dve.wait_ge(sem(tp), t + 1)
                    dve.scalar_tensor_tensor(out[:, :].rearrange("p (j n) -> p j n", j=J),
                                             ps[:, 7, col:col + P].unsqueeze(1).broadcast_to([P, J, P]), scale,
                                             cst("block_j").unsqueeze(2).broadcast_to([P, J, P]), ALU.mult, ALU.mult)\
                       .then_inc(sem(done), 1)

                def updated(m, grad, q, done):
                    dve.wait_ge(sem(grad), t + (1 if m < 3 else 2))
                    dve.wait_ge(sem(q), t + 1)
                    if m < 3:
                        dve.tensor_tensor(we[:, m, :], ps[:, m, :], qe[:, m, :], ALU.add).then_inc(sem(done), 1)
                    else:
                        dve.tensor_tensor(w10[:, :], ps[:, 3, :], q10[:, :], ALU.add).then_inc(sem(done), 1)

                mom_scale(1)
                dve.wait_ge(sem("h1_ps"), t + 1)
                dve.tensor_tensor(h1bd[:, :], ps[:, 5, 0:P], cst("own_half"), ALU.mult).then_inc(sem("h1_ready"), 1)
                arg(0, "z0_kept", "y0")
                updated(2, "g21", "q_21", "w21_new")
                mom_scale(2)
                slope_1(0, "t2_0")
                arg(1, "z1_kept", "y1")
                slope_2(0)
                slope_3(0)
                dve.wait_ge(sem("h2_ps"), t + 1)
                dve.tensor_tensor(rbd[:, :], ps[:, 5, P:2 * P], cst("own_half"), ALU.mult).then_inc(sem("r_ready"), 1)
                slope_1(1, "t2_1")
                slope_2(1)
                slope_3(1)
                dve.wait_ge(sem("slope"), 6 * t + 6)
                dve.wait_ge(sem("du1_done"), t + 1)
                dve.scalar_tensor_tensor(dz1[:, :], z_g[:, 1, :], 1.0, ps[:, 4, 2 * P:3 * P], ALU.add, ALU.mult).then_inc(sem("dz1_ready"), 1)
                by_pair(r_fbd, 2 * P, "r_tp", "r_fbd", lrn[:, bass.ds(t, 1)])
                dve.wait_ge(sem("dh1_ps"), t + 1)
                dve.scalar_tensor_tensor(dhbd[:, :], ps[:, 5, 2 * P:3 * P], 0.5, cst("own_half"), ALU.mult, ALU.mult)\
                   .then_inc(sem("dh1_ready"), 1)
                mom_scale(3)
                mom_scale(0)
                dve.wait_ge(sem("dz1_tok"), t + 1)
                dve.wait_ge(sem("du0_done"), t + 1)
                dve.scalar_tensor_tensor(dz_tok[:, 0, :], dz_tok[:, 2, :], 1.0, ps[:, 4, 3 * P:4 * P], ALU.add, ALU.mult)\
                   .then_inc(sem("dz0_ready"), 1)
                by_pair(dh_fbd, 3 * P, "dh1_tp", "dh_fbd", lrn[:, bass.ds(t, 1)])
                updated(3, "g10", "q_10", "w10_new")
                updated(1, "g11", "q_11", "w11_new")
                updated(0, "g20", "q_20", "w20_new")

            dve.wait_ge(sem("w11_new"), NS + 1)
            dve.wait_ge(sem("w20_new"), NS + 1)
            link(dve.tensor_reduce(wms[:, 0:2, :], we[:, 0:2, :].rearrange("p m (b d) -> p m d b", b=8), AX_X, ALU.add))
            dve.tensor_scalar(w11s[:, :, :], wms[:, 1, :].unsqueeze(1).broadcast_to([P, 2, C]), 1.0 / B, None, ALU.mult)
            dve.tensor_scalar(wme[:, 0, :], wms[:, 0, :], 1.0 / B, None, ALU.mult).then_inc(sem("wm_sum"), 1)
            dve.wait_ge(sem("g21"), NS + 1)
            dve.wait_ge(sem("q_21"), NS + 1)
            link(dve.tensor_tensor(we[:, 2, :], ps[:, 2, :], qe[:, 2, :], ALU.add))
            link(dve.tensor_reduce(wms[:, 2, :], we[:, 2, :].rearrange("p (b d) -> p d b", b=8), AX_X, ALU.add))
            dve.tensor_scalar(wme[:, 2, :], wms[:, 2, :], 1.0 / B, None, ALU.mult).then_inc(sem("wm_sum"), 1)
            dve.wait_ge(sem("hf_done"), 1)
            dve.tensor_tensor(hf[:, :], psf[:, 4 * BANK:6 * BANK], qt[:, :], ALU.add).then_inc(sem("hf_ready"), 1)
            dve.wait_ge(sem("hf_ready"), 1)
            link(dve.tensor_tensor(xh[:, :], xc[:, :], hf[:, :], ALU.add))
            dve.wait_ge(sem("hf_done"), 2)
            link(dve.tensor_tensor(xc[:, :], psf[:, 6 * BANK:8 * BANK], xh[:, :], ALU.add))
            group_norm(1)

            dve.tensor_scalar(wout[0:C, :], par("out_w")[0:C, 0:C], par("ln_gamma")[0:C], None, ALU.mult).then_inc(sem("wout"), 1)
            dve.wait_ge(sem("pool_set"), POOL_SET["kv"] - 1)
            dve.wait_ge(sem("aqkv_done"), 2)
            dve.tensor_copy(kpad[:, :, 3:3 + H, 3:3 + W], bhw(psf[:, 2 * BANK:4 * BANK], J)).then_inc(sem("ak_ready"), 1)
            dve.wait_ge(sem("ak_ready"), 1)
            dve.wait_ge(sem("aq_ready"), 1)

            def gate_chunk(wc):
                n = W // NWC
                dve.wait_ge(sem("og_ready"), 4)
                dve.wait_ge(sem("sum_done"), wc + 1)
                dve.tensor_tensor(bhw(tot)[:, :, :, wc * n:(wc + 1) * n],
                                  ps[:, 4 + wc, :].rearrange("p (b w h) -> p b h w", b=B, w=n),
                                  bhw(og[:, :])[:, :, :, wc * n:(wc + 1) * n], ALU.mult).then_inc(sem("tot_ready"), 1)

            def head_sums(n):
                dve.wait_ge(sem("qk_tp"), n + 1)
                dve.tensor_reduce(att[:, n, :], psf[:, (n % 2) * 2 * BANK:(n % 2 + 1) * 2 * BANK].rearrange("p (n d) -> p n d", d=C // NHD),
                                  AX_X, ALU.add).then_inc(sem("score_done"), 1)

            for n in range(NK):
                if n % 2 == 0:
                    if n >= 4:
                        dve.wait_ge(sem("qk_tp"), n - 3)
                    dve.tensor_tensor(bhw(prod[n % 4], J), bhw(aq[:, :], J), shifted(kpad, n), ALU.mult).then_inc(sem("qk_dve"), 1)
                if n >= 2:
                    head_sums(n - 2)
            head_sums(NK - 2)
            head_sums(NK - 1)
            dve.wait_ge(sem("score_done"), NK)
            link(dve.tensor_reduce(mx[:, :], att[:, :, :].rearrange("p k n -> p n k"), AX_X, ALU.max))
            dve.tensor_tensor(att[:, :, :], att[:, :, :],
                              mx[:, :].unsqueeze(1).broadcast_to([P, NK, P]), ALU.subtract).then_inc(sem("sub_ready"), 1)
            dve.wait_ge(sem("exp_done"), 1)
            link(dve.tensor_reduce(rs[:, :], ex.rearrange("p (k n) -> p n k", k=NK), AX_X, ALU.add))
            dve.reciprocal(rs[:, :], rs[:, :]).then_inc(sem("att_ready"), 1)
            dve.wait_ge(sem("av_ready"), 1)

            def att_cols_of(n):
                return psf[:, n % 3 * 2 * BANK:(n % 3 + 1) * 2 * BANK]

            def times_v(n):
                dve.wait_ge(sem("att_tp"), n + 1)
                if n >= 5 and n % 2:
                    dve.wait_ge(sem("odd_sum"), n // 2 - 1)
                if n >= 6 and n % 2 == 0:
                    dve.wait_ge(sem("even_sum"), n // 2 - 2)
                out = prod[1 + n // 2 % 2] if n % 2 else acc if n == 2 else prod[3] if n else prod[0]
                dve.tensor_tensor(bhw(out, J), bhw(att_cols_of(n), J), shifted(vpad, n), ALU.mult).then_inc(sem("pv_ready"), 1)

            def add_even(n):
                dve.wait_ge(sem("pv_ready"), n + 1)
                if n > 4:
                    dve.wait_ge(sem("even_sum"), n // 2 - 2)
                dve.tensor_tensor(acc[:, :], acc[:, :], prod[3], ALU.add).then_inc(sem("even_sum"), 1)

            for n in range(NK):
                times_v(n)
                if n in (5, 7):
                    add_even(n - 1)
            add_even(NK - 1)
            dve.wait_ge(sem("even_sum"), 3)
            dve.wait_ge(sem("odd_sum"), NK // 2)
            link(dve.tensor_tensor(acc[:, :], acc[:, :], prod[0], ALU.add))
            dve.wait_ge(sem("att_tp"), NK + 1)
            link(dve.tensor_tensor(acc[:, :], acc[:, :], att_cols_of(NK), ALU.mult))
            dve.tensor_tensor(xc[:, :], acc[:, :], xc[:, :], ALU.add).then_inc(sem("x3_ready"), 1)
            dve.wait_ge(sem("x3_ready"), 1)
            group_norm(2)

            dve.wait_ge(sem("xrow_tp"), 1)
            dve.tensor_copy(cm[:, 0:C], cst("center_neg"))
            dve.tensor_copy(cm[:, C:2 * C], ps[:, 6, 0:C])
            link(dve.tensor_copy(bout[:, :], ps[:, 6, C:2 * C]))
            dve.tensor_tensor(xrow[:, :, :, :].rearrange("p q j (g c) -> p (q j g) c", c=C),
                              psf[:, 4 * BANK:6 * BANK].rearrange("p (n c) -> p n c", c=C),
                              bout[:, :].unsqueeze(1).broadcast_to([P, 16, C]), ALU.add).then_inc(sem("xrow_ready"), 1)
            for n in range(4):
                cols = slice(n * BANK, (n + 1) * BANK)
                rows = slice(2 * n * ROW, 2 * (n + 1) * ROW)
                dve.wait_ge(sem("lam_ready"), n + 1)
                dve.wait_ge(sem("sig_ready"), n + 1)
                dve.scalar_tensor_tensor(silu[:, cols], ps[:, 4 + n, :], par("scan_b")[:, 1:2], sig_i[:, cols], ALU.add, ALU.mult)\
                   .then_inc(sem("silu"), 1)
                dve.wait_ge(sem("silu"), n + 1)
                for b in (2 * n, 2 * n + 1):
                    last = dve.scalar_tensor_tensor(seq_w(inp, b, b + 1)[:, 0], seq_w(lam, b, b + 1)[:, 0], -1.0,
                                                    bhw(silu)[:, b], ALU.add, ALU.mult)
                last.then_inc(sem("inp_ready"), 1)
                dve.wait_ge(sem("inp_ready"), n + 1)
                dve.tensor_tensor_scan(sw[:, rows], lam[:, rows], inp[:, rows], 0.0, ALU.mult, ALU.add)
                dve.tensor_tensor_scan(rw[:, rows][:, ::-1], lam[:, rows][:, ::-1], inp[:, rows][:, ::-1], 0.0, ALU.mult, ALU.add)\
                   .then_inc(sem("scan_w"), 1)
            dve.wait_ge(sem("lam_b"), 4)
            dve.wait_ge(sem("inp_b"), 4)
            for wc in range(NWC):
                f, r, la, x = (seqs_b(buf, wc) for buf in (fb, rb, lam_b, inp_b))
                dve.tensor_tensor_scan(f, la, x, 0.0, ALU.mult, ALU.add)
                dve.tensor_tensor_scan(r[:, ::-1], la[:, ::-1], x[:, ::-1], 0.0, ALU.mult, ALU.add).then_inc(sem("scan_b"), 1)
            for wc in range(NWC):
                gate_chunk(wc)
            for n in range(4):
                dve.wait_ge(sem("ysq"), n + 1)
                dve.tensor_reduce(yv[:, 4 * n:4 * n + 4], ysq[:, n * 4 * C:(n + 1) * 4 * C].rearrange("p (i c) -> p i c", c=C), AX_X,
                                  ALU.add).then_inc(sem("yvar"), 1)
            dve.wait_ge(sem("ystd"), 1)
            link(dve.reciprocal(yv[:, :], yv[:, :]))
            for q in range(2):
                o = xo[:, q, :, :].rearrange("p j (g c) -> p g j c", g=BH)
                pr = psf[:, 0:4 * BANK].rearrange("p (g j q s c) -> p q s g j c", g=BH, j=J, q=2, s=2)[:, q, 1]
                rstd = yv[:, :].rearrange("p (g j q) -> p q g j", g=BH, j=J)[:, q].unsqueeze(3).broadcast_to([P, BH, J, C])
                last = dve.tensor_tensor(o, pr, rstd, ALU.mult)
                last.then_inc(sem("scaled_out"), 1)
            dve.wait_ge(sem("scaled_out"), 2)
            dve.wait_ge(sem("xo_ready"), 1)
            dve.tensor_tensor(xo[:, 1], xo[:, 1], xrow[:, 1], ALU.add).then_inc(sem("xo_ready"), 1)

        @block.tensor
        def _(pe):
            pe.wait_ge(sem("pool_set"), POOL_SET["inv512"])
            pe.wait_ge(sem("x_in"), 16)
            for q in range(2):
                pe.matmul(ps[:, 0, :], inv512[:, :], xs[:, q, :], start=(q == 0), stop=(q == 1))
            pe.wait_ge(sem("sq0"), 1)
            for q in range(2):
                mm = pe.matmul(ps[:, 1, :], inv512[:, :], sq[:, q, :], start=(q == 0), stop=(q == 1))
            mm.then_inc(sem("gsum0"), 1)
            pe.wait_ge(sem("band_in"), 16)
            pe.wait_ge(sem("const_in"), 16)
            for m in range(2):
                for q in range(2):
                    pe.wait_ge(sem("xpad_ready"), q + 1)
                    for d in range(3):
                        mm = pe.matmul(ps[:, m, :], bandv[:, q, d, m, :], xpad[:, q, :, d:d + C],
                                       start=(q == 0 and d == 0), stop=(q == 1 and d == 2))
                mm.then_inc(sem("conv_done"), 1)
            pe.wait_ge(sem("csum"), 1)
            pe.matmul(ps[:, 2, 0:4], cst("sum16"), csum[:, :, :].rearrange("p s m -> p (s m)"), start=True, stop=True)\
              .then_inc(sem("cgroup"), 1)
            pe.wait_ge(sem("caff"), 1)
            pe.wait_ge(sem("x1_rows"), 2)
            for j in range(J):
                for q in range(2):
                    col = 2 * BANK + j * HW + q * P
                    mm = pe.transpose(psf[:, col:col + P], xs[:, q, j * P:(j + 1) * P], ident)
            mm.then_inc(sem("x1_tp"), 1)

            def keep_warm(bank, n):
                for _ in range(n):
                    pe.matmul(ps[:, bank, :], zero_bf[:, 0:P], zero_bf[:, :], start=True, stop=True)

            pe.wait_ge(sem("pool_set"), POOL_SET["zero"])
            keep_warm(0, 8)

            def norm_group(n):
                pe.wait_ge(sem("npart"), n + 1)
                pe.matmul(ps[:, 7, 0:2 * J], cst("pair_half"), nsm[:, 6:8, :].rearrange("p s j -> p (s j)"), start=True, stop=True)\
                  .then_inc(sem("ngroup"), 1)

            norm_group(0)
            keep_warm(0, 6)
            pe.wait_ge(sem("param_in"), 16)
            pe.wait_ge(sem("xn_ready"), J)

            def project(bank, w, src):
                for n in range(2):
                    mm = pe.matmul(ps[:, bank + n, :], w, src[:, n * BANK:(n + 1) * BANK], start=True, stop=True)
                return mm

            for n in range(2):
                mm = pe.matmul(ps[0:6, n, :], par("gates"), xn[:, n * BANK:(n + 1) * BANK], start=True, stop=True)
            mm.then_inc(sem("gate_done"), 1)
            project(2, par("wk"), xn).then_inc(sem("kq_done"), 1)
            project(4, par("wq"), xn).then_inc(sem("kq_done"), 1)

            def square_sums(col):
                for i in range(2 * J):
                    mm = pe.matmul(ps[:, 6, col + BH * i:col + BH * i + BH], sq[:, i // J, (i % J) * P:(i % J + 1) * P],
                                   cst("ones64")[:, 0:P:64], start=True, stop=True)
                return mm

            def turn_all(at, src):
                for i in range(2 * J):
                    mm = pe.transpose(psf[:, at * BANK + i * P:at * BANK + (i + 1) * P], src[:, i * P:(i + 1) * P], ident)
                return mm

            pe.wait_ge(sem("kq_sq"), 1)
            square_sums(0).then_inc(sem("kq_sum"), 1)
            pe.wait_ge(sem("vals"), 1)
            for i, gate in ((0, 2), (1, 1)):
                for b2 in range(BH):
                    r = 3 * b2 + gate
                    pe.matmul(ps[:, 7, 128 * i + 64 * b2:128 * i + 64 * b2 + 64], const[0:6, r:r + 1].broadcast_to([6, P]),
                              vals[:, :], start=True, stop=True)
                pe.matmul(ps[:, 7, 256 + 64 * i:320 + 64 * i], cst("half_sel", 6)[:, i * P:(i + 1) * P], vals[:, :], start=True, stop=True)
            for j in range(J):
                mm = pe.matmul(ps[:, 7, 384:384 + NS], cst("tok_sel", 6)[:, j * P:(j + 1) * P], vals[:, j * NS:(j + 1) * NS],
                               start=(j == 0), stop=(j == J - 1))
            mm.then_inc(sem("coef_ps"), 1)
            pe.wait_ge(sem("gate_sig"), 1)
            pe.wait_ge(sem("k_spread"), 1)
            turn_all(0, nrm).then_inc(sem("inv_tp"), 1)
            pe.wait_ge(sem("kq_sq"), 2)
            pe.wait_ge(sem("kq_norm"), 1)
            square_sums(2 * J * BH).then_inc(sem("kq_sum"), 1)
            pe.wait_ge(sem("qraw"), 1)
            project(4, par("wv"), xn).then_inc(sem("v_done"), 1)
            def turn_keys(bank, half):
                for t in range(NS // 2):
                    mm = pe.transpose(psf[:, bank * BANK + t * P:bank * BANK + (t + 1) * P],
                                      kbd[:, half * POS + t * P:half * POS + (t + 1) * P], ident)
                mm.then_inc(sem("ktok_tp"), 1)

            pe.wait_ge(sem("kbd_ready"), 1)
            pe.wait_ge(sem("kq_norm"), 2)
            pe.wait_ge(sem("coef_ready"), 1)
            turn_keys(6, 0)
            pe.wait_ge(sem("kraw"), 1)
            pe.wait_ge(sem("q_spread"), 1)
            turn_all(2, hf).then_inc(sem("inv_tp"), 1)
            pe.wait_ge(sem("v_ready"), 2)
            turn_keys(4, 1)
            for m in range(4):
                if m == 2:
                    pe.wait_ge(sem("qt_ready"), 1)
                pe.matmul(ps[:, m, :], zero_bf[:, 0:P], zero_bf[:, :], start=True, stop=True)\
                  .then_inc(sem("m_zero" if m < 3 else "g10"), 1)
            pe.wait_ge(sem("ktok_ready"), 2)
            pe.wait_ge(sem("pool_set"), POOL_SET["bd"])

            with pe.Fori(0, NS) as t:
                def per_pair(bank, col, w, x, start=True):
                    for j in range(J):
                        mm = pe.matmul(ps[:, bank, col + 32 * j:col + 32 * j + 32], w[:, P * j:P * j + P],
                                       x[:, 32 * j:32 * j + 32], start=start, stop=True, skip_group_check=not start)
                    return mm

                def begin(col, scale, x):
                    pe.matmul(ps[:, 5, col:col + P], cst(scale), x, start=True, stop=False, skip_group_check=True)

                def turn(bank, col, x):
                    return pe.transpose(ps[:, bank, col:col + P], x, ident)

                def turn_weights(bank, m):
                    for j in range(J):
                        mm = turn(bank, P * j, we[:, m, P * j:P * j + P])
                    return mm

                def gradient(m, left, right, half):
                    cols = slice(half * BANK // 2, (half + 1) * BANK // 2)
                    return pe.matmul(ps[:, m, cols], left, right[:, cols], start=False, stop=False, skip_group_check=True)

                pe.wait_ge(sem("w10_new"), t + 1)
                for j in range(J):
                    mm = pe.matmul(ps[:, 4, 32 * j:32 * j + 32], w10[:, P * j:P * j + P], kbd[:, bass.ds(t * P + 32 * j, 32)],
                                   start=True, stop=True)
                mm.then_inc(sem("z0_done"), 1)
                keep_warm(5, FILL[0])
                pe.wait_ge(sem("w11_new"), t + 1)
                turn_weights(7, 1).then_inc(sem("w11_tp"), 1)
                begin(0, "ident", kbd[:, bass.ts(t, P)])
                pe.wait_ge(sem("w20_new"), t + 1)
                pe.wait_ge(sem("u0_ready"), t + 1)
                per_pair(5, 0, we[:, 0, :], act_u[:, 0, :], start=False).then_inc(sem("h1_ps"), 1)
                gradient(2, u_tok[:, 1, :], r_fbd, 1).then_inc(sem("g21"), 1)
                pe.wait_ge(sem("w11_d"), t + 1)
                turn(7, P, act_u[:, 0, :]).then_inc(sem("u0_tp"), 1)
                pe.wait_ge(sem("z0_kept"), t + 1)
                keep_warm(4, FILL[1])
                pe.wait_ge(sem("h1_ready"), t + 1)
                per_pair(4, P, wd[:, 1, :], h1bd).then_inc(sem("z1_done"), 1)
                pe.wait_ge(sem("u0_tok"), t + 1)
                turn(7, 0, h1bd[:, :]).then_inc(sem("h1_tp"), 1)
                pe.wait_ge(sem("w21_new"), t + 1)
                turn_weights(6, 2).then_inc(sem("w21_tp"), 1)
                pe.wait_ge(sem("h1mv"), t + 1)
                begin(P, "ident", h1mv[:, :])
                pe.wait_ge(sem("u1_ready"), t + 1)
                per_pair(5, P, we[:, 2, :], act_u[:, 1, :], start=False).then_inc(sem("h2_ps"), 1)
                pe.wait_ge(sem("h1_tok"), t + 1)
                turn(7, P, act_u[:, 1, :]).then_inc(sem("u1_tp"), 1)
                pe.wait_ge(sem("w21_d"), t + 1)
                turn_weights(6, 0).then_inc(sem("w20_tp"), 1)
                pe.wait_ge(sem("z1_kept"), t + 1)
                keep_warm(4, FILL[2])
                pe.wait_ge(sem("r_ready"), t + 1)
                per_pair(4, 2 * P, wd[:, 2, :], rbd).then_inc(sem("du1_done"), 1)
                pe.wait_ge(sem("u1_tok"), t + 1)
                turn(7, 2 * P, rbd[:, :]).then_inc(sem("r_tp"), 1)
                keep_warm(5, FILL[3])
                begin(2 * P, "twice", rbd[:, :])
                pe.wait_ge(sem("dz1_ready"), t + 1)
                per_pair(5, 2 * P, we[:, 1, :], dz1, start=False).then_inc(sem("dh1_ps"), 1)
                pe.wait_ge(sem("w20_d"), t + 1)
                turn(6, 2 * P, dz1[:, :])
                turn(6, 3 * P, z_g[:, 0, :]).then_inc(sem("dz1_tp"), 1)
                pe.wait_ge(sem("scaled"), 4 * t + 2)
                pe.wait_ge(sem("r_fbd"), t + 1)
                gradient(2, u_tok[:, 1, :], r_fbd, 0)
                pe.wait_ge(sem("dh1_ready"), t + 1)
                for j in range(J):
                    mm = pe.matmul(ps[32 * j:32 * j + 32, 4, 3 * P:4 * P], dhbd[:, 32 * j:32 * j + 32], wd[:, 0, P * j:P * j + P],
                                   start=True, stop=True)
                mm.then_inc(sem("du0_done"), 1)
                turn(7, 3 * P, dhbd[:, :]).then_inc(sem("dh1_tp"), 1)
                pe.wait_ge(sem("dz1_tok"), t + 1)
                pe.wait_ge(sem("h1_fbd"), t + 1)
                gradient(1, dz_tok[:, 1, :], h1_fbd, 0)
                pe.wait_ge(sem("scaled"), 4 * t + 3)
                pe.wait_ge(sem("k_fbd"), t + 1)
                pe.wait_ge(sem("dz0_ready"), t + 1)
                for j in range(J):
                    mm = pe.matmul(ps[:, 3, P * j:P * j + P], k_fbd[:, P * j:P * j + P], dz_tok[:, 0, :], start=False, stop=False,
                                   skip_group_check=True)
                mm.then_inc(sem("g10"), 1)
                gradient(1, dz_tok[:, 1, :], h1_fbd, 1).then_inc(sem("g11"), 1)
                pe.wait_ge(sem("scaled"), 4 * t + 4)
                pe.wait_ge(sem("dh_fbd"), t + 1)
                gradient(0, u_tok[:, 0, :], dh_fbd, 0)
                gradient(0, u_tok[:, 0, :], dh_fbd, 1).then_inc(sem("g20"), 1)

            pe.matmul(ps[:, 2, BANK // 2:], u_tok[:, 1, :], r_fbd[:, BANK // 2:], start=False, stop=False,
                      skip_group_check=True).then_inc(sem("g21"), 1)

            pe.wait_ge(sem("w10_new"), NS + 1)
            for j in range(J):
                mm = pe.matmul(ps[:, 4, 0:E1], cst("dup64"), w10[:, j * E1:(j + 1) * E1], start=(j == 0), stop=(j == J - 1))
            mm.then_inc(sem("wm_tp"), 1)
            keep_warm(5, 4)
            pe.wait_ge(sem("wm_ready"), 1)

            def up(w, src, i):
                for n in range(4):
                    bh, half = n // 2, n % 2
                    if i:
                        pe.wait_ge(sem("uf_ready"), 4 * i)
                    pe.matmul(ps[:, UP_BANKS[i][n], :], w[64 * bh:64 * bh + 64, :], src[64 * bh:64 * bh + 64, half * BANK:(half + 1) * BANK],
                              start=True, stop=True).then_inc(sem("zf_done"), 1)

            def down(w, bank, i):
                for n in range(4):
                    bh, half = n // 2, n % 2
                    pe.wait_ge(sem("uf_ready"), 4 * i + n + 1)
                    mm = pe.matmul(ps[64 * bh:64 * bh + 64, bank + half, :], w, uf[:, n * BANK:(n + 1) * BANK], start=True, stop=True)
                mm.then_inc(sem("hf_done"), 1)

            pe.wait_ge(sem("w11_new"), NS + 1)
            pe.wait_ge(sem("w20_new"), NS + 1)
            up(w10m, qt, 0)
            pe.wait_ge(sem("wm_sum"), 1)
            pe.transpose(ps[:, 6, 0:E1], w11s[:, :, :].rearrange("p g d -> p (g d)"), ident).then_inc(sem("wm_tp"), 1)
            down(wme[:, 0, :], 4, 0)
            pe.wait_ge(sem("wm_sum"), 2)
            pe.wait_ge(sem("wm_ready"), 2)
            keep_warm(7, 5)
            pe.wait_ge(sem("hf_ready"), 1)
            up(w11m, hf, 1)
            down(wme[:, 2, :], 6, 1)

            keep_warm(0, 14)
            norm_group(1)
            keep_warm(0, 5)
            pe.wait_ge(sem("xn_ready"), 2 * J)
            project(0, par("attn_q"), xn).then_inc(sem("aqkv_done"), 1)
            project(2, par("attn_k"), xn).then_inc(sem("aqkv_done"), 1)
            project(4, par("attn_v"), xn).then_inc(sem("aqkv_done"), 1)
            pe.wait_ge(sem("aq_ready"), 1)
            pe.wait_ge(sem("ak_ready"), 1)
            for n in range(NK):
                pe.wait_ge(sem("qk_pool" if n % 2 else "qk_dve"), n // 2 + 1)
                if n >= 2:
                    pe.wait_ge(sem("score_done"), n - 1)
                turn_all((n % 2) * 2, prod[n % 4]).then_inc(sem("qk_tp"), 1)

            pe.wait_ge(sem("av_ready"), 1)
            pe.wait_ge(sem("score_done"), NK)
            for n in range(NK + 1):
                if n >= 3:
                    pe.wait_ge(sem("pv_ready"), n - 2)
                pe.wait_ge(sem("attx_ready"), n + 1)
                turn_all(n % 3 * 2, attx[n % 2]).then_inc(sem("att_tp"), 1)

            pe.wait_ge(sem("pv_ready"), NK)
            keep_warm(6, 6)
            pe.wait_ge(sem("x3_ready"), 1)
            keep_warm(6, 4)
            norm_group(2)
            for q in range(2):
                for j in range(J):
                    col = 4 * BANK + (q * J + j) * P
                    pe.transpose(psf[:, col:col + P], xc[:, j * HW + q * P:j * HW + (q + 1) * P], ident)
            pe.wait_ge(sem("wout"), 1)
            pe.matmul(ps[:, 6, 0:C], cst("center_neg_t", C), wout[0:C, :], start=True, stop=True)
            pe.matmul(ps[:, 6, C:2 * C], par("ln_beta")[0:C].broadcast_to([C, P]), par("out_w")[0:C, 0:C], start=True, stop=False)
            pe.matmul(ps[:, 6, C:2 * C], par("out_b")[0:C].broadcast_to([C, P]), cst("ident", C)[:, 0:C], start=False, stop=True)\
              .then_inc(sem("xrow_tp"), 1)
            keep_warm(0, 3)
            pe.wait_ge(sem("xn_ready"), 3 * J)

            def feature(f, n, bank):
                bh, half = n // 2, n % 2
                pe.matmul(ps[:, bank, :], par("scan_w")[64 * bh:64 * bh + 64, f * P:(f + 1) * P],
                          xn[64 * bh:64 * bh + 64, half * BANK:(half + 1) * BANK], start=True, stop=True).then_inc(sem("feat_done"), 1)

            for n in range(4):
                feature(0, n, n)
                if n == 0:
                    pe.wait_ge(sem("xrow_ready"), 1)
                feature(1, n, 4 + n)
            for n in range(4):
                pe.wait_ge(sem("lam_b"), n + 1)
                feature(2, n, n)
            pe.wait_ge(sem("silu"), 4)
            keep_warm(4, 7)
            pe.wait_ge(sem("sw_ready"), 4)
            for wc in range(NWC):
                n = W // NWC
                pe.matmul(ps[:, 4 + wc, :], ident,
                          sw[:, :].rearrange("p (b w s) -> p b w s", b=B, w=W)[:, :, wc * n:(wc + 1) * n, 1:], start=True, stop=False)
                pe.wait_ge(sem("sb_ready"), wc + 1)
                pe.matmul(ps[:, 4 + wc, :], ident, seqs_b(fb, wc).rearrange("p (n s) -> p s n", s=B + 1)[:, 1:, :],
                          start=False, stop=True).then_inc(sem("sum_done"), 1)
            pe.wait_ge(sem("og_ready"), 4)
            pe.wait_ge(sem("tot_ready"), NWC)
            for n in range(4):
                for i in range(4 * n, 4 * n + 4):
                    mm = pe.matmul(psf[:, i * P:(i + 1) * P], tot[:, i * P:(i + 1) * P], cm[:, :], start=True, stop=True)
                mm.then_inc(sem("out_mm"), 1)


def _constants():
    c = np.zeros((P, NCONST), np.float32)

    def put(name, value):
        a, b = CONST_COLS[name]
        v = np.asarray(value, np.float32).reshape(-1, b - a)
        c[:v.shape[0], a:b] = v

    i = np.arange(P)
    put("ident", np.eye(P))
    put("twice", 2 * np.eye(P))
    put("own_half", i[:, None] // 64 == i[None] // W % BH)
    put("pair_half", 0.5 * (i[:, None] // 2 == i[None] // 2))
    put("sum16", (i[:, None] // 16 == i[None] // 16) / 16.0)
    put("ones64", i[:, None] // 64 == i[None] // 64)
    put("dup64", i[:, None] % 64 == i[None] % 64)
    put("head_sel", i[:, None] // 8 == np.arange(BH * NHD)[None])
    ch = 2 * (i // 4) + i % 2
    center_neg = 1.0 / C - (ch[:, None] == np.arange(C)[None])
    put("center_neg", center_neg)
    put("center_neg_t", center_neg.T)
    put("block_j", i[:, None] // 32 == np.arange(J)[None])
    half = np.zeros((6, 2, BH, 64), np.float32)
    tok = np.zeros((6, J, J, BH, W), np.float32)
    for b2 in range(BH):
        half[3 * b2 + 2, 0, b2] = 1
        half[3 * b2 + 1, 1, b2] = 1
        for j in range(J):
            tok[3 * b2, j, j, b2] = 1
    put("half_sel", half.reshape(6, -1))
    put("tok_sel", tok.reshape(6, -1))
    one = [(-MAX_LR / W * GRAD_SCALE / 2, -MAX_LR * GRAD_SCALE / 2), (-0.5 / W, 0.5), (0.5 / W, 0.5)]
    put("gate_scale", np.array(one * 2))
    put("eps", np.full((P, 1), GEPS))
    return c


def _block_diag(m):
    out = np.zeros((2 * m.shape[0], 2 * m.shape[1]), np.float32)
    out[:m.shape[0], :m.shape[1]] = m
    out[m.shape[0]:, m.shape[1]:] = m
    return out


def kernel(x, L0_conv_weight, L0_conv_bias, L0_conv_gamma, L0_conv_beta, L0_conv_alpha, L1_conv_Wq, L1_conv_Wk, L1_conv_Wv,
           L1_conv_w_lr, L1_conv_w_forget, L1_conv_w_eta, L1_conv_w1_0, L1_conv_w2_0, L1_conv_w1_1, L1_conv_w2_1,
           L2_conv_W_qkv, L3_conv_in_w, L3_conv_in_b, L3_conv_out_w, L3_conv_out_b, L3_conv_gamma, L3_conv_beta):
    import concourse.bacc as bacc
    from concourse.bass_utils import run_bass_kernel_spmd

    xs = np.asarray(x).reshape(BH, J, 2, P, C).transpose(3, 2, 1, 0, 4)
    w = np.asarray(L0_conv_weight).reshape(2, 8, 3, 3, 2, 8, 16)
    band = np.zeros((8, 16, 2, 3, 2, 8, 16), np.float32)
    for i in range(3):
        for l in range(16):
            if 0 <= l + i - 1 < 16:
                band[:, l + i - 1, :, :, :, :, l] = w[:, :, i, :, :, :, l].transpose(1, 0, 2, 3, 4)
    blk = np.zeros((P, NPARAM), np.float32)

    def put(name, value):
        a, b = PARAM_COLS[name]
        blk[:, a:b] = np.asarray(value).reshape(P, b - a)

    def rows16(v):
        return np.repeat(np.asarray(v).reshape(2, 8), 16, axis=1).T

    def twice(m):
        return np.concatenate([np.asarray(m)] * 2, axis=0)

    put("conv_bias", np.asarray(L0_conv_bias).reshape(2, P).T)
    put("conv_gamma", rows16(L0_conv_gamma))
    put("conv_beta", rows16(L0_conv_beta))
    put("conv_alpha", np.broadcast_to(np.asarray(L0_conv_alpha), (P, 1)))
    put("wk", _block_diag(np.asarray(L1_conv_Wk)))
    put("wv", _block_diag(np.asarray(L1_conv_Wv)))
    put("wq", _block_diag(np.asarray(L1_conv_Wq)))
    put("gates", _block_diag(np.stack([np.asarray(L1_conv_w_lr), np.asarray(L1_conv_w_forget), np.asarray(L1_conv_w_eta)], axis=1)))
    put("mats_e", np.concatenate([np.asarray(L1_conv_w2_0), np.asarray(L1_conv_w1_1).T, np.asarray(L1_conv_w2_1)], axis=1))
    put("w1_0", twice(L1_conv_w1_0))
    wqkv = np.asarray(L2_conv_W_qkv).reshape(3, C, C)
    for n, name in enumerate(("attn_q", "attn_k", "attn_v")):
        put(name, _block_diag(wqkv[n].T))
    hd = np.repeat(np.arange(C), 2)
    he = (np.arange(C).reshape(-1, 1, 2).repeat(2, axis=1)).reshape(-1)
    pick = (2 * C + hd, he, C + hd)
    put("scan_w", twice(np.concatenate([np.asarray(L3_conv_in_w)[:, s] for s in pick], axis=1)))
    put("scan_b", np.stack([np.asarray(L3_conv_in_b)[s] for s in pick], axis=1))
    put("out_w", _block_diag(np.asarray(L3_conv_out_w)))
    put("out_b", twice(L3_conv_out_b))
    put("ln_gamma", twice(L3_conv_gamma))
    put("ln_beta", twice(L3_conv_beta))

    arrays = {"xs": np.ascontiguousarray(xs.reshape(P, 2, BANK)), "band": band.reshape(P, -1), "const": _constants(), "param": blk}
    nc = bacc.Bacc("TRN2", target_bir_lowering=False, num_devices=1)
    args = [nc.dram_tensor(n, a.shape, F32, kind="ExternalInput").ap() for n, a in arrays.items()]
    out = nc.dram_tensor("out", (P, 2, J, P), F32, kind="ExternalOutput").ap()
    conv_attn_scan_kernel(nc, *args, out)
    r = run_bass_kernel_spmd(nc, [arrays], core_ids=[0])
    got = r.results[0]["out"].reshape(P, 2, J, BH, C).transpose(3, 2, 1, 0, 4)
    return np.ascontiguousarray(got.reshape(B, H, W, C))
```

```python
from contextlib import ExitStack

import numpy as np

import concourse.bass as bass
from concourse import mybir

F32 = mybir.dt.float32
BF16 = mybir.dt.bfloat16
ALU = mybir.AluOpType
ACT = mybir.ActivationFunctionType
AX_X = mybir.AxisListType.X

B, H, W, C = 8, 16, 16, 64
BH, J = 2, 4
HW = H * W
POS = J * HW
NT = 2 * POS
P = 128
E1 = 128
NS = H
TOK = B * W
NK = 9
PADW = H + 6
NHD = 8
BANK = 512
GEPS = 1e-5
GC = 0.044715
GS = float(np.sqrt(2.0 / np.pi))

NORM_BANK = (7, 7, 5)
UP_BANKS = ((0, 1, 3, 7), (0, 1, 2, 3))
POOL_SET = {"zero": 1, "inv512": 2, "xpad": 3, "bd": 10, "kv": 12, "scan": 16}
GRAD_SCALE = 2.0 / (W * C)
MAX_LR = 0.1

CONST_COLS = {}


def _const_layout():
    at = 0
    for name, width in (("ident", P), ("twice", P), ("own_half", P), ("pair_half", P), ("sum16", P), ("ones64", P), ("dup64", P), ("head_sel", BH * NHD),
                        ("center", C), ("center_t", P), ("block_j", J), ("half_sel", 2 * P), ("tok_sel", J * P), ("gate_scale", 2),
                        ("eps", 1)):
        CONST_COLS[name] = (at, at + width)
        at += width
    return at


NCONST = _const_layout()

PARAM_COLS = {}


def _param_layout():
    at = 0
    for name, width in (("conv_bias", 2), ("conv_gamma", 2), ("conv_beta", 2), ("conv_alpha", 1), ("wk", P), ("wv", P),
                        ("wq", P), ("gates", 6), ("mats_e", 3 * C), ("w1_0", E1), ("attn_q", P),
                        ("attn_k", P), ("attn_v", P), ("scan_w", 3 * P), ("scan_b", 3), ("out_w", P), ("out_b", 1),
                        ("ln_gamma", 1), ("ln_beta", 1)):
        PARAM_COLS[name] = (at, at + width)
        at += width
    return at


NPARAM = _param_layout()


def conv_attn_scan_kernel(nc, xs_d, band_d, const_d, param_d, out_d):
    ctx = ExitStack()
    with ctx:
        def sb(name, shape):
            return ctx.enter_context(nc.sbuf_tensor(name, shape, F32))

        sems = {}

        def sem(name):
            if name not in sems:
                sems[name] = ctx.enter_context(nc.semaphore(name))
            return sems[name]

        ps = ctx.enter_context(nc.psum_tensor("ps", [P, 8, BANK], F32))
        psf = ps[:, :, :].rearrange("p b n -> p (b n)")

        const = sb("const_sb", [P, NCONST])
        param = sb("param_sb", [P, NPARAM])

        def cst(name, rows=P):
            a, b = CONST_COLS[name]
            return const[0:rows, a:b]

        def par(name):
            a, b = PARAM_COLS[name]
            return param[:, a:b]

        ident = cst("ident")

        def carve(arena):
            at = [0]

            def take(*dims):
                n = int(np.prod(dims))
                flat = arena[:, at[0]:at[0] + n]
                at[0] += n
                if len(dims) == 1:
                    return flat
                names = "abc"[:len(dims)]
                return flat.rearrange(f"p ({' '.join(names)}) -> p {' '.join(names)}", **dict(zip(names, dims)))
            return take

        arena_conv = sb("arena_conv", [P, 1536 + 1056 + 2048])
        arena_mem = sb("arena_mem", [P, 3 * 512 * 3 + 512 * 6])
        arena_att = sb("arena_att", [P, 2 * J * PADW * PADW + 2 * POS + NK * P + 2 * P])
        conv_cols, mem_cols, att_cols = carve(arena_conv), carve(arena_mem), carve(arena_att)

        xs = sb("xs_sb", [P, 2, BANK])
        sq = sb("sq", [P, 2, BANK])
        band = conv_cols(2 * 3 * 2 * P)
        bandv = band[:, :].rearrange("p (q d m n) -> p q d m n", q=2, d=3, m=2)
        inv512 = sb("inv512", [P, P])
        gst = sb("gst", [P, 4, 256])
        xpad = conv_cols(2, B, C + 2)
        cstat = sb("cstat", [P, 2, 6])
        cmv = sb("cmv", [P, 2, 2])
        csum = sb("csum", [P, 2, 2])
        csm = sb("csm", [P, 8, 2])
        relu_p = conv_cols(2, BANK)
        relu_n = conv_cols(2, BANK)
        alpha_n = sb("alpha_n", [P, 1])

        xc = sb("xc", [P, POS])
        xn = sb("xn", [P, POS])
        nst = sb("nst", [P, J, 6])
        nmv = sb("nmv", [P, J, 2])
        nsm = sb("nsm", [P, 8, J])

        kraw = sb("kraw", [P, POS])
        qraw = sb("qraw", [P, POS])
        nrm = sb("nrm", [P, POS])
        qt = sb("qt", [P, POS])
        kbd = sb("kbd", [P, NS * TOK])
        vbd = sb("vbd", [P, NS * TOK])
        silu_ex = sb("silu_ex", [P, NT])
        k_now = sb("k_now", [P, P])
        k_tok = sb("k_tok", [P, P])
        gates = sb("gates", [6, POS])
        gsum = sb("gsum", [6, J * NS])
        vals = sb("vals", [6, J * NS])
        eta_e = sb("eta_e", [P, NS * 8])
        keep_e = sb("keep_e", [P, NS * 8])
        eta_d = sb("eta_d", [P, NS * J])
        keep_d = sb("keep_d", [P, NS * J])
        keep_now = sb("keep_now", [P, 12])
        lrn = sb("lrn", [P, NS])
        lrh = sb("lrh", [P, NS])
        we = mem_cols(3, 8 * C)
        w10 = mem_cols(J * E1)
        wd = mem_cols(3, J * E1)
        qe = mem_cols(3, 8 * C)
        q10 = mem_cols(J * E1)
        zero = sb("zero", [P, BANK])
        zero_bf = zero[:, 0:BANK // 2].bitcast(BF16)
        act_u = sb("act_u", [P, 2, P])
        z_sq = sb("z_sq", [P, 2, P])
        z_cp = sb("z_cp", [P, 2, P])
        z_y = sb("z_y", [P, 2, P])
        z_t = sb("z_t", [P, 2, P])
        z_t2 = sb("z_t2", [P, 2, P])
        z_s1 = sb("z_s1", [P, 2, P])
        z_s2 = sb("z_s2", [P, 2, P])
        z_g = sb("z_g", [P, 2, P])
        h1bd = sb("h1bd", [P, P])
        h1mv = sb("h1mv", [P, P])
        h1_tok = sb("h1_tok", [P, P])
        spread_now = sb("spread_now", [P, J])
        k_inv = sb("k_inv", [P, 2 * J * BH])
        q_inv = sb("q_inv", [P, 2 * J * BH])
        rbd = sb("rbd", [P, P])
        dhbd = sb("dhbd", [P, P])
        dz1 = sb("dz1", [P, P])
        u_tok = sb("u_tok", [P, 2, P])
        dz_tok = sb("dz_tok", [P, 3, P])
        k_fbd = mem_cols(BANK)
        h1_fbd = mem_cols(BANK)
        r_fbd = mem_cols(BANK)
        dh_fbd = mem_cols(BANK)
        wme = sb("wme", [P, 3, C])
        wms = sb("wms", [P, 3, C])
        w11s = sb("w11s", [P, 2, C])
        w10s = sb("w10s", [P, E1])
        w10m = sb("w10m", [P, E1])
        w11m = sb("w11m", [P, E1])
        uf = sb("uf", [P, NT])
        hf = sb("hf", [P, POS])
        xh = sb("xh", [P, POS])

        aq = kraw
        kpad = att_cols(J, PADW, PADW)
        vpad = att_cols(J, PADW, PADW)
        prod2 = att_cols(2, POS)
        mx = att_cols(P)
        att = att_cols(NK, P)
        rs = att_cols(P)
        attx = (qraw, qt)
        ex = silu_ex[:, 0:NK * P]
        acc = hf
        prod = (prod2[:, 0], prod2[:, 1], uf[:, 0:POS], uf[:, POS:2 * POS])

        ROW = W * (H + 1)
        mem_again, att_again, conv_again = carve(arena_mem), carve(arena_att), carve(arena_conv)
        lam = mem_again(B * ROW)
        inp = mem_again(B * ROW)
        sw = mem_again(B * ROW)
        rw = att_again(B * ROW)
        lam_b = att_again(HW * (B + 1))
        inp_b = att_again(HW * (B + 1))
        fb = conv_again(HW * (B + 1))
        rb = sb("rb", [P, HW * (B + 1)])
        tot = conv_again(NT)
        xrow = mem_again(2, J, P)
        sig_i = vbd
        silu = silu_ex
        rest = kbd
        forget_neg = sb("forget_neg", [P, 1])
        og = uf
        wout = sb("wout", [P, C])
        cm = sb("cm", [P, 2 * C])
        bout = sb("bout", [P, C])
        ysq = qt
        yv = sb("yv", [P, 2 * B])
        xo = xh[:, :].rearrange("p (q j n) -> p q j n", q=2, j=J)
        NWC = 4

        def seq_w(buf, lo, hi):
            return buf[:, :].rearrange("p (b w s) -> p b s w", w=W, s=H + 1)[:, lo:hi, 1:H + 1, :]

        def seq_b(buf, n):
            return buf[:, :].rearrange("p (w h s) -> p s h w", w=W, h=H)[:, 1 + 2 * n:3 + 2 * n]

        def seqs_b(buf, wc):
            n = W // NWC * H * (B + 1)
            return buf[:, wc * n:(wc + 1) * n]

        def bhw(ap, n=B):
            return ap.rearrange("p (b h w) -> p b h w", b=n, h=H)

        def halves(buf_cols, b2):
            return buf_cols.rearrange("p (j g w) -> p j g w", j=J, g=BH)[64 * b2:64 * b2 + 64, :, b2, :]

        def shifted(buf, n):
            dy, dx = 3 * (n // 3), 3 * (n % 3)
            return buf[:, :, dy:dy + H, dx:dx + W]

        block = ctx.enter_context(nc.Block())

        @block.sync
        def _(sp):
            sp.dma_start(xs[:, :, :], xs_d).then_inc(sem("x_in"), 16)
            sp.dma_start(const[:, :], const_d).then_inc(sem("const_in"), 16)
            sp.dma_start(band[:, :], band_d).then_inc(sem("band_in"), 16)
            sp.dma_start(param[:, :], param_d).then_inc(sem("param_in"), 16)
            for q, half_ready in enumerate(("xo_ready", "xo_last")):
                sp.wait_ge(sem(half_ready), 1)
                sp.dma_start(out_d[:, q, :, :], xo[:, q, :, :]).then_inc(sem("out_done"), 16)
            sp.wait_ge(sem("out_done"), 32)

        @block.gpsimd
        def _(pool):
            pool.memset(zero[:, :], 0.0).then_inc(sem("pool_set"), 1)
            pool.memset(inv512[:, :], 1.0 / 512.0).then_inc(sem("pool_set"), 1)
            pool.memset(xpad[:, :, :, :], 0.0).then_inc(sem("pool_set"), 1)
            pool.memset(kbd[:, :], 0.0).then_inc(sem("pool_set"), 1)
            pool.memset(vbd[:, :], 0.0).then_inc(sem("pool_set"), 1)
            pool.memset(h1bd[:, :], 0.0).then_inc(sem("pool_set"), 1)
            pool.memset(rbd[:, :], 0.0).then_inc(sem("pool_set"), 1)
            pool.memset(dhbd[:, :], 0.0).then_inc(sem("pool_set"), 1)
            pool.memset(r_fbd[:, :], 0.0).then_inc(sem("pool_set"), 1)
            pool.memset(u_tok[:, 1, :], 0.0).then_inc(sem("pool_set"), 1)
            pool.memset(kpad[:, :, :, :], 0.0).then_inc(sem("pool_set"), 1)
            pool.memset(vpad[:, :, :, :], 0.0).then_inc(sem("pool_set"), 1)
            pool.wait_ge(sem("const_in"), 16)
            pool.wait_ge(sem("coef_ready"), 1)
            with pool.Fori(0, NS) as t:
                pool.wait_ge(sem("g10"), t + 1)
                pool.wait_ge(sem("coef_ready"), 1)
                pool.tensor_copy(k_now[:, :], kbd[:, bass.ts(t, P)]).then_inc(sem("k_now"), 1)
                pool.tensor_copy(keep_now[:, 0:8], keep_e[:, bass.ts(t, 8)]).then_inc(sem("keep_now"), 1)
                pool.tensor_copy(keep_now[:, 8:12], keep_d[:, bass.ts(t, J)]).then_inc(sem("keep_now"), 1)
                pool.tensor_tensor(spread_now[:, :], cst("block_j"), lrh[:, bass.ds(t, 1)].broadcast_to([P, J]),
                                   ALU.mult).then_inc(sem("keep_now"), 1)
                pool.wait_ge(sem("keep_now"), 3 * t + 3)
                def kept_part(m, new, done):
                    pool.wait_ge(sem(new), t + 1)
                    pool.tensor_tensor(qe[:, m, :].rearrange("p (b d) -> p b d", b=8),
                                       we[:, m, :].rearrange("p (b d) -> p b d", b=8),
                                       keep_now[:, 0:8].unsqueeze(2).broadcast_to([P, 8, C]),
                                       ALU.mult).then_inc(sem(done), 1)

                kept_part(1, "w11_new", "q_11")
                kept_part(0, "w20_new", "q_20")
                pool.wait_ge(sem("h1_ready"), t + 1)
                pool.wait_ge(sem("v_ready"), 2)
                pool.tensor_tensor(h1mv[:, :], h1bd[:, :], vbd[:, bass.ts(t, P)], ALU.subtract).then_inc(sem("h1mv"), 1)
                pool.wait_ge(sem("k_tok"), t + 1)
                pool.tensor_tensor(k_fbd[:, :].rearrange("p (j n) -> p j n", j=J),
                                   k_tok[:, :].unsqueeze(1).broadcast_to([P, J, P]),
                                   spread_now[:, :].unsqueeze(2).broadcast_to([P, J, P]), ALU.mult).then_inc(sem("k_fbd"), 1)
                kept_part(2, "w21_new", "q_21")
                pool.wait_ge(sem("w10_new"), t + 1)
                pool.tensor_tensor(q10[:, :].rearrange("p (j e) -> p j e", j=J), w10[:, :].rearrange("p (j e) -> p j e", j=J),
                                   keep_now[:, 8:12].unsqueeze(2).broadcast_to([P, J, E1]),
                                   ALU.mult).then_inc(sem("q_10"), 1)
                pool.wait_ge(sem("h1_tok"), t + 1)
                pool.tensor_tensor(h1_fbd[:, :].rearrange("p (j n) -> p j n", j=J),
                                   h1_tok[:, :].unsqueeze(1).broadcast_to([P, J, P]),
                                   spread_now[:, :].unsqueeze(2).broadcast_to([P, J, P]), ALU.mult).then_inc(sem("h1_fbd"), 1)
            pool.wait_ge(sem("aq_ready"), 1)
            pool.wait_ge(sem("ak_ready"), 1)
            for n in range(1, NK, 2):
                if n >= 4:
                    pool.wait_ge(sem("qk_tp"), n - 3)
                pool.tensor_tensor(bhw(prod[n % 4], J), bhw(aq[:, :], J), shifted(kpad, n), ALU.mult).then_inc(sem("qk_pool"), 1)
            def separators(buf, length):
                pool.memset(buf[:, :].rearrange("p (n s) -> p n s", s=length + 1)[:, :, 0], 0.0).then_inc(sem("pool_set"), 1)

            pool.wait_ge(sem("hf_done"), 2)
            separators(lam, H)
            separators(inp, H)
            for n in range(1, NK, 2):
                pool.wait_ge(sem("pv_ready"), n + 1)
                if n > 1:
                    pool.wait_ge(sem("odd_sum"), n // 2)
                pool.tensor_tensor(prod[0], prod[0], prod[1 + n // 2 % 2], ALU.add).then_inc(sem("odd_sum"), 1)
            pool.wait_ge(sem("x3_ready"), 1)
            separators(lam_b, B)
            separators(inp_b, B)
            def scan_input(n):
                pool.wait_ge(sem("silu"), n + 1)
                pool.wait_ge(sem("lam_ready"), 2 * n + 2)
                pool.tensor_tensor(seq_w(inp, 2 * n, 2 * n + 2), bhw(rest)[:, 2 * n:2 * n + 2], bhw(silu)[:, 2 * n:2 * n + 2],
                                   ALU.mult).then_inc(sem("inp_ready"), 1)

            def both_along_h(n):
                cols = slice(2 * n * ROW, 2 * (n + 1) * ROW)
                pool.wait_ge(sem("scan_w"), n + 1)
                pool.tensor_tensor(sw[:, cols], sw[:, cols], rw[:, cols], ALU.add).then_inc(sem("pool_sum"), 1)

            for n in range(3):
                scan_input(n)
            both_along_h(0)
            scan_input(3)
            for n in range(1, 4):
                both_along_h(n)
            for wc in range(NWC - 2):
                pool.wait_ge(sem("scan_b"), wc + 1)
                pool.tensor_tensor(seqs_b(fb, wc), seqs_b(fb, wc), seqs_b(rb, wc), ALU.add).then_inc(sem("pool_sum"), 1)
            pool.wait_ge(sem("scaled_out"), 1)
            pool.tensor_tensor(xo[:, 0], xo[:, 0], xrow[:, 0], ALU.add).then_inc(sem("xo_ready"), 1)

        @block.scalar
        def _(act):
            act.preload_act_table_set("sqrt_and_others")
            act.wait_ge(sem("x_in"), 16)
            act.activation(sq[:, :, :], xs[:, :, :], ACT.Square).then_inc(sem("sq0"), 1)
            act.wait_ge(sem("const_in"), 16)
            act.wait_ge(sem("gvar0"), 1)
            act.activation(gst[:, 3, :], gst[:, 2, :], ACT.Sqrt, bias=cst("eps")).then_inc(sem("gstd0"), 1)
            act.wait_ge(sem("cvar"), 1)
            act.activation(csm[:, 2, :], csm[:, 1, :], ACT.Sqrt, bias=cst("eps")).then_inc(sem("cstd"), 1)
            act.wait_ge(sem("caff"), 1)
            for m in range(2):
                act.activation(relu_p[:, m, :], ps[:, m, :], ACT.Relu, bias=csm[:, 5, m:m + 1], scale=csm[:, 4, m:m + 1])
                act.activation(relu_n[:, m, :], ps[:, m, :], ACT.Relu, bias=csm[:, 7, m:m + 1],
                               scale=csm[:, 6, m:m + 1]).then_inc(sem("relu"), 1)
            act.wait_ge(sem("x1_tp"), 1)
            for n in range(2):
                act.activation(xc[:, n * BANK:(n + 1) * BANK], ps[:, 2 + n, :], ACT.Copy).then_inc(sem("x1_ready"), 1)
            act.wait_ge(sem("nvar"), 1)
            act.activation(nsm[:, 2, :], nsm[:, 1, :], ACT.Sqrt, bias=cst("eps")).then_inc(sem("nstd"), 1)
            act.preload_act_table_set("gelu_apprx_tanh_and_others")
            act.wait_ge(sem("gate_done"), 1)
            act.activation(gates[:, :], psf[0:6, 0:POS], ACT.Tanh, scale=0.5).then_inc(sem("gate_sig"), 1)
            act.wait_ge(sem("kq_done"), 1)
            act.activation(sq[:, :, :], ps[:, 2:4, :], ACT.Square).then_inc(sem("kq_sq"), 1)
            act.preload_act_table_set("sqrt_and_others")
            act.activation(kraw[:, :], psf[:, 2 * BANK:4 * BANK], ACT.Copy).then_inc(sem("kraw"), 1)
            act.wait_ge(sem("kq_sum"), 1)
            act.activation(k_inv[:, :], ps[:, 0, 0:2 * J * BH], ACT.Sqrt).then_inc(sem("kq_norm"), 1)
            act.wait_ge(sem("kq_done"), 2)
            act.activation(sq[:, :, :], ps[:, 4:6, :], ACT.Square).then_inc(sem("kq_sq"), 1)
            act.wait_ge(sem("pool_set"), POOL_SET["bd"] - 2)
            act.wait_ge(sem("v_done"), 1)
            for b2 in range(BH):
                act.activation(vbd[:, :].rearrange("p (t j g w) -> p g t j w", t=NS, j=J, g=BH)[64 * b2:64 * b2 + 64, b2],
                               psf[64 * b2:64 * b2 + 64, 6 * BANK:8 * BANK].rearrange("p (j t w) -> p t j w", j=J, t=NS),
                               ACT.Copy).then_inc(sem("v_ready"), 1)
            act.activation(qraw[:, :], psf[:, 4 * BANK:6 * BANK], ACT.Copy).then_inc(sem("qraw"), 1)
            act.wait_ge(sem("kq_sum"), 2)
            act.activation(q_inv[:, :], ps[:, 0, 2 * J * BH:4 * J * BH], ACT.Sqrt).then_inc(sem("kq_norm"), 1)
            act.preload_act_table_set("gelu_apprx_tanh_and_others")
            with act.Fori(0, NS) as t:
                def hidden(i, done, ready, kept):
                    act.wait_ge(sem(done), t + 1)
                    act.activation(act_u[:, i, :], ps[:, 4, P * i:P * i + P], ACT.Gelu_apprx_tanh).then_inc(sem(ready), 1)
                    act.activation(z_sq[:, i, :], ps[:, 4, P * i:P * i + P], ACT.Square)
                    act.activation(z_cp[:, i, :], ps[:, 4, P * i:P * i + P], ACT.Copy).then_inc(sem(kept), 1)

                def tanh(i, y, th):
                    act.wait_ge(sem(y), t + 1)
                    act.activation(z_t[:, i, :], z_y[:, i, :], ACT.Tanh, scale=GS * GC).then_inc(sem(th), 1)

                def tanh_sq(i, th, t2):
                    act.wait_ge(sem(th), t + 1)
                    act.activation(z_t2[:, i, :], z_t[:, i, :], ACT.Square).then_inc(sem(t2), 1)

                def turned(m, bank, tp, cp):
                    act.wait_ge(sem(tp), t + 1)
                    act.activation(wd[:, m, :], ps[:, bank, :], ACT.Copy).then_inc(sem(cp), 1)

                def token_rows(out, bank, col, tp, done):
                    act.wait_ge(sem(tp), t + 1)
                    act.activation(out, ps[:, bank, col:col + P], ACT.Copy).then_inc(sem(done), 1)

                hidden(0, "z0_done", "u0_ready", "z0_kept")
                turned(1, 7, "w11_tp", "w11_d")
                token_rows(k_tok[:, :], 6, 0, "k_tp", "k_tok")
                token_rows(u_tok[:, 0, :], 7, P, "u0_tp", "u0_tok")
                tanh(0, "y0", "tanh0")
                tanh_sq(0, "tanh0", "t2_0")
                hidden(1, "z1_done", "u1_ready", "z1_kept")
                turned(2, 6, "w21_tp", "w21_d")
                token_rows(h1_tok[:, :], 7, 0, "h1_tp", "h1_tok")
                tanh(1, "y1", "tanh1")
                tanh_sq(1, "tanh1", "t2_1")
                token_rows(u_tok[:, 1, :], 7, P, "u1_tp", "u1_tok")
                turned(0, 6, "w20_tp", "w20_d")
                act.wait_ge(sem("dz1_tp"), t + 1)
                act.activation(dz_tok[:, 1:3, :], ps[:, 6, 2 * P:4 * P].rearrange("p (s n) -> p s n", s=2), ACT.Copy)\
                   .then_inc(sem("dz1_tok"), 1)

            act.wait_ge(sem("wm_tp"), 1)
            act.activation(w10m[:, :], ps[:, 6, 0:E1], ACT.Copy, scale=1.0 / B).then_inc(sem("wm_ready"), 1)
            for i in range(2):
                for n in range(4):
                    act.wait_ge(sem("zf_done"), 4 * i + n + 1)
                    act.activation(uf[:, n * BANK:(n + 1) * BANK], ps[:, UP_BANKS[i][n], :], ACT.Gelu_apprx_tanh).then_inc(sem("uf_ready"), 1)
                if i == 0:
                    act.wait_ge(sem("wm_tp"), 2)
                    act.activation(w11m[:, :], ps[:, 6, 0:E1], ACT.Copy).then_inc(sem("wm_ready"), 1)

            act.wait_ge(sem("nvar"), 2)
            act.activation(nsm[:, 2, :], nsm[:, 1, :], ACT.Sqrt, bias=cst("eps")).then_inc(sem("nstd"), 1)
            act.wait_ge(sem("aqkv_done"), 1)
            act.activation(aq[:, :], psf[:, 0:2 * BANK], ACT.Copy).then_inc(sem("aq_ready"), 1)
            act.wait_ge(sem("pool_set"), POOL_SET["kv"])
            act.wait_ge(sem("aqkv_done"), 3)
            act.activation(vpad[:, :, 3:3 + H, 3:3 + W], bhw(psf[:, 4 * BANK:6 * BANK], J), ACT.Copy).then_inc(sem("av_ready"), 1)
            act.wait_ge(sem("sub_ready"), 1)
            def spread_heads(n, src, func, scale):
                if n >= 2:
                    act.wait_ge(sem("att_tp"), n - 1)
                act.activation(attx[n % 2][:, :].rearrange("p (h d) -> p h d", d=C // NHD),
                               src.unsqueeze(2).broadcast_to([P, P, C // NHD]), func, scale=scale).then_inc(sem("attx_ready"), 1)

            dph_scale = float((C // NHD) ** -0.5)
            for n in range(NK):
                spread_heads(n, att[:, n, :], ACT.Exp, dph_scale)
                if n == 1:
                    act.wait_ge(sem("sub_ready"), 2)
                    act.activation(ex, att[:, :, :].rearrange("p k n -> p (k n)"), ACT.Exp, scale=dph_scale).then_inc(sem("exp_done"), 1)
            act.wait_ge(sem("att_ready"), 1)
            spread_heads(NK, rs[:, :], ACT.Copy, 1.0)

            act.wait_ge(sem("nvar"), 3)
            act.activation(nsm[:, 2, :], nsm[:, 1, :], ACT.Sqrt, bias=cst("eps")).then_inc(sem("nstd"), 1)
            act.preload_act_table_set("sigmoid_and_others")
            act.wait_ge(sem("pool_set"), POOL_SET["scan"])
            for n in range(4):
                act.wait_ge(sem("feat_done"), 2 * n + 1)
                act.activation(seq_w(lam, 2 * n, 2 * n + 2), bhw(ps[:, n, :], 2), ACT.Sigmoid, bias=par("scan_b")[:, 0:1])\
                   .then_inc(sem("lam_ready"), 1)
                if n == 0:
                    act.wait_ge(sem("cm_ready"), 1)
                act.wait_ge(sem("feat_done"), 2 * n + 2)
                act.activation(sig_i[:, n * BANK:(n + 1) * BANK], ps[:, 4 + n, :], ACT.Sigmoid, bias=par("scan_b")[:, 1:2])\
                   .then_inc(sem("sig_ready"), 1)
                act.activation(rest[:, n * BANK:(n + 1) * BANK], ps[:, n, :], ACT.Sigmoid, scale=-1.0, bias=forget_neg[:, :])\
                   .then_inc(sem("lam_ready"), 1)
                act.activation(seq_b(lam_b, n), bhw(ps[:, n, :], 2), ACT.Sigmoid, bias=par("scan_b")[:, 0:1])\
                   .then_inc(sem("lam_b"), 1)
            for n in range(4):
                act.wait_ge(sem("inp_ready"), n + 1)
                act.activation(seq_b(inp_b, n), seq_w(inp, 2 * n, 2 * n + 2), ACT.Copy).then_inc(sem("inp_b"), 1)
            for n in range(4):
                act.wait_ge(sem("feat_done"), 8 + n + 1)
                act.activation(og[:, n * BANK:(n + 1) * BANK], ps[:, n, :], ACT.Sigmoid, bias=par("scan_b")[:, 2:3])\
                   .then_inc(sem("og_ready"), 1)
            act.preload_act_table_set("sqrt_and_others")
            def root(q):
                act.wait_ge(sem("yvar"), 2 * q + 2)
                act.activation(yv[:, q * B:(q + 1) * B], yv[:, q * B:(q + 1) * B], ACT.Sqrt, scale=1.0 / C, bias=cst("eps"))\
                   .then_inc(sem("ystd"), 1)

            for n in range(4):
                if n == 3:
                    root(0)
                act.wait_ge(sem("out_mm"), n + 1)
                act.activation(ysq[:, n * 4 * C:(n + 1) * 4 * C].rearrange("p (i c) -> p i c", c=C),
                               ps[:, n, :].rearrange("p (i c) -> p i c", c=2 * C)[:, :, 0:C], ACT.Square).then_inc(sem("ysq"), 1)
            root(1)

        @block.vector
        def _(dve):
            linked = [0]

            def link(ins):
                linked[0] += 1
                ins.then_inc(sem("dve_link"), 1)
                dve.wait_ge(sem("dve_link"), linked[0])

            dve.wait_ge(sem("gsum0"), 1)
            dve.tensor_reduce(gst[:, 0, :], ps[:, 0, :].rearrange("p (g k) -> p g k", k=2), AX_X, ALU.add)
            link(dve.tensor_reduce(gst[:, 1, :], ps[:, 1, :].rearrange("p (g k) -> p g k", k=2), AX_X, ALU.add))
            link(dve.tensor_tensor(gst[:, 2, :], gst[:, 0, :], gst[:, 0, :], ALU.mult))
            dve.tensor_tensor(gst[:, 2, :], gst[:, 1, :], gst[:, 2, :], ALU.subtract).then_inc(sem("gvar0"), 1)

            def group_cols(row):
                return gst[:, row, :].rearrange("p (b g) -> p b g", b=B).unsqueeze(3).broadcast_to([P, B, C // 2, 2])

            def inner(q):
                return xpad[:, q, :, 1:C + 1].rearrange("p b (g k) -> p b g k", k=2)

            dve.wait_ge(sem("pool_set"), POOL_SET["xpad"])
            for q in range(2):
                dve.tensor_tensor(inner(q), xs[:, q, :].rearrange("p (b g k) -> p b g k", b=B, k=2), group_cols(0), ALU.subtract)
            dve.wait_ge(sem("gstd0"), 1)
            link(dve.reciprocal(gst[:, 3, :], gst[:, 3, :]))
            for q in range(2):
                dve.tensor_tensor(inner(q), inner(q), group_cols(3), ALU.mult).then_inc(sem("xpad_ready"), 1)

            dve.wait_ge(sem("param_in"), 16)
            for m in range(2):
                dve.wait_ge(sem("conv_done"), m + 1)
                link(dve.bn_stats(cstat[:, m, :], ps[:, m, :]))
                link(dve.bn_aggr(cmv[:, m, :], cstat[:, m, :]))
            mean, var = cmv[:, :, 0], cmv[:, :, 1]
            link(dve.tensor_tensor(csum[:, 0, :], mean, par("conv_bias"), ALU.add))
            link(dve.tensor_tensor(csum[:, 1, :], csum[:, 0, :], csum[:, 0, :], ALU.mult))
            dve.tensor_tensor(csum[:, 1, :], csum[:, 1, :], var, ALU.add).then_inc(sem("csum"), 1)
            dve.wait_ge(sem("cgroup"), 1)
            link(dve.tensor_copy(csm[:, 0:2, :], ps[:, 2, 0:4].rearrange("p (s m) -> p s m", s=2)))
            link(dve.tensor_tensor(csm[:, 3, :], csm[:, 0, :], csm[:, 0, :], ALU.mult))
            dve.tensor_tensor(csm[:, 1, :], csm[:, 1, :], csm[:, 3, :], ALU.subtract).then_inc(sem("cvar"), 1)
            dve.wait_ge(sem("cstd"), 1)
            link(dve.reciprocal(csm[:, 2, :], csm[:, 2, :]))
            link(dve.tensor_tensor(csm[:, 4, :], csm[:, 2, :], par("conv_gamma"), ALU.mult))
            link(dve.tensor_tensor(csm[:, 3, :], par("conv_bias"), csm[:, 0, :], ALU.subtract))
            link(dve.tensor_tensor(csm[:, 3, :], csm[:, 3, :], csm[:, 4, :], ALU.mult))
            link(dve.tensor_tensor(csm[:, 5, :], csm[:, 3, :], par("conv_beta"), ALU.add))
            dve.tensor_scalar(alpha_n[:, :], par("conv_alpha"), -1.0, None, ALU.mult)
            dve.tensor_scalar(csm[:, 6:8, :], csm[:, 4:6, :], -1.0, None, ALU.mult).then_inc(sem("caff"), 1)
            for m in range(2):
                dve.wait_ge(sem("relu"), m + 1)
                link(dve.tensor_tensor(xs[:, m, :], xs[:, m, :], relu_p[:, m, :], ALU.add))
                dve.scalar_tensor_tensor(xs[:, m, :], relu_n[:, m, :], alpha_n[:, 0:1], xs[:, m, :], ALU.mult, ALU.add)\
                   .then_inc(sem("x1_rows"), 1)

            def group_norm(n):
                for j in range(J):
                    if n == 0 and j % 2 == 0:
                        dve.wait_ge(sem("x1_ready"), j // 2 + 1)
                    dve.bn_stats(nst[:, j, :], xc[:, j * HW:(j + 1) * HW]).then_inc(sem("bn_part"), 1)
                dve.wait_ge(sem("bn_part"), J * (n + 1))
                for j in range(J):
                    last = dve.bn_aggr(nmv[:, j, :], nst[:, j, :])
                link(last)
                link(dve.tensor_tensor(nsm[:, 4, :], nmv[:, :, 0], nmv[:, :, 0], ALU.mult))
                dve.tensor_copy(nsm[:, 6, :], nmv[:, :, 0])
                dve.tensor_tensor(nsm[:, 7, :], nsm[:, 4, :], nmv[:, :, 1], ALU.add).then_inc(sem("npart"), 1)
                dve.wait_ge(sem("ngroup"), n + 1)
                link(dve.tensor_copy(nsm[:, 0:2, :], ps[:, NORM_BANK[n], 0:2 * J].rearrange("p (s j) -> p s j", s=2)))
                link(dve.tensor_tensor(nsm[:, 3, :], nsm[:, 0, :], nsm[:, 0, :], ALU.mult))
                dve.tensor_tensor(nsm[:, 1, :], nsm[:, 1, :], nsm[:, 3, :], ALU.subtract).then_inc(sem("nvar"), 1)
                dve.wait_ge(sem("nstd"), n + 1)
                link(dve.reciprocal(nsm[:, 5, :], nsm[:, 2, :]))
                for j in range(J):
                    dve.tensor_scalar(xn[:, j * HW:(j + 1) * HW], xc[:, j * HW:(j + 1) * HW], nsm[:, 0, j:j + 1],
                                      nsm[:, 5, j:j + 1], ALU.subtract, ALU.mult).then_inc(sem("xn_ready"), 1)

            group_norm(0)
            for m, new, buf in ((0, "w20_new", we), (1, "w11_new", we), (2, "q_21", qe)):
                dve.tensor_copy(buf[:, m, :].rearrange("p (b d) -> p b d", b=8),
                                par("mats_e")[:, m * C:(m + 1) * C].unsqueeze(1).broadcast_to([P, 8, C])).then_inc(sem(new), 1)
            dve.tensor_copy(w10[:, :].rearrange("p (j e) -> p j e", j=J), par("w1_0").unsqueeze(1).broadcast_to([P, J, E1]))\
               .then_inc(sem("w10_new"), 1)
            dve.wait_ge(sem("gate_sig"), 1)
            link(dve.tensor_reduce(gsum[:, :], gates[:, :].rearrange("p (n w) -> p n w", w=W), AX_X, ALU.add))
            dve.tensor_scalar(vals[:, :], gsum[:, :], cst("gate_scale", 6)[:, 0:1], cst("gate_scale", 6)[:, 1:2], ALU.mult, ALU.add)\
               .then_inc(sem("vals"), 1)
            dve.wait_ge(sem("kq_norm"), 1)
            link(dve.tensor_scalar(k_inv[:, :], k_inv[:, :], 1e-12, None, ALU.max))
            link(dve.reciprocal(k_inv[:, :], k_inv[:, :]))
            dve.tensor_copy(nrm[:, :].rearrange("p (n c) -> p n c", c=C),
                            k_inv[:, :].unsqueeze(2).broadcast_to([P, 2 * J * BH, C])).then_inc(sem("k_spread"), 1)
            dve.wait_ge(sem("pool_set"), POOL_SET["bd"] - 2)
            dve.wait_ge(sem("kraw"), 1)
            dve.wait_ge(sem("inv_tp"), 1)
            for b2 in range(BH):
                s = slice(64 * b2, 64 * b2 + 64)
                last = dve.tensor_tensor(kbd[:, :].rearrange("p (t j g w) -> p g t j w", t=NS, j=J, g=BH)[s, b2],
                                         kraw[s, :].rearrange("p (j t w) -> p t j w", j=J, t=NS),
                                         psf[s, 2 * BANK:4 * BANK].rearrange("p (j t w) -> p t j w", j=J, t=NS), ALU.mult)
            last.then_inc(sem("kbd_ready"), 1)
            dve.wait_ge(sem("coef_ps"), 1)
            for i, buf in ((0, eta_e), (1, keep_e)):
                dve.tensor_copy(buf[:, :].rearrange("p (t j g) -> p g j t", t=NS, j=J),
                                ps[:, 1, 128 * i:128 * i + 128].rearrange("p (g j t) -> p g j t", g=BH, j=J))
            for i, buf in ((0, eta_d), (1, keep_d)):
                dve.tensor_copy(buf[:, :].rearrange("p (t j) -> p j t", t=NS),
                                ps[:, 1, 256 + 64 * i:320 + 64 * i].rearrange("p (j t) -> p j t", j=J))
            dve.tensor_copy(lrn[:, :], ps[:, 1, 384:384 + NS])
            dve.tensor_scalar(lrh[:, :], ps[:, 1, 384:384 + NS], 0.5, None, ALU.mult).then_inc(sem("coef_ready"), 1)
            dve.wait_ge(sem("kq_norm"), 2)
            link(dve.tensor_scalar(q_inv[:, :], q_inv[:, :], 1e-12, None, ALU.max))
            link(dve.reciprocal(q_inv[:, :], q_inv[:, :]))
            dve.tensor_copy(hf[:, :].rearrange("p (n c) -> p n c", c=C),
                            q_inv[:, :].unsqueeze(2).broadcast_to([P, 2 * J * BH, C])).then_inc(sem("q_spread"), 1)
            dve.wait_ge(sem("m_zero"), 3)
            dve.wait_ge(sem("g10"), 1)
            dve.wait_ge(sem("coef_ready"), 1)

            with dve.Fori(0, NS) as t:
                def mom_scale(m):
                    if m < 3:
                        v = ps[:, m, :].rearrange("p (b d) -> p b d", b=8)
                        dve.tensor_tensor(v, v, eta_e[:, bass.ts(t, 8)].unsqueeze(2).broadcast_to([P, 8, C]), ALU.mult)\
                           .then_inc(sem("scaled"), 1)
                    else:
                        v = ps[:, 3, :].rearrange("p (j e) -> p j e", j=J)
                        dve.tensor_tensor(v, v, eta_d[:, bass.ts(t, J)].unsqueeze(2).broadcast_to([P, J, E1]), ALU.mult)\
                           .then_inc(sem("scaled"), 1)

                def arg(i, kept, y):
                    dve.wait_ge(sem(kept), t + 1)
                    dve.scalar_tensor_tensor(z_y[:, i, :], z_sq[:, i, :], 1.0 / GC, z_cp[:, i, :], ALU.add, ALU.mult)\
                       .then_inc(sem(y), 1)

                def slope_1(i, t2):
                    dve.wait_ge(sem(t2), t + 1)
                    dve.scalar_tensor_tensor(z_s1[:, i, :], z_t2[:, i, :], -1.0, z_cp[:, i, :], ALU.add, ALU.mult).then_inc(sem("slope"), 1)

                def slope_2(i):
                    dve.wait_ge(sem("slope"), 6 * t + 3 * i + 1)
                    dve.scalar_tensor_tensor(z_s2[:, i, :], z_sq[:, i, :], 1.0 / (3.0 * GC), z_s1[:, i, :], ALU.add, ALU.mult)\
                       .then_inc(sem("slope"), 1)

                def slope_3(i):
                    dve.wait_ge(sem("slope"), 6 * t + 3 * i + 2)
                    dve.scalar_tensor_tensor(z_g[:, i, :], z_s2[:, i, :], -3.0 * GC * GS, z_t[:, i, :], ALU.mult, ALU.add)\
                       .then_inc(sem("slope"), 1)

                def by_pair(out, col, tp, done, scale):
                    dve.wait_ge(sem(tp), t + 1)
                    dve.scalar_tensor_tensor(out[:, :].rearrange("p (j n) -> p j n", j=J),
                                             ps[:, 7, col:col + P].unsqueeze(1).broadcast_to([P, J, P]), scale,
                                             cst("block_j").unsqueeze(2).broadcast_to([P, J, P]), ALU.mult, ALU.mult)\
                       .then_inc(sem(done), 1)

                def updated(m, grad, q, done):
                    dve.wait_ge(sem(grad), t + (1 if m < 3 else 2))
                    dve.wait_ge(sem(q), t + 1)
                    if m < 3:
                        dve.tensor_tensor(we[:, m, :], ps[:, m, :], qe[:, m, :], ALU.add).then_inc(sem(done), 1)
                    else:
                        dve.tensor_tensor(w10[:, :], ps[:, 3, :], q10[:, :], ALU.add).then_inc(sem(done), 1)

                mom_scale(1)
                dve.wait_ge(sem("h1_ps"), t + 1)
                dve.tensor_tensor(h1bd[:, :], ps[:, 5, 0:P], cst("own_half"), ALU.mult).then_inc(sem("h1_ready"), 1)
                arg(0, "z0_kept", "y0")
                updated(2, "g21", "q_21", "w21_new")
                mom_scale(2)
                slope_1(0, "t2_0")
                arg(1, "z1_kept", "y1")
                slope_2(0)
                slope_3(0)
                dve.wait_ge(sem("h2_ps"), t + 1)
                dve.tensor_tensor(rbd[:, :], ps[:, 5, P:2 * P], cst("own_half"), ALU.mult).then_inc(sem("r_ready"), 1)
                slope_1(1, "t2_1")
                slope_2(1)
                slope_3(1)
                dve.wait_ge(sem("slope"), 6 * t + 6)
                dve.wait_ge(sem("du1_done"), t + 1)
                dve.scalar_tensor_tensor(dz1[:, :], z_g[:, 1, :], 1.0, ps[:, 4, 2 * P:3 * P], ALU.add, ALU.mult).then_inc(sem("dz1_ready"), 1)
                by_pair(r_fbd, 2 * P, "r_tp", "r_fbd", lrn[:, bass.ds(t, 1)])
                dve.wait_ge(sem("dh1_ps"), t + 1)
                dve.scalar_tensor_tensor(dhbd[:, :], ps[:, 5, 2 * P:3 * P], 0.5, cst("own_half"), ALU.mult, ALU.mult)\
                   .then_inc(sem("dh1_ready"), 1)
                mom_scale(3)
                dve.wait_ge(sem("dz1_tok"), t + 1)
                dve.wait_ge(sem("du0_done"), t + 1)
                dve.scalar_tensor_tensor(dz_tok[:, 0, :], dz_tok[:, 2, :], 1.0, ps[:, 4, 3 * P:4 * P], ALU.add, ALU.mult)\
                   .then_inc(sem("dz0_ready"), 1)
                by_pair(dh_fbd, 3 * P, "dh1_tp", "dh_fbd", lrn[:, bass.ds(t, 1)])
                mom_scale(0)
                updated(3, "g10", "q_10", "w10_new")
                updated(1, "g11", "q_11", "w11_new")
                updated(0, "g20", "q_20", "w20_new")

            dve.wait_ge(sem("qraw"), 1)
            dve.wait_ge(sem("inv_tp"), 2)
            dve.tensor_tensor(qt[:, :], qraw[:, :], psf[:, 4 * BANK:6 * BANK], ALU.mult).then_inc(sem("qt_ready"), 1)
            dve.wait_ge(sem("w11_new"), NS + 1)
            dve.wait_ge(sem("w20_new"), NS + 1)
            link(dve.tensor_reduce(wms[:, 0:2, :], we[:, 0:2, :].rearrange("p m (b d) -> p m d b", b=8), AX_X, ALU.add))
            dve.tensor_scalar(w11s[:, :, :], wms[:, 1, :].unsqueeze(1).broadcast_to([P, 2, C]), 1.0 / B, None, ALU.mult)
            dve.tensor_scalar(wme[:, 0, :], wms[:, 0, :], 1.0 / B, None, ALU.mult).then_inc(sem("wm_sum"), 1)
            dve.wait_ge(sem("g21"), NS + 1)
            dve.wait_ge(sem("q_21"), NS + 1)
            link(dve.tensor_tensor(we[:, 2, :], ps[:, 2, :], qe[:, 2, :], ALU.add))
            link(dve.tensor_reduce(wms[:, 2, :], we[:, 2, :].rearrange("p (b d) -> p d b", b=8), AX_X, ALU.add))
            dve.tensor_scalar(wme[:, 2, :], wms[:, 2, :], 1.0 / B, None, ALU.mult).then_inc(sem("wm_sum"), 1)
            dve.wait_ge(sem("hf_done"), 1)
            dve.tensor_tensor(hf[:, :], psf[:, 4 * BANK:6 * BANK], qt[:, :], ALU.add).then_inc(sem("hf_ready"), 1)
            dve.wait_ge(sem("hf_ready"), 1)
            link(dve.tensor_tensor(xh[:, :], xc[:, :], hf[:, :], ALU.add))
            dve.wait_ge(sem("hf_done"), 2)
            link(dve.tensor_tensor(xc[:, :], psf[:, 6 * BANK:8 * BANK], xh[:, :], ALU.add))
            group_norm(1)

            dve.tensor_scalar(wout[0:C, :], par("out_w")[0:C, 0:C], par("ln_gamma")[0:C], None, ALU.mult).then_inc(sem("wout"), 1)
            dve.wait_ge(sem("pool_set"), POOL_SET["kv"] - 1)
            dve.wait_ge(sem("aqkv_done"), 2)
            dve.tensor_copy(kpad[:, :, 3:3 + H, 3:3 + W], bhw(psf[:, 2 * BANK:4 * BANK], J)).then_inc(sem("ak_ready"), 1)
            dve.wait_ge(sem("ak_ready"), 1)
            dve.wait_ge(sem("aq_ready"), 1)

            def gate_chunk(wc):
                n = W // NWC
                dve.wait_ge(sem("og_ready"), 4)
                dve.wait_ge(sem("sum_done"), wc + 1)
                dve.tensor_tensor(bhw(tot)[:, :, :, wc * n:(wc + 1) * n],
                                  ps[:, 4 + wc, :].rearrange("p (b w h) -> p b h w", b=B, w=n),
                                  bhw(og[:, :])[:, :, :, wc * n:(wc + 1) * n], ALU.mult).then_inc(sem("tot_ready"), 1)

            def head_sums(n):
                dve.wait_ge(sem("qk_tp"), n + 1)
                dve.tensor_reduce(att[:, n, :], psf[:, (n % 2) * 2 * BANK:(n % 2 + 1) * 2 * BANK].rearrange("p (n d) -> p n d", d=C // NHD),
                                  AX_X, ALU.add).then_inc(sem("score_done"), 1)

            for n in range(NK):
                if n % 2 == 0:
                    if n >= 4:
                        dve.wait_ge(sem("qk_tp"), n - 3)
                    dve.tensor_tensor(bhw(prod[n % 4], J), bhw(aq[:, :], J), shifted(kpad, n), ALU.mult).then_inc(sem("qk_dve"), 1)
                if n >= 2:
                    head_sums(n - 2)
            head_sums(NK - 2)
            head_sums(NK - 1)
            dve.wait_ge(sem("score_done"), NK)
            link(dve.tensor_reduce(mx[:, :], att[:, :, :].rearrange("p k n -> p n k"), AX_X, ALU.max))
            for first, end in ((0, 2), (2, NK)):
                dve.tensor_tensor(att[:, first:end, :], att[:, first:end, :],
                                  mx[:, :].unsqueeze(1).broadcast_to([P, end - first, P]), ALU.subtract).then_inc(sem("sub_ready"), 1)
            dve.wait_ge(sem("av_ready"), 1)

            def att_cols_of(n):
                return psf[:, n % 3 * 2 * BANK:(n % 3 + 1) * 2 * BANK]

            def times_v(n):
                dve.wait_ge(sem("att_tp"), n + 1)
                if n >= 5 and n % 2:
                    dve.wait_ge(sem("odd_sum"), n // 2 - 1)
                if n >= 6 and n % 2 == 0:
                    dve.wait_ge(sem("even_sum"), n // 2 - 2)
                out = prod[1 + n // 2 % 2] if n % 2 else acc if n == 2 else prod[3] if n else prod[0]
                dve.tensor_tensor(bhw(out, J), bhw(att_cols_of(n), J), shifted(vpad, n), ALU.mult).then_inc(sem("pv_ready"), 1)

            def add_even(n):
                dve.wait_ge(sem("pv_ready"), n + 1)
                if n > 4:
                    dve.wait_ge(sem("even_sum"), n // 2 - 2)
                dve.tensor_tensor(acc[:, :], acc[:, :], prod[3], ALU.add).then_inc(sem("even_sum"), 1)

            for n in range(NK):
                times_v(n)
                if n == 1:
                    dve.wait_ge(sem("exp_done"), 1)
                    link(dve.tensor_reduce(rs[:, :], ex.rearrange("p (k n) -> p n k", k=NK), AX_X, ALU.add))
                    dve.reciprocal(rs[:, :], rs[:, :]).then_inc(sem("att_ready"), 1)
                if n in (5, 7):
                    add_even(n - 1)
            add_even(NK - 1)
            dve.wait_ge(sem("even_sum"), 3)
            dve.wait_ge(sem("odd_sum"), NK // 2)
            link(dve.tensor_tensor(acc[:, :], acc[:, :], prod[0], ALU.add))
            dve.wait_ge(sem("att_tp"), NK + 1)
            link(dve.tensor_tensor(acc[:, :], acc[:, :], att_cols_of(NK), ALU.mult))
            dve.tensor_tensor(xc[:, :], acc[:, :], xc[:, :], ALU.add).then_inc(sem("x3_ready"), 1)
            dve.wait_ge(sem("x3_ready"), 1)
            group_norm(2)

            dve.wait_ge(sem("xrow_tp"), 1)
            dve.tensor_scalar(forget_neg[:, :], par("scan_b")[:, 0:1], -1.0, None, ALU.mult)
            dve.tensor_copy(cm[:, 0:C], cst("center"))
            dve.tensor_copy(cm[:, C:2 * C], ps[:, 4, 0:C])
            dve.tensor_copy(bout[:, :], ps[:, 4, C:2 * C]).then_inc(sem("cm_ready"), 1)
            dve.wait_ge(sem("cm_ready"), 1)
            dve.tensor_tensor(xrow[:, :, :, :].rearrange("p q j (g c) -> p (q j g) c", c=C),
                              psf[:, 6 * BANK:8 * BANK].rearrange("p (n c) -> p n c", c=C),
                              bout[:, :].unsqueeze(1).broadcast_to([P, 16, C]), ALU.add).then_inc(sem("xrow_ready"), 1)
            def silu_chunk(n):
                cols = slice(n * BANK, (n + 1) * BANK)
                dve.wait_ge(sem("sig_ready"), n + 1)
                dve.scalar_tensor_tensor(silu[:, cols], ps[:, 4 + n, :], par("scan_b")[:, 1:2], sig_i[:, cols], ALU.add, ALU.mult)\
                   .then_inc(sem("silu"), 1)

            def scan_along_h(n):
                rows = slice(2 * n * ROW, 2 * (n + 1) * ROW)
                dve.wait_ge(sem("lam_ready"), 2 * n + 1)
                dve.wait_ge(sem("inp_ready"), n + 1)
                dve.tensor_tensor_scan(sw[:, rows], lam[:, rows], inp[:, rows], 0.0, ALU.mult, ALU.add)
                dve.tensor_tensor_scan(rw[:, rows][:, ::-1], lam[:, rows][:, ::-1], inp[:, rows][:, ::-1], 0.0, ALU.mult, ALU.add)\
                   .then_inc(sem("scan_w"), 1)

            for n in range(4):
                silu_chunk(n)
                if n:
                    scan_along_h(n - 1)
            scan_along_h(3)
            dve.wait_ge(sem("lam_b"), 4)
            dve.wait_ge(sem("inp_b"), 4)
            for wc in range(NWC):
                f, r, la, x = (seqs_b(buf, wc) for buf in (fb, rb, lam_b, inp_b))
                dve.tensor_tensor_scan(f, la, x, 0.0, ALU.mult, ALU.add)
                dve.tensor_tensor_scan(r[:, ::-1], la[:, ::-1], x[:, ::-1], 0.0, ALU.mult, ALU.add).then_inc(sem("scan_b"), 1)
            dve.wait_ge(sem("scan_b"), NWC)
            for wc in range(NWC - 2, NWC):
                dve.tensor_tensor(seqs_b(fb, wc), seqs_b(fb, wc), seqs_b(rb, wc), ALU.add).then_inc(sem("sb_ready"), 1)
            for wc in range(NWC):
                gate_chunk(wc)
            for q in range(2):
                for n in (2 * q, 2 * q + 1):
                    dve.wait_ge(sem("ysq"), n + 1)
                    dve.tensor_reduce(yv[:, 4 * n:4 * n + 4], ysq[:, n * 4 * C:(n + 1) * 4 * C].rearrange("p (i c) -> p i c", c=C),
                                      AX_X, ALU.add).then_inc(sem("yvar"), 1)
                dve.wait_ge(sem("ystd"), q + 1)
                link(dve.reciprocal(yv[:, q * B:(q + 1) * B], yv[:, q * B:(q + 1) * B]))
                o = xo[:, q, :, :].rearrange("p j (g c) -> p g j c", g=BH)
                pr = psf[:, 2 * q * BANK:(2 * q + 2) * BANK].rearrange("p (g j s c) -> p s g j c", g=BH, j=J, s=2)[:, 1]
                rstd = yv[:, q * B:(q + 1) * B].rearrange("p (g j) -> p g j", g=BH).unsqueeze(3).broadcast_to([P, BH, J, C])
                dve.tensor_tensor(o, pr, rstd, ALU.mult).then_inc(sem("scaled_out"), 1)
            dve.wait_ge(sem("scaled_out"), 2)
            dve.tensor_tensor(xo[:, 1], xo[:, 1], xrow[:, 1], ALU.add).then_inc(sem("xo_last"), 1)

        @block.tensor
        def _(pe):
            def keep_warm(bank, n):
                for _ in range(n):
                    pe.matmul(ps[:, bank, :], zero_bf[:, 0:P], zero_bf[:, :], start=True, stop=True)

            pe.wait_ge(sem("pool_set"), POOL_SET["zero"])
            keep_warm(0, 7)
            pe.wait_ge(sem("pool_set"), POOL_SET["inv512"])
            pe.wait_ge(sem("x_in"), 16)
            for q in range(2):
                pe.matmul(ps[:, 0, :], inv512[:, :], xs[:, q, :], start=(q == 0), stop=(q == 1))
            pe.wait_ge(sem("sq0"), 1)
            for q in range(2):
                mm = pe.matmul(ps[:, 1, :], inv512[:, :], sq[:, q, :], start=(q == 0), stop=(q == 1))
            mm.then_inc(sem("gsum0"), 1)
            keep_warm(2, 16)
            pe.wait_ge(sem("band_in"), 16)
            pe.wait_ge(sem("const_in"), 16)
            for m in range(2):
                for q in range(2):
                    pe.wait_ge(sem("xpad_ready"), q + 1)
                    for d in range(3):
                        mm = pe.matmul(ps[:, m, :], bandv[:, q, d, m, :], xpad[:, q, :, d:d + C],
                                       start=(q == 0 and d == 0), stop=(q == 1 and d == 2))
                mm.then_inc(sem("conv_done"), 1)
            keep_warm(4, 7)
            pe.wait_ge(sem("csum"), 1)
            pe.matmul(ps[:, 2, 0:4], cst("sum16"), csum[:, :, :].rearrange("p s m -> p (s m)"), start=True, stop=True)\
              .then_inc(sem("cgroup"), 1)
            keep_warm(4, 18)
            pe.wait_ge(sem("caff"), 1)
            for q in range(2):
                pe.wait_ge(sem("x1_rows"), q + 1)
                for j in range(J):
                    col = 2 * BANK + j * HW + q * P
                    mm = pe.transpose(psf[:, col:col + P], xs[:, q, j * P:(j + 1) * P], ident)
            mm.then_inc(sem("x1_tp"), 1)
            keep_warm(0, 8)

            def norm_group(n):
                pe.wait_ge(sem("npart"), n + 1)
                pe.matmul(ps[:, NORM_BANK[n], 0:2 * J], cst("pair_half"), nsm[:, 6:8, :].rearrange("p s j -> p (s j)"), start=True, stop=True)\
                  .then_inc(sem("ngroup"), 1)

            norm_group(0)
            keep_warm(0, 6)
            pe.wait_ge(sem("param_in"), 16)
            pe.wait_ge(sem("xn_ready"), J)

            def project(bank, w, src):
                for n in range(2):
                    mm = pe.matmul(ps[:, bank + n, :], w, src[:, n * BANK:(n + 1) * BANK], start=True, stop=True)
                return mm

            for n in range(2):
                mm = pe.matmul(ps[0:6, n, :], par("gates"), xn[:, n * BANK:(n + 1) * BANK], start=True, stop=True)
            mm.then_inc(sem("gate_done"), 1)
            project(2, par("wk"), xn).then_inc(sem("kq_done"), 1)
            project(4, par("wq"), xn).then_inc(sem("kq_done"), 1)
            pe.wait_ge(sem("gate_sig"), 1)

            def square_sums(col):
                for i in range(2 * J):
                    mm = pe.matmul(ps[:, 0, col + BH * i:col + BH * i + BH], sq[:, i // J, (i % J) * P:(i % J + 1) * P],
                                   cst("ones64")[:, 0:P:64], start=True, stop=True)
                return mm

            def turn_all(at, src):
                for i in range(2 * J):
                    mm = pe.transpose(psf[:, at * BANK + i * P:at * BANK + (i + 1) * P], src[:, i * P:(i + 1) * P], ident)
                return mm

            pe.wait_ge(sem("kq_sq"), 1)
            square_sums(0).then_inc(sem("kq_sum"), 1)
            project(6, par("wv"), xn).then_inc(sem("v_done"), 1)
            pe.wait_ge(sem("kraw"), 1)
            pe.wait_ge(sem("k_spread"), 1)
            turn_all(2, nrm).then_inc(sem("inv_tp"), 1)
            keep_warm(1, 6)
            pe.wait_ge(sem("vals"), 1)
            for i, gate in ((0, 2), (1, 1)):
                for b2 in range(BH):
                    r = 3 * b2 + gate
                    pe.matmul(ps[:, 1, 128 * i + 64 * b2:128 * i + 64 * b2 + 64], const[0:6, r:r + 1].broadcast_to([6, P]),
                              vals[:, :], start=True, stop=True)
                pe.matmul(ps[:, 1, 256 + 64 * i:320 + 64 * i], cst("half_sel", 6)[:, i * P:(i + 1) * P], vals[:, :], start=True, stop=True)
            for j in range(J):
                mm = pe.matmul(ps[:, 1, 384:384 + NS], cst("tok_sel", 6)[:, j * P:(j + 1) * P], vals[:, j * NS:(j + 1) * NS],
                               start=(j == 0), stop=(j == J - 1))
            mm.then_inc(sem("coef_ps"), 1)
            pe.wait_ge(sem("kq_sq"), 2)
            pe.wait_ge(sem("kq_norm"), 1)
            square_sums(2 * J * BH).then_inc(sem("kq_sum"), 1)
            pe.wait_ge(sem("v_ready"), 2)
            keep_warm(6, 3)
            pe.wait_ge(sem("kbd_ready"), 1)
            for m in (2, 3, 0, 1):
                if m == 0:
                    pe.wait_ge(sem("kq_norm"), 2)
                    pe.wait_ge(sem("coef_ready"), 1)
                pe.matmul(ps[:, m, :], zero_bf[:, 0:P], zero_bf[:, :], start=True, stop=True)\
                  .then_inc(sem("m_zero" if m < 3 else "g10"), 1)
            pe.wait_ge(sem("v_ready"), 2)
            pe.wait_ge(sem("qraw"), 1)
            pe.wait_ge(sem("pool_set"), POOL_SET["bd"])

            with pe.Fori(0, NS) as t:
                def per_pair(bank, col, w, x, start=True):
                    for j in range(J):
                        mm = pe.matmul(ps[:, bank, col + 32 * j:col + 32 * j + 32], w[:, P * j:P * j + P],
                                       x[:, 32 * j:32 * j + 32], start=start, stop=True, skip_group_check=not start)
                    return mm

                def begin(col, scale, x):
                    pe.matmul(ps[:, 5, col:col + P], cst(scale), x, start=True, stop=False, skip_group_check=True)

                def turn(bank, col, x):
                    return pe.transpose(ps[:, bank, col:col + P], x, ident)

                def turn_weights(bank, m):
                    for j in range(J):
                        mm = turn(bank, P * j, we[:, m, P * j:P * j + P])
                    return mm

                def gradient(m, left, right, half):
                    cols = slice(half * BANK // 2, (half + 1) * BANK // 2)
                    return pe.matmul(ps[:, m, cols], left, right[:, cols], start=False, stop=False, skip_group_check=True)

                pe.wait_ge(sem("w10_new"), t + 1)
                for j in range(J):
                    mm = pe.matmul(ps[:, 4, 32 * j:32 * j + 32], w10[:, P * j:P * j + P], kbd[:, bass.ds(t * P + 32 * j, 32)],
                                   start=True, stop=True)
                mm.then_inc(sem("z0_done"), 1)

                pe.wait_ge(sem("w11_new"), t + 1)
                turn_weights(7, 1).then_inc(sem("w11_tp"), 1)
                begin(0, "ident", kbd[:, bass.ts(t, P)])
                pe.wait_ge(sem("w20_new"), t + 1)
                pe.wait_ge(sem("u0_ready"), t + 1)
                per_pair(5, 0, we[:, 0, :], act_u[:, 0, :], start=False).then_inc(sem("h1_ps"), 1)
                pe.wait_ge(sem("k_now"), t + 1)
                turn(6, 0, k_now[:, :]).then_inc(sem("k_tp"), 1)
                gradient(2, u_tok[:, 1, :], r_fbd, 1).then_inc(sem("g21"), 1)
                pe.wait_ge(sem("w11_d"), t + 1)
                turn(7, P, act_u[:, 0, :]).then_inc(sem("u0_tp"), 1)
                pe.wait_ge(sem("z0_kept"), t + 1)

                pe.wait_ge(sem("h1_ready"), t + 1)
                per_pair(4, P, wd[:, 1, :], h1bd).then_inc(sem("z1_done"), 1)
                pe.wait_ge(sem("u0_tok"), t + 1)
                turn(7, 0, h1bd[:, :]).then_inc(sem("h1_tp"), 1)
                pe.wait_ge(sem("k_tok"), t + 1)
                pe.wait_ge(sem("w21_new"), t + 1)
                turn_weights(6, 2).then_inc(sem("w21_tp"), 1)
                pe.wait_ge(sem("h1mv"), t + 1)
                begin(P, "ident", h1mv[:, :])
                pe.wait_ge(sem("u1_ready"), t + 1)
                per_pair(5, P, we[:, 2, :], act_u[:, 1, :], start=False).then_inc(sem("h2_ps"), 1)
                pe.wait_ge(sem("h1_tok"), t + 1)
                turn(7, P, act_u[:, 1, :]).then_inc(sem("u1_tp"), 1)
                pe.wait_ge(sem("w21_d"), t + 1)
                turn_weights(6, 0).then_inc(sem("w20_tp"), 1)
                pe.wait_ge(sem("z1_kept"), t + 1)

                pe.wait_ge(sem("r_ready"), t + 1)
                per_pair(4, 2 * P, wd[:, 2, :], rbd).then_inc(sem("du1_done"), 1)
                pe.wait_ge(sem("u1_tok"), t + 1)
                turn(7, 2 * P, rbd[:, :]).then_inc(sem("r_tp"), 1)

                begin(2 * P, "twice", rbd[:, :])
                pe.wait_ge(sem("dz1_ready"), t + 1)
                per_pair(5, 2 * P, we[:, 1, :], dz1, start=False).then_inc(sem("dh1_ps"), 1)
                pe.wait_ge(sem("w20_d"), t + 1)
                turn(6, 2 * P, dz1[:, :])
                turn(6, 3 * P, z_g[:, 0, :]).then_inc(sem("dz1_tp"), 1)
                pe.wait_ge(sem("scaled"), 4 * t + 2)
                pe.wait_ge(sem("r_fbd"), t + 1)
                gradient(2, u_tok[:, 1, :], r_fbd, 0)
                pe.wait_ge(sem("dh1_ready"), t + 1)
                for j in range(J):
                    mm = pe.matmul(ps[32 * j:32 * j + 32, 4, 3 * P:4 * P], dhbd[:, 32 * j:32 * j + 32], wd[:, 0, P * j:P * j + P],
                                   start=True, stop=True)
                mm.then_inc(sem("du0_done"), 1)
                turn(7, 3 * P, dhbd[:, :]).then_inc(sem("dh1_tp"), 1)
                pe.wait_ge(sem("dz1_tok"), t + 1)
                pe.wait_ge(sem("h1_fbd"), t + 1)
                gradient(1, dz_tok[:, 1, :], h1_fbd, 0)
                pe.wait_ge(sem("scaled"), 4 * t + 3)
                pe.wait_ge(sem("k_fbd"), t + 1)
                pe.wait_ge(sem("dz0_ready"), t + 1)
                for j in range(J):
                    mm = pe.matmul(ps[:, 3, P * j:P * j + P], k_fbd[:, P * j:P * j + P], dz_tok[:, 0, :], start=False, stop=False,
                                   skip_group_check=True)
                mm.then_inc(sem("g10"), 1)
                gradient(1, dz_tok[:, 1, :], h1_fbd, 1).then_inc(sem("g11"), 1)
                pe.wait_ge(sem("scaled"), 4 * t + 4)
                pe.wait_ge(sem("dh_fbd"), t + 1)
                gradient(0, u_tok[:, 0, :], dh_fbd, 0)
                gradient(0, u_tok[:, 0, :], dh_fbd, 1).then_inc(sem("g20"), 1)

            pe.matmul(ps[:, 2, BANK // 2:], u_tok[:, 1, :], r_fbd[:, BANK // 2:], start=False, stop=False,
                      skip_group_check=True).then_inc(sem("g21"), 1)

            pe.wait_ge(sem("w10_new"), NS + 1)
            for j in range(J):
                mm = pe.matmul(ps[:, 6, 0:E1], cst("dup64"), w10[:, j * E1:(j + 1) * E1], start=(j == 0), stop=(j == J - 1))
            mm.then_inc(sem("wm_tp"), 1)
            pe.wait_ge(sem("q_spread"), 1)
            turn_all(4, hf).then_inc(sem("inv_tp"), 1)
            pe.wait_ge(sem("wm_ready"), 1)
            pe.wait_ge(sem("qt_ready"), 1)

            def up(w, src, i):
                for n in range(4):
                    bh, half = n // 2, n % 2
                    if i:
                        pe.wait_ge(sem("uf_ready"), 4 * i)
                    pe.matmul(ps[:, UP_BANKS[i][n], :], w[64 * bh:64 * bh + 64, :], src[64 * bh:64 * bh + 64, half * BANK:(half + 1) * BANK],
                              start=True, stop=True).then_inc(sem("zf_done"), 1)

            def down(w, bank, i):
                for n in range(4):
                    bh, half = n // 2, n % 2
                    pe.wait_ge(sem("uf_ready"), 4 * i + n + 1)
                    mm = pe.matmul(ps[64 * bh:64 * bh + 64, bank + half, :], w, uf[:, n * BANK:(n + 1) * BANK], start=True, stop=True)
                mm.then_inc(sem("hf_done"), 1)

            pe.wait_ge(sem("w11_new"), NS + 1)
            pe.wait_ge(sem("w20_new"), NS + 1)
            up(w10m, qt, 0)
            pe.wait_ge(sem("wm_sum"), 1)
            pe.transpose(ps[:, 6, 0:E1], w11s[:, :, :].rearrange("p g d -> p (g d)"), ident).then_inc(sem("wm_tp"), 1)
            down(wme[:, 0, :], 4, 0)
            pe.wait_ge(sem("wm_sum"), 2)
            pe.wait_ge(sem("wm_ready"), 2)
            keep_warm(7, 5)
            pe.wait_ge(sem("hf_ready"), 1)
            up(w11m, hf, 1)
            down(wme[:, 2, :], 6, 1)

            keep_warm(0, 14)
            norm_group(1)
            keep_warm(0, 5)
            pe.wait_ge(sem("xn_ready"), 2 * J)
            project(0, par("attn_q"), xn).then_inc(sem("aqkv_done"), 1)
            project(2, par("attn_k"), xn).then_inc(sem("aqkv_done"), 1)
            project(4, par("attn_v"), xn).then_inc(sem("aqkv_done"), 1)
            pe.wait_ge(sem("aq_ready"), 1)
            pe.wait_ge(sem("ak_ready"), 1)
            for n in range(NK):
                pe.wait_ge(sem("qk_pool" if n % 2 else "qk_dve"), n // 2 + 1)
                if n >= 2:
                    pe.wait_ge(sem("score_done"), n - 1)
                turn_all((n % 2) * 2, prod[n % 4]).then_inc(sem("qk_tp"), 1)

            pe.wait_ge(sem("av_ready"), 1)
            pe.wait_ge(sem("score_done"), NK)
            keep_warm(0, 7)
            for n in range(NK + 1):
                if n >= 3:
                    pe.wait_ge(sem("pv_ready"), n - 2)
                pe.wait_ge(sem("attx_ready"), n + 1)
                turn_all(n % 3 * 2, attx[n % 2]).then_inc(sem("att_tp"), 1)

            pe.wait_ge(sem("pv_ready"), NK)
            keep_warm(6, 16)
            pe.wait_ge(sem("x3_ready"), 1)
            keep_warm(6, 8)
            norm_group(2)
            for q in range(2):
                for j in range(J):
                    col = 6 * BANK + (q * J + j) * P
                    pe.transpose(psf[:, col:col + P], xc[:, j * HW + q * P:j * HW + (q + 1) * P], ident)
            pe.wait_ge(sem("wout"), 1)
            pe.matmul(ps[:, 4, 0:C], cst("center_t", C), wout[0:C, :], start=True, stop=True)
            pe.matmul(ps[:, 4, C:2 * C], par("ln_beta")[0:C].broadcast_to([C, P]), par("out_w")[0:C, 0:C], start=True, stop=False)
            pe.matmul(ps[:, 4, C:2 * C], par("out_b")[0:C].broadcast_to([C, P]), cst("ident", C)[:, 0:C], start=False, stop=True)\
              .then_inc(sem("xrow_tp"), 1)
            keep_warm(0, 5)
            pe.wait_ge(sem("xn_ready"), 3 * J)

            def feature(f, n, bank):
                bh, half = n // 2, n % 2
                pe.matmul(ps[:, bank, :], par("scan_w")[64 * bh:64 * bh + 64, f * P:(f + 1) * P],
                          xn[64 * bh:64 * bh + 64, half * BANK:(half + 1) * BANK], start=True, stop=True).then_inc(sem("feat_done"), 1)

            for n in range(4):
                feature(0, n, n)
                if n == 0:
                    pe.wait_ge(sem("cm_ready"), 1)
                if n == 2:
                    pe.wait_ge(sem("xrow_ready"), 1)
                feature(1, n, 4 + n)
            for n in range(4):
                if n == 3:
                    pe.wait_ge(sem("silu"), 2)
                    keep_warm(4, 8)
                pe.wait_ge(sem("lam_b"), n + 1)
                feature(2, n, n)
            pe.wait_ge(sem("silu"), 4)
            keep_warm(4, 4)
            n = W // NWC
            for wc in range(NWC):
                pe.matmul(ps[:, 4 + wc, :], zero_bf[:, 0:P], zero_bf[:, :], start=True, stop=False)
            for bp in range(B // 2):
                pe.wait_ge(sem("pool_sum"), bp + 1)
                for wc in range(NWC):
                    pe.matmul(ps[:, 4 + wc, bp * BANK // 4:(bp + 1) * BANK // 4], ident,
                              sw[:, :].rearrange("p (b w s) -> p b w s", b=B, w=W)[:, 2 * bp:2 * bp + 2, wc * n:(wc + 1) * n, 1:],
                              start=False, stop=False)
            for wc in range(NWC):
                if wc < NWC - 2:
                    pe.wait_ge(sem("pool_sum"), B // 2 + wc + 1)
                else:
                    pe.wait_ge(sem("sb_ready"), wc - (NWC - 2) + 1)
                pe.matmul(ps[:, 4 + wc, :], ident, seqs_b(fb, wc).rearrange("p (n s) -> p s n", s=B + 1)[:, 1:, :],
                          start=False, stop=True).then_inc(sem("sum_done"), 1)
            pe.wait_ge(sem("og_ready"), 4)
            pe.wait_ge(sem("tot_ready"), NWC)
            for q in range(2):
                for b in range(B):
                    i = q * B + b
                    mm = pe.matmul(psf[:, i * P:(i + 1) * P], tot[:, (2 * b + q) * P:(2 * b + q + 1) * P], cm[:, :], start=True, stop=True)
                    if b % 4 == 3:
                        mm.then_inc(sem("out_mm"), 1)


def _constants():
    c = np.zeros((P, NCONST), np.float32)

    def put(name, value):
        a, b = CONST_COLS[name]
        v = np.asarray(value, np.float32).reshape(-1, b - a)
        c[:v.shape[0], a:b] = v

    i = np.arange(P)
    put("ident", np.eye(P))
    put("twice", 2 * np.eye(P))
    put("own_half", i[:, None] // 64 == i[None] // W % BH)
    put("pair_half", 0.5 * (i[:, None] // 2 == i[None] // 2))
    put("sum16", (i[:, None] // 16 == i[None] // 16) / 16.0)
    put("ones64", i[:, None] // 64 == i[None] // 64)
    put("dup64", i[:, None] % 64 == i[None] % 64)
    put("head_sel", i[:, None] // 8 == np.arange(BH * NHD)[None])
    ch = 2 * (i // 4) + i % 2
    center = (ch[:, None] == np.arange(C)[None]) - 1.0 / C
    put("center", center)
    put("center_t", center.T)
    put("block_j", i[:, None] // 32 == np.arange(J)[None])
    half = np.zeros((6, 2, BH, 64), np.float32)
    tok = np.zeros((6, J, J, BH, W), np.float32)
    for b2 in range(BH):
        half[3 * b2 + 2, 0, b2] = 1
        half[3 * b2 + 1, 1, b2] = 1
        for j in range(J):
            tok[3 * b2, j, j, b2] = 1
    put("half_sel", half.reshape(6, -1))
    put("tok_sel", tok.reshape(6, -1))
    one = [(-MAX_LR / W * GRAD_SCALE / 2, -MAX_LR * GRAD_SCALE / 2), (-0.5 / W, 0.5), (0.5 / W, 0.5)]
    put("gate_scale", np.array(one * 2))
    put("eps", np.full((P, 1), GEPS))
    return c


def _block_diag(m):
    out = np.zeros((2 * m.shape[0], 2 * m.shape[1]), np.float32)
    out[:m.shape[0], :m.shape[1]] = m
    out[m.shape[0]:, m.shape[1]:] = m
    return out


def kernel(x, L0_conv_weight, L0_conv_bias, L0_conv_gamma, L0_conv_beta, L0_conv_alpha, L1_conv_Wq, L1_conv_Wk, L1_conv_Wv,
           L1_conv_w_lr, L1_conv_w_forget, L1_conv_w_eta, L1_conv_w1_0, L1_conv_w2_0, L1_conv_w1_1, L1_conv_w2_1,
           L2_conv_W_qkv, L3_conv_in_w, L3_conv_in_b, L3_conv_out_w, L3_conv_out_b, L3_conv_gamma, L3_conv_beta):
    import concourse.bacc as bacc
    from concourse.bass_utils import run_bass_kernel_spmd

    xs = np.asarray(x).reshape(BH, J, 2, P, C).transpose(3, 2, 1, 0, 4)
    w = np.asarray(L0_conv_weight).reshape(2, 8, 3, 3, 2, 8, 16)
    band = np.zeros((8, 16, 2, 3, 2, 8, 16), np.float32)
    for i in range(3):
        for l in range(16):
            if 0 <= l + i - 1 < 16:
                band[:, l + i - 1, :, :, :, :, l] = w[:, :, i, :, :, :, l].transpose(1, 0, 2, 3, 4)
    blk = np.zeros((P, NPARAM), np.float32)

    def put(name, value):
        a, b = PARAM_COLS[name]
        blk[:, a:b] = np.asarray(value).reshape(P, b - a)

    def rows16(v):
        return np.repeat(np.asarray(v).reshape(2, 8), 16, axis=1).T

    def twice(m):
        return np.concatenate([np.asarray(m)] * 2, axis=0)

    put("conv_bias", np.asarray(L0_conv_bias).reshape(2, P).T)
    put("conv_gamma", rows16(L0_conv_gamma))
    put("conv_beta", rows16(L0_conv_beta))
    put("conv_alpha", np.broadcast_to(np.asarray(L0_conv_alpha), (P, 1)))
    put("wk", _block_diag(np.asarray(L1_conv_Wk)))
    put("wv", _block_diag(np.asarray(L1_conv_Wv)))
    put("wq", _block_diag(np.asarray(L1_conv_Wq)))
    put("gates", _block_diag(np.stack([np.asarray(L1_conv_w_lr), np.asarray(L1_conv_w_forget), np.asarray(L1_conv_w_eta)], axis=1)))
    put("mats_e", np.concatenate([np.asarray(L1_conv_w2_0), np.asarray(L1_conv_w1_1).T, np.asarray(L1_conv_w2_1)], axis=1))
    put("w1_0", twice(L1_conv_w1_0))
    wqkv = np.asarray(L2_conv_W_qkv).reshape(3, C, C)
    for n, name in enumerate(("attn_q", "attn_k", "attn_v")):
        put(name, _block_diag(wqkv[n].T))
    hd = np.repeat(np.arange(C), 2)
    he = (np.arange(C).reshape(-1, 1, 2).repeat(2, axis=1)).reshape(-1)
    pick = (2 * C + hd, he, C + hd)
    put("scan_w", twice(np.concatenate([np.asarray(L3_conv_in_w)[:, s] for s in pick], axis=1)))
    put("scan_b", np.stack([np.asarray(L3_conv_in_b)[s] for s in pick], axis=1))
    put("out_w", _block_diag(np.asarray(L3_conv_out_w)))
    put("out_b", twice(L3_conv_out_b))
    put("ln_gamma", twice(L3_conv_gamma))
    put("ln_beta", twice(L3_conv_beta))

    arrays = {"xs": np.ascontiguousarray(xs.reshape(P, 2, BANK)), "band": band.reshape(P, -1), "const": _constants(), "param": blk}
    nc = bacc.Bacc("TRN2", target_bir_lowering=False, num_devices=1)
    args = [nc.dram_tensor(n, a.shape, F32, kind="ExternalInput").ap() for n, a in arrays.items()]
    out = nc.dram_tensor("out", (P, 2, J, P), F32, kind="ExternalOutput").ap()
    conv_attn_scan_kernel(nc, *args, out)
    r = run_bass_kernel_spmd(nc, [arrays], core_ids=[0])
    got = r.results[0]["out"].reshape(P, 2, J, BH, C).transpose(3, 2, 1, 0, 4)
    return np.ascontiguousarray(got.reshape(B, H, W, C))
```
